# Optimizing a Trainium2 kernel written in Bass

```python
import numpy as np
import jax
import jax.numpy as jnp

def _softmax(x, axis=-1):
    return jax.nn.softmax(x, axis=axis)

def _gelu(x):
    return jax.nn.gelu(x, approximate=True)

def _silu(x):
    return jax.nn.silu(x)

def _sigmoid(x):
    return jax.nn.sigmoid(x)

def _layernorm(x, axis=-1, eps=1e-05):
    m = jnp.mean(x, axis=axis, keepdims=True)
    v = jnp.var(x, axis=axis, keepdims=True)
    return (x - m) / jnp.sqrt(v + eps)

def _scatter_add(tgt, idx, src, axis=0):
    return tgt.at[idx].add(src)

def _segment_sum(src, seg, n):
    return jax.ops.segment_sum(src, seg, n)
kernel_name = 'mk_seq_postln_d2_jaxref_r8_bf396b'

def setup_inputs(seed: int=0):
    np.random.seed(seed)
    _w = jnp.asarray

    def _L0_attn_setup():
        import jax, jax.numpy as jnp
        import numpy as np
        key = jax.random.key(seed)
        x = jax.random.normal(key, (8, 96, 256), dtype=jnp.float32)
        return {'x': x}
    _L0_attn_in = _L0_attn_setup()

    def _L0_ffn_setup():
        import jax, jax.numpy as jnp
        import numpy as np
        B, S, H, F, E, R, K = (2, 128, 256, 896, 8, 32, 2)

        def _gather_slot(a_all, e):
            return jnp.take_along_axis(a_all, e[:, None, None], axis=1)[:, 0]
        key = jax.random.key(seed)
        ks = jax.random.split(key, 12)
        sc = 0.02
        n = lambda k, shape, s: jax.random.normal(k, shape, dtype=jnp.float32) * s
        return {'hidden_states': n(ks[0], (B, S, H), 1.0), 'Wg': n(ks[1], (E, H), sc), 'W1': n(ks[2], (F, H), sc), 'W2': n(ks[3], (H, F), sc), 'W3': n(ks[4], (F, H), sc), 'A1': n(ks[5], (E, R, H), sc), 'B1': n(ks[6], (E, F, R), sc), 'A2': n(ks[7], (E, R, F), sc), 'B2': n(ks[8], (E, H, R), sc), 'A3': n(ks[9], (E, R, H), sc), 'B3': n(ks[10], (E, F, R), sc)}
    _L0_ffn_in = _L0_ffn_setup()

    def _L1_attn_setup():
        import jax, jax.numpy as jnp
        import numpy as np
        E2M1_GRID = jnp.array([0.0, 0.5, 1.0, 1.5, 2.0, 3.0, 4.0, 6.0], dtype=jnp.float32)
        E2M1_MIDS = (E2M1_GRID[1:] + E2M1_GRID[:-1]) / 2.0
        FP4_MAX = 6.0
        FP8_E4M3_MAX = 448.0

        def nvfp4_quant_dequant(w):
            O, I = w.shape
            w16 = w.reshape(O, I // 128, 8, 16)
            amax128 = jnp.max(jnp.abs(w16), axis=(-2, -1))
            outer = amax128 / (FP4_MAX * FP8_E4M3_MAX)
            outer = jnp.where(outer > 0, outer, 1.0)
            amax16 = jnp.max(jnp.abs(w16), axis=-1)
            inner = amax16 / FP4_MAX / outer[..., None]
            inner = inner.astype(jnp.float8_e4m3fn).astype(jnp.float32)
            scale = outer[..., None] * inner
            safe = jnp.where(scale > 0, scale, 1.0)[..., None]
            code = w16 / safe
            a = jnp.abs(code)
            idx = jnp.searchsorted(E2M1_MIDS, a)
            q = E2M1_GRID[idx] * jnp.sign(code)
            return (q * scale[..., None]).reshape(O, I)
        key = jax.random.key(seed)
        k0, k1, k2 = jax.random.split(key, 3)
        B, S, H = (2, 256, 256)
        hidden_states = jax.random.normal(k0, (B, S, H), dtype=jnp.float32)
        w_qkv = jax.random.normal(k1, (3 * H, H), dtype=jnp.float32) * 0.023
        w_o = jax.random.normal(k2, (H, H), dtype=jnp.float32) * 0.023
        w_qkv = nvfp4_quant_dequant(w_qkv)
        w_o = nvfp4_quant_dequant(w_o)
        return {'hidden_states': hidden_states, 'w_qkv': w_qkv, 'w_o': w_o}
    _L1_attn_in = _L1_attn_setup()

    def _L1_ffn_setup():
        import jax, jax.numpy as jnp
        import numpy as np
        NUM_EXPERTS = 32
        TOP_K = 8
        THRESHOLD = 0.8
        HIDDEN = 256
        INTER = 96
        key = jax.random.key(seed)
        k1, k2, k3, k4 = jax.random.split(key, 4)
        hidden_states = jax.random.normal(k1, (2, 128, HIDDEN), jnp.float32)
        gate_weight = jax.random.normal(k2, (NUM_EXPERTS, HIDDEN), jnp.float32) * 0.02
        gate_up_proj = jax.random.normal(k3, (NUM_EXPERTS, 2 * INTER, HIDDEN), jnp.float32) * 0.02
        down_proj = jax.random.normal(k4, (NUM_EXPERTS, HIDDEN, INTER), jnp.float32) * 0.02
        return {'hidden_states': hidden_states, 'gate_weight': gate_weight, 'gate_up_proj': gate_up_proj, 'down_proj': down_proj}
    _L1_ffn_in = _L1_ffn_setup()
    _d = {'L0_attn_x': _L0_attn_in['x'], 'L0_ffn_Wg': _L0_ffn_in['Wg'], 'L0_ffn_W1': _L0_ffn_in['W1'], 'L0_ffn_W2': _L0_ffn_in['W2'], 'L0_ffn_W3': _L0_ffn_in['W3'], 'L0_ffn_A1': _L0_ffn_in['A1'], 'L0_ffn_B1': _L0_ffn_in['B1'], 'L0_ffn_A2': _L0_ffn_in['A2'], 'L0_ffn_B2': _L0_ffn_in['B2'], 'L0_ffn_A3': _L0_ffn_in['A3'], 'L0_ffn_B3': _L0_ffn_in['B3'], 'L1_attn_w_qkv': _L1_attn_in['w_qkv'], 'L1_attn_w_o': _L1_attn_in['w_o'], 'L1_ffn_gate_weight': _L1_ffn_in['gate_weight'], 'L1_ffn_gate_up_proj': _L1_ffn_in['gate_up_proj'], 'L1_ffn_down_proj': _L1_ffn_in['down_proj']}
    _x0 = _d['L0_attn_x']
    _d['L0_attn_x'] = jax.random.normal(jax.random.fold_in(jax.random.key(seed), 1), (1, 2048, 256), dtype=_x0.dtype)
    del _x0
    return _d

def reference(L0_attn_x, L0_ffn_Wg, L0_ffn_W1, L0_ffn_W2, L0_ffn_W3, L0_ffn_A1, L0_ffn_B1, L0_ffn_A2, L0_ffn_B2, L0_ffn_A3, L0_ffn_B3, L1_attn_w_qkv, L1_attn_w_o, L1_ffn_gate_weight, L1_ffn_gate_up_proj, L1_ffn_down_proj):

    def _L0_attn_ref(x):
        import jax, jax.numpy as jnp
        import numpy as np
        energy = jnp.einsum('bci,bcj->bij', x, x)
        attention = jax.nn.softmax(energy, axis=-1)
        out = jnp.einsum('bcj,bij->bci', x, attention)
        return out

    def _L0_ffn_ref(hidden_states, Wg, W1, W2, W3, A1, B1, A2, B2, A3, B3):
        import jax, jax.numpy as jnp
        import numpy as np
        B, S, H, F, E, R, K = (2, 128, 256, 896, 8, 32, 2)

        def _gather_slot(a_all, e):
            return jnp.take_along_axis(a_all, e[:, None, None], axis=1)[:, 0]
        b, s, h = hidden_states.shape
        x = hidden_states.reshape(-1, h)
        nE = Wg.shape[0]
        logits = x @ Wg.T
        probs = jax.nn.softmax(logits.astype(jnp.float32), axis=-1)
        rw, sel = jax.lax.top_k(probs, K)
        rw = (rw / rw.sum(axis=-1, keepdims=True)).astype(x.dtype)
        base1 = x @ W1.T
        base3 = x @ W3.T
        a1_all = jnp.einsum('th,erh->ter', x, A1)
        a3_all = jnp.einsum('th,erh->ter', x, A3)
        out = jnp.zeros_like(x)
        for k in range(K):
            e = sel[:, k]
            mask = jax.nn.one_hot(e, nE, dtype=x.dtype)
            a1 = _gather_slot(a1_all, e)
            a3 = _gather_slot(a3_all, e)
            lora1 = jnp.einsum('ter,efr->tf', mask[:, :, None] * a1[:, None, :], B1)
            lora3 = jnp.einsum('ter,efr->tf', mask[:, :, None] * a3[:, None, :], B3)
            x1 = base1 + lora1
            x3 = base3 + lora3
            x2 = jax.nn.silu(x1) * x3
            down = x2 @ W2.T
            a2_all = jnp.einsum('tf,erf->ter', x2, A2)
            a2 = _gather_slot(a2_all, e)
            lora2 = jnp.einsum('ter,ehr->th', mask[:, :, None] * a2[:, None, :], B2)
            out = out + (down + lora2) * rw[:, k:k + 1]
        return out.reshape(b, s, h)

    def _L1_attn_ref(hidden_states, w_qkv, w_o):
        import jax, jax.numpy as jnp
        import numpy as np
        E2M1_GRID = jnp.array([0.0, 0.5, 1.0, 1.5, 2.0, 3.0, 4.0, 6.0], dtype=jnp.float32)
        E2M1_MIDS = (E2M1_GRID[1:] + E2M1_GRID[:-1]) / 2.0
        FP4_MAX = 6.0
        FP8_E4M3_MAX = 448.0

        def nvfp4_quant_dequant(w):
            O, I = w.shape
            w16 = w.reshape(O, I // 128, 8, 16)
            amax128 = jnp.max(jnp.abs(w16), axis=(-2, -1))
            outer = amax128 / (FP4_MAX * FP8_E4M3_MAX)
            outer = jnp.where(outer > 0, outer, 1.0)
            amax16 = jnp.max(jnp.abs(w16), axis=-1)
            inner = amax16 / FP4_MAX / outer[..., None]
            inner = inner.astype(jnp.float8_e4m3fn).astype(jnp.float32)
            scale = outer[..., None] * inner
            safe = jnp.where(scale > 0, scale, 1.0)[..., None]
            code = w16 / safe
            a = jnp.abs(code)
            idx = jnp.searchsorted(E2M1_MIDS, a)
            q = E2M1_GRID[idx] * jnp.sign(code)
            return (q * scale[..., None]).reshape(O, I)
        B, S, H = hidden_states.shape
        num_heads = 16
        head_dim = H // num_heads
        qkv = jnp.einsum('bsh,oh->bso', hidden_states, w_qkv)
        qkv = qkv.reshape(B, S, 3, num_heads, head_dim)
        qkv = jnp.transpose(qkv, (2, 0, 3, 1, 4))
        q, k, v = (qkv[0], qkv[1], qkv[2])
        scale = 1.0 / jnp.sqrt(jnp.float32(head_dim))
        scores = jnp.einsum('bhqd,bhkd->bhqk', q, k) * scale
        causal = jnp.tril(jnp.ones((S, S), dtype=bool))
        scores = jnp.where(causal, scores, jnp.finfo(scores.dtype).min)
        probs = jax.nn.softmax(scores, axis=-1)
        attn = jnp.einsum('bhqk,bhkd->bhqd', probs, v)
        attn = jnp.transpose(attn, (0, 2, 1, 3)).reshape(B, S, H)
        return jnp.einsum('bsh,oh->bso', attn, w_o)

    def _L1_ffn_ref(hidden_states, gate_weight, gate_up_proj, down_proj):
        import jax, jax.numpy as jnp
        import numpy as np
        NUM_EXPERTS = 32
        TOP_K = 8
        THRESHOLD = 0.8
        HIDDEN = 256
        INTER = 96
        B, S, H = hidden_states.shape
        x = hidden_states.reshape(-1, H)
        logits = x @ gate_weight.T
        probs = jax.nn.softmax(logits.astype(jnp.float32), axis=-1).astype(logits.dtype)
        top_vals, top_idx = jax.lax.top_k(probs, TOP_K)
        renorm = top_vals / jnp.clip(jnp.sum(top_vals, axis=-1, keepdims=True), 1e-12)
        cum = jnp.cumsum(renorm, axis=-1)
        num_keep = jnp.minimum(jnp.sum((cum < THRESHOLD).astype(jnp.int32), axis=-1) + 1, TOP_K)
        active = jnp.arange(TOP_K)[None, :] < num_keep[:, None]
        rw = top_vals * active.astype(top_vals.dtype)
        rw = rw / jnp.clip(jnp.sum(rw, axis=-1, keepdims=True), 1e-12)
        combine = jnp.sum(jax.nn.one_hot(top_idx, NUM_EXPERTS, dtype=rw.dtype) * rw[..., None], axis=1)

        def body(acc, params):
            w_gu, w_d, ce = params
            gu = x @ w_gu.T
            g, u = jnp.split(gu, 2, axis=-1)
            h = jax.nn.silu(g) * u
            return (acc + h @ w_d.T * ce[:, None], None)
        out, _ = jax.lax.scan(body, jnp.zeros_like(x), (gate_up_proj, down_proj, combine.T))
        return out.reshape(B, S, H)
    x = L0_attn_x
    x = _layernorm(x + _L0_attn_ref(x), axis=-1)
    x = _layernorm(x + _L0_ffn_ref(x, L0_ffn_Wg, L0_ffn_W1, L0_ffn_W2, L0_ffn_W3, L0_ffn_A1, L0_ffn_B1, L0_ffn_A2, L0_ffn_B2, L0_ffn_A3, L0_ffn_B3), axis=-1)
    x = _layernorm(x + _L1_attn_ref(x, L1_attn_w_qkv, L1_attn_w_o), axis=-1)
    x = _layernorm(x + _L1_ffn_ref(x, L1_ffn_gate_weight, L1_ffn_gate_up_proj, L1_ffn_down_proj), axis=-1)
    return x

_drawn_inputs = setup_inputs


def setup_inputs(seed=0):
    import zlib

    import numpy as np

    out = dict(_drawn_inputs(seed))
    spreads = {}
    factors = {'L0_ffn_Wg': 8.0,
     'L0_ffn_A1': 8.0,
     'L0_ffn_B1': 8.0,
     'L0_ffn_A2': 8.0,
     'L0_ffn_B2': 8.0,
     'L0_ffn_A3': 8.0,
     'L0_ffn_B3': 8.0,
     'L1_attn_w_qkv': 6.505,
     'L1_attn_w_o': 6.475,
     'L1_ffn_gate_weight': 8.0,
     'L1_ffn_gate_up_proj': 8.0,
     'L1_ffn_down_proj': 8.0}
    for name, (base, spread) in spreads.items():
        noise = np.random.default_rng([zlib.crc32(name.encode()), seed]).standard_normal(out[name].shape)
        drawn = base * np.exp(spread * noise) if base else spread * noise
        out[name] = jnp.asarray(drawn.astype(out[name].dtype))
    for name, factor in factors.items():
        out[name] = (out[name] * factor).astype(out[name].dtype)
    return out
```

```python
from contextlib import ExitStack

import concourse.bass as bass
import concourse.bacc as bacc
from concourse import mybir
import numpy as np

F32, F32R, BF16, U32 = mybir.dt.float32, mybir.dt.float32r, mybir.dt.bfloat16, mybir.dt.uint32
ALU = mybir.AluOpType
ACT = mybir.ActivationFunctionType
AX_X = mybir.AxisListType.X

P = 128
T, H = 2048, 256
NT = T // P
NB, BLK = 4, 512
TPB = BLK // P
NC = H // P
F, FT = 896, 896 // P
E0, R0 = 8, 32
HEADS, HD = 16, 16
GH, NG = 4, 4
E1, I1, TOP = 32, 96, 8
RPT = P // E1
JT = I1 // RPT
KEEP = 0.8
EPS = 1e-5
NEG = -3.0e38
STK = 4 * HD + 2
VW = HD + 1
PARTS = ((1, 0), (0, 1), (0, 0))


class Signal:

    def __init__(self, sem, events, by=1):
        self.sem, self.by = sem, by
        self.at = {e: n + 1 for n, e in enumerate(events)}

    def after(self, event):
        return self.sem, self.by * self.at[event]


def attention_plan():
    steps = [None] * 34
    for g in range(NG):
        steps += [(g, qb, kt) for qb in range(NB) for kt in range(TPB * (qb + 1))]
    return steps


def build(nc, x_tm, x_fm, w13_d, a13_d, b13_d, w2a2_d, b2_d, wg0_d, wqkv_d, wo_d, wg1_d, wgu_d, wdn_d,
          ident_d, identb_d, trimax_d, triexp_d, iota_d, out_d):
    with ExitStack() as ctx:
        def sem(name):
            return ctx.enter_context(nc.semaphore(name))

        def sig(name, events, by=1):
            return Signal(sem(name), list(events), by)

        base = (nc.sbuf_base + 31) // 32 * 32
        cursor = [base]

        def at(name, shape, dt, offset=None):
            size = int(np.prod(shape[1:])) * (2 if dt == BF16 else 4)
            if offset is None:
                offset = cursor[0]
            cursor[0] = (offset + size + 31) // 32 * 32
            return nc.alloc_sbuf_tensor_at(name, list(shape), dt, offset=offset)

        x = at("x", [P, NT, H], F32)
        ident = at("ident", [P, P], F32)
        identb = at("identb", [P, P], BF16)
        trimax = at("trimax", [P, P], BF16)
        triexp = at("triexp", [P, P], BF16)
        iota = at("iota", [P, E1], F32)
        half_neg = at("half_neg", [P, TPB], F32)
        ln_stats = at("ln_stats", [P, 2, TPB, 6], F32)
        ln_mv = at("ln_mv", [P, 2, TPB, 2], F32)
        ln_var = at("ln_var", [P, 2, TPB], F32)
        ln_rstd = at("ln_rstd", [P, 2, TPB], F32)
        row_ones = at("row_ones", [2, 512], F32R)
        row_zero = at("row_zero", [2, 512], F32R)
        R = cursor[0]

        xtb = at("xtb", [P, 2, NC, BLK], F32R, R)
        w13 = at("w13", [P, 2, NC, 2, F], F32R)
        a13 = at("a13", [P, 2, NC, 2, E0 * R0], F32R)
        b13 = at("b13", [P, NC, 2, F], F32)
        w2a2 = at("w2a2", [P, 2, FT, 2 * H], F32R)
        b2 = at("b2", [P, NC, H], F32)
        wg0_raw = at("wg0_raw", [P, NC, E0], F32)
        wg0 = at("wg0", [P, 2, NC, E0], F32R)
        ma = at("ma", [P, 2, 2, NC, BLK], F32)
        silu0 = at("silu0", [P, 3, BLK], F32)
        x2f = at("x2f", [P, 2, BLK], F32)
        maskbc = at("maskbc", [P, 2, BLK], F32)
        mx = at("mx", [P, 2, TPB, P], F32)
        gk = at("gk", [P, 2, H], F32)
        gsum = at("gsum", [P, H], F32)
        gt = at("gt", [P, NC, P], F32)
        lg0 = at("lg0", [P, TPB, E0], F32)
        top0 = at("top0", [P, TPB, 8], F32)
        idx0 = at("idx0", [P, TPB, 8], U32)
        idx0f = at("idx0f", [P, TPB, 8], F32)
        mask0 = at("mask0", [P, 2, TPB, E0], F32)
        mdiff = at("mdiff", [P, TPB, E0], F32)
        mw0 = at("mw0", [P, 2, TPB, E0], F32)
        gap0 = at("gap0", [P, TPB], F32)
        exp0 = at("exp0", [P, TPB], F32)
        den0 = at("den0", [P, TPB], F32)
        rw0 = at("rw0", [P, 2, TPB], F32)
        X2 = cursor[0]
        x2 = at("x2", [P, 2, 2, FT, BLK], F32R)
        xt_in = at("xt_in", [P, NC, T], F32, X2)
        att = at("att", [P, NC, H], F32)
        attn = at("attn", [P, NC, H], F32)
        att_t = at("att_t", [P, NC, H], F32)
        nmax_a = at("nmax_a", [P, NC], F32)
        sum_a = at("sum_a", [P, NC], F32)
        rec_a = at("rec_a", [P, NC], F32)
        w13_raw = at("w13_raw", [P, NC, 2, F], F32)
        w2a2_raw = at("w2a2_raw", [P, FT, 2 * H], F32)
        assert cursor[0] <= X2 + 4 * 4 * FT * BLK, cursor[0] - X2
        a13_raw = at("a13_raw", [P, NC, 2, E0 * R0], F32, R)

        o_tm = at("o_tm", [P, NT, H], F32, R)
        vaug = at("vaug", [P, NT * HEADS * VW + 15], F32)
        stack = at("stack", [STK, 2, 2, GH, T], F32R)
        SET = 2 * GH * T * 4
        S0 = cursor[0] - 2 * SET
        S1 = S0 + SET
        probs = at("probs", [P, 4, 2, BLK], F32)
        PR = cursor[0] - 4 * 2 * BLK * 4
        usum = at("usum", [P, BLK], F32)
        mpart = at("mpart", [P, 2, NT, NB], F32)
        nmx = at("nmx", [P, 2, NT], F32)
        mrow = at("mrow", [NT, 2, 2, P], F32R)
        rec_c = at("rec_c", [P, TPB, GH], F32)
        xtc = at("xtc", [P, 2, NC, T], F32R, S1)
        wqkv = at("wqkv", [P, 2, NC, 3 * H], F32R)
        qk_out = at("qk_out", [P, 2, 2, BLK], F32R)
        assert cursor[0] <= S1 + SET
        wqkv_raw = at("wqkv_raw", [P, NC, 3 * H], F32, PR)
        ot = at("ot", [P, 2, NC, T], F32R, S0)
        wo = at("wo", [P, 2, NC, H], F32R)
        wo_raw = at("wo_raw", [P, NC, H], F32)
        gu_raw = at("gu_raw", [P, 3, NC * 2 * P], F32)
        dn_raw = at("dn_raw", [P, 3, H], F32)
        wg1_raw = at("wg1_raw", [P, NC, E1], F32)
        wg1 = at("wg1", [P, 2, NC, E1], F32R)
        assert cursor[0] <= S1
        xtd = at("xtd", [P, 2, NC, T], F32R, S1)
        gu = at("gu", [P, 3, 2, NC, 2, P], F32R)
        dn = at("dn", [P, 3, 2, H], F32R)
        assert cursor[0] <= PR
        lg1 = at("lg1", [P, NT, E1], F32, R)
        prob1 = at("prob1", [P, NT, E1], F32)
        hit1 = at("hit1", [P, NT, E1], F32)
        comb1 = at("comb1", [P, NT, E1], F32)
        cex = at("cex", [P, NT, P], F32)
        ce_bc = at("ce_bc", [P, T], F32)
        assert cursor[0] <= S0, (cursor[0], S0)
        silu1 = at("silu1", [P, 2, BLK], F32, PR)
        hmul = at("hmul", [P, 2, BLK], F32)
        hfull = at("hfull", [P, 2, BLK], F32)
        r_max = at("r_max", [P, NT], F32)
        r_sum = at("r_sum", [P, NT], F32)
        r_rec = at("r_rec", [P, NT], F32)
        r_top = at("r_top", [P, NT, 8], F32)
        r_idx = at("r_idx", [P, NT, 8], U32)
        r_idxf = at("r_idxf", [P, NT, 8], F32)
        r_cum = at("r_cum", [P, NT, 8], F32)
        r_on = at("r_on", [P, NT, 8], F32)
        r_rw = at("r_rw", [P, NT, 8], F32)
        assert cursor[0] <= nc.sbuf_usable_end
        hpart = at("hpart", [P, 2, 2, 2, BLK], F32R, S0)

        ps = nc.alloc_psum_tensor("ps", [P, 8, 512], F32)
        qk_dram = nc.dram_tensor("qk_dram", [4, 2, P, T], F32)

        consts_in = sem("consts_in")
        x_in = [sem(f"x_in{b}") for b in range(NB)]
        xfm_in = sem("xfm_in")
        w0_in = {n: sem(f"w0_in_{n}") for n in ("w13", "a13", "w2a2", "wg0")}
        lora_in = sem("lora_in")
        pool_const = sem("pool_const")
        act_split = sig("act_split", ["w13", "w2a2", "a13", "wg0"])
        dve_step = sem("dve_step")
        pool_step = sem("pool_step")
        w0_ready = sig("w0_ready", ["a13", "w13", "w2a2", "wg0"])

        energy_ready = sig("energy_ready", range(NC))
        nmax_ready = sig("nmax_ready", range(NC))
        att_exp = sig("att_exp", range(NC))
        att_norm = sig("att_norm", range(NC))
        att_tps = sig("att_tps", range(NC))
        att_tsb = sig("att_tsb", range(NC))
        mix_ready = sig("mix_ready", range(NT))
        mix_read = sig("mix_read", range(NT))

        blocks = [(st, b) for st in "ABCD" for b in range(NB)]
        var_ready = sig("var_ready", blocks)
        rstd_ready = sig("rstd_ready", blocks)
        ln_ready = sig("ln_ready", blocks)

        turns = [(st, b, c) for st in "BCOD" for b in range(NB) for c in range(NC)]
        turned = sig("turned", turns)
        turned_hi = sig("turned_hi", turns)
        turned_lo = sig("turned_lo", turns)

        bb = range(NB)
        logits0 = sig("logits0", bb)
        gap_ready = sig("gap_ready", bb)
        gap_exp = sig("gap_exp", bb)
        mask_wide = sig("mask_wide", [(b, k) for b in bb for k in range(2)])
        mask_ps = sig("mask_ps", [(b, k) for b in bb for k in range(2)])
        mask_sb = sig("mask_sb", [(b, k) for b in bb for k in range(2)])
        a_ps = sig("a_ps", [(b, w, c) for b in bb for w in range(2) for c in range(NC)])
        ma_ready = sig("ma_ready", [(b, k, w, c) for b in bb for k in range(2) for w in range(2) for c in range(NC)])

        def tile_order():
            for j in range(FT + 1):
                if j < FT:
                    yield j, 0
                if j:
                    yield j - 1, 1

        jk = [(b, j, k) for b in bb for j, k in tile_order()]
        mlp_ps = sig("mlp_ps", jk)
        silu_ready = sig("silu_ready", jk)
        x2_full = sig("x2_full", jk)
        x2_hi = sig("x2_hi", jk)
        x2_lo = sig("x2_lo", jk)
        tk = [(b, t, k) for b in bb for t in range(TPB) for k in range(2)]
        down0 = sig("down0", tk)
        down0_read = sig("down0_read", tk)
        bt = [(b, t) for b in bb for t in range(TPB)]
        g_ready = sig("g_ready", bt)
        g_turned = sig("g_turned", bt)
        gt_ready = sig("gt_ready", bt)
        lora2_ps = sig("lora2_ps", bt)
        lora2_read = sig("lora2_read", bt)

        wqkv_in = sem("wqkv_in")
        wqkv_hi = sem("wqkv_hi")
        wqkv_ready = sem("wqkv_ready")
        bm = [(b, m) for b in bb for m in range(4)]
        qk_ps = sig("qk_ps", bm)
        qk_hi = sig("qk_hi", bm)
        qk_lo = sig("qk_lo", bm)
        qk_out_sem = [sem(f"qk_out_slot{i}") for i in range(2)]
        v_ps = sig("v_ps", range(NT))
        v_ready = sig("v_ready", range(NT))
        v_ones = sem("v_ones")

        rows_ready = sem("rows_ready")
        ones_in = sem("ones_in")
        stack_in = [[sem(f"stack_in{i}{h}") for h in range(GH)] for i in range(2)]
        max_in = [sem(f"max_in{h}") for h in range(GH)]

        steps = attention_plan()
        n_pre = 34
        per_group = (len(steps) - n_pre) // NG
        max_units = [(qt, kb) for qt in range(NT) for kb in range(qt // TPB + 1)]
        units_of = {}
        for g in range(NG):
            todo = [(g, h, qt, kb) for h in range(GH) for qt, kb in max_units]
            first = 0 if g == 0 else n_pre + (g - 1) * per_group + 4
            while todo:
                units_of[first] = todo[:5]
                todo, first = todo[5:], first + 1
        all_units = [u for s in sorted(units_of) for u in units_of[s]]
        unit_no = {u: n for n, u in enumerate(all_units)}
        scored = sig("scored", all_units)
        reduced = sig("reduced", all_units)
        gh = [(g, h) for g in range(NG) for h in range(GH)]
        head_max = sig("head_max", gh)
        max_turned = sig("max_turned", gh)
        max_hi = sig("max_hi", gh)
        max_lo = sig("max_lo", gh)
        real = steps[n_pre:]
        sp = [(s, p) for s in range(len(real)) for p in range(2)]
        st_ready = sig("st_ready", sp)
        exp_done = sig("exp_done", sp)
        pv_done = sig("pv_done", range(len(real)))
        gq = [(g, qb) for g in range(NG) for qb in range(NB)]
        u_copied = sig("u_copied", gq)
        u_turned = sig("u_turned", gq)
        o_ready = sig("o_ready", gq)
        misc = []
        head_end = {}
        for s in sorted(units_of):
            for u in units_of[s]:
                if u[2:] == max_units[-1]:
                    head_end[s + 1] = u[:2]
        out_at = {}
        for n, (g, qb, kt) in enumerate(real):
            if kt == TPB * (qb + 1) - 1:
                out_at[n_pre + n + 2] = (g, qb)
        for s in range(len(steps) + 3):
            if s in head_end:
                misc.append(("max", head_end[s]))
            if s in out_at:
                misc.append(("out", out_at[s]))

        def misc_free(eng, item):
            n = misc.index(item)
            if n:
                kind, key = misc[n - 1]
                eng.wait_ge(*(max_lo if kind == "max" else o_ready).after(key))

        wo_in = sem("wo_in")
        wo_hi = sem("wo_hi")
        wo_ready = sem("wo_ready")
        proj_ps = sig("proj_ps", range(NT))
        proj_read = sig("proj_read", range(NT))

        wg1_in = sem("wg1_in")
        wg1_hi = sem("wg1_hi")
        wg1_ready = sem("wg1_ready")
        logits1 = sem("logits1")
        lg1_shift = sem("lg1_shift")
        prob_exp = sem("prob_exp")
        ce_wide = sig("ce_wide", bb)
        ce_ps = sig("ce_ps", bb)
        ce_sb = sig("ce_sb", bb)
        hj = [(hf, j) for hf in range(2) for j in range(JT)]
        raw_in = [sem(f"raw_in{i}") for i in range(3)]
        gu_hi_only = sem("gu_hi")
        wd_hi = sig("wd_hi", hj)
        wd_lo = sig("wd_lo", hj)
        hjt = [(hf, j, tb) for hf, j in hj for tb in range(2)]
        gu_ps = sig("gu_ps", hjt)
        silu1_ready = sig("silu1_ready", hjt)
        hmul_ready = sig("hmul_ready", hjt)
        h_full = sig("h_full", hjt)
        h_hi = sig("h_hi", hjt)
        h_lo = sig("h_lo", hjt)
        down1 = sig("down1", hj)
        acc_read = sig("acc_read", [(hf, t) for hf in range(2) for t in range(8)])
        stored = sem("stored")

        def hj_no(hf, j):
            return hf * JT + j

        block = ctx.enter_context(nc.Block())

        @block.sync
        def _(sp_):
            for b in range(NB):
                sp_.dma_start(x[:, TPB * b:TPB * (b + 1), :], x_tm[:, TPB * b:TPB * (b + 1), :]).then_inc(x_in[b], 16)
            sp_.dma_start(ident[:, :], ident_d).then_inc(consts_in, 16)
            sp_.dma_start(identb[:, :], identb_d).then_inc(consts_in, 16)
            sp_.dma_start(trimax[:, :], trimax_d).then_inc(consts_in, 16)
            sp_.dma_start(triexp[:, :], triexp_d).then_inc(consts_in, 16)
            sp_.dma_start(iota[:, :], iota_d).then_inc(consts_in, 16)
            sp_.dma_start(xt_in[:, :, :], x_fm).then_inc(xfm_in, 16)
            sp_.dma_start(a13_raw[:, :, :, :], a13_d).then_inc(w0_in["a13"], 16)
            sp_.dma_start(w13_raw[:, :, :, :], w13_d).then_inc(w0_in["w13"], 16)
            sp_.dma_start(w2a2_raw[:, :, :], w2a2_d).then_inc(w0_in["w2a2"], 16)
            sp_.dma_start(wg0_raw[:, :, :], wg0_d).then_inc(w0_in["wg0"], 16)
            sp_.dma_start(b13[:, :, :, :], b13_d).then_inc(lora_in, 16)
            sp_.dma_start(b2[:, :, :], b2_d).then_inc(lora_in, 16)
            sp_.wait_ge(*lora2_read.after((NB - 1, TPB - 1)))
            sp_.dma_start(wqkv_raw[:, :, :], wqkv_d).then_inc(wqkv_in, 16)
            for n, (b, m) in enumerate(bm):
                sp_.wait_ge(*qk_lo.after((b, m)))
                sp_.dma_start(qk_dram[m, :, :, BLK * b:BLK * (b + 1)].rearrange("s p t -> p s t"),
                              qk_out[:, n % 2, :, :].bitcast(F32)).then_inc(qk_out_sem[n % 2], 16)
            for i in range(2):
                sp_.wait_ge(qk_out_sem[i], 16 * len(bm) // 2)
            for g in range(NG):
                if g >= 2:
                    sp_.wait_ge(*st_ready.after(((g - 1) * per_group - 1, 1)))
                if g == 0:
                    sp_.wait_ge(rows_ready, 2)
                    sp_.wait_ge(*v_ps.after(NT - 1))
                    for q in range(2):
                        for h in range(GH):
                            for i in range(4):
                                sp_.dma_start(stack[STK - 2:STK, q, 1, h, 512 * i:512 * (i + 1)].bitcast(F32),
                                              row_ones[:, :].bitcast(F32)).then_inc(ones_in, 16)
                for h in range(GH):
                    head = GH * g + h
                    m, r = head // 8, HD * (head % 8)
                    for i in range(4):
                        sp_.dma_start(stack[STK - 2:STK, g % 2, 0, h, 512 * i:512 * (i + 1)].bitcast(F32),
                                      row_zero[:, :].bitcast(F32)).then_inc(stack_in[g % 2][h], 16)
                    for i in range(2):
                        for rep in range(2):
                            lo = HD * (2 * i + rep)
                            sp_.dma_start(stack[lo:lo + HD, g % 2, 0, h, :].bitcast(F32),
                                          qk_dram[m, i, r:r + HD, :]).then_inc(stack_in[g % 2][h], 16)
                            sp_.dma_start(stack[lo:lo + HD, g % 2, 1, h, :].bitcast(F32),
                                          qk_dram[2 + m, rep, r:r + HD, :]).then_inc(stack_in[g % 2][h], 16)
            sp_.wait_ge(*st_ready.after(((NG - 1) * per_group - 1, 1)))
            sp_.dma_start(wo_raw[:, :, :], wo_d).then_inc(wo_in, 16)
            sp_.dma_start(wg1_raw[:, :, :], wg1_d).then_inc(wg1_in, 16)
            for n, (hf, j) in enumerate(hj):
                if n >= 3:
                    sp_.wait_ge(*wd_lo.after(hj[n - 3]))
                sp_.dma_start(gu_raw[:, n % 3, :], wgu_d[:, j, :]).then_inc(raw_in[n % 3], 16)
                sp_.dma_start(dn_raw[:, n % 3, :], wdn_d[:, j, :]).then_inc(raw_in[n % 3], 16)
            for b in range(NB):
                sp_.wait_ge(*ln_ready.after(("D", b)))
                sp_.dma_start(out_d[:, TPB * b:TPB * (b + 1), :], x[:, TPB * b:TPB * (b + 1), :]).then_inc(stored, 16)
            sp_.wait_ge(stored, 16 * NB)

        @block.gpsimd
        def _(pool):
            steps_done = [0]

            def settle(ins):
                steps_done[0] += 1
                ins.then_inc(pool_step, 1)
                pool.wait_ge(pool_step, steps_done[0])

            pool.memset(half_neg[:, :], -0.5).then_inc(pool_const, 1)
            pool.memset(row_ones[:, :].bitcast(F32), 1.0).then_inc(rows_ready, 1)
            pool.memset(row_zero[:, :].bitcast(F32), 0.0).then_inc(rows_ready, 1)
            pool.wait_ge(pool_const, 1)

            def rstd(st, b):
                pool.wait_ge(*var_ready.after((st, b)))
                pool.tensor_tensor(ln_rstd[:, b % 2, :], ln_var[:, b % 2, :], half_neg[:, :], ALU.pow) \
                    .then_inc(rstd_ready.sem, 1)

            def max_rows(g, h):
                n = GH * g + h
                pool.wait_ge(*max_hi.after((g, h)))
                pool.wait_ge(*max_lo.after((g, h)))
                for s in range(2):
                    pool.dma_start(stack[4 * HD + s:4 * HD + s + 1, g % 2, 0, h, :].bitcast(F32)
                                   .rearrange("a (t q) -> a t q", t=NT), mrow[:, n % 2, s, :].bitcast(F32)).then_inc(max_in[h], 16)

            for b in range(NB):
                rstd("A", b)
            for b in range(NB):
                rstd("B", b)
            for g, h in gh:
                max_rows(g, h)
            for b in range(NB):
                rstd("C", b)
            for hf in range(2):
                for j in range(JT):
                    n = hj_no(hf, j)
                    pool.wait_ge(*wd_hi.after((hf, j)))
                    settle(pool.tensor_tensor(gu[:, n % 3, 1, :, :, :].rearrange("p a b c -> p (a b c)"),
                                              gu_raw[:, n % 3, :],
                                              gu[:, n % 3, 0, :, :, :].rearrange("p a b c -> p (a b c)").bitcast(F32),
                                              ALU.subtract))
                    pool.tensor_tensor(dn[:, n % 3, 1, :], dn_raw[:, n % 3, :], dn[:, n % 3, 0, :].bitcast(F32),
                                       ALU.subtract).then_inc(wd_lo.sem, 1)
                for b in range(2 * hf, 2 * hf + 2):
                    rstd("D", b)

        @block.scalar
        def _(act):
            def copy(out, in_):
                return act.activation(out, in_, ACT.Copy)

            for n, raw, part in (("w13", w13_raw, w13), ("w2a2", w2a2_raw, w2a2), ("a13", a13_raw, a13),
                                 ("wg0", wg0_raw, wg0)):
                act.wait_ge(w0_in[n], 16)
                full = (slice(None),) * (len(raw.shape) - 1)
                copy(part[(full[0], 0) + full[1:]], raw[full + (slice(None),)]).then_inc(act_split.sem, 1)
            for c in range(NC):
                act.wait_ge(*nmax_ready.after(c))
                act.activation(att[:, c, :], ps[:, c, 0:H], ACT.Exp, bias=nmax_a[:, c:c + 1],
                               accum_out=sum_a[:, c:c + 1]).then_inc(att_exp.sem, 1)

            def turn_hi(st, b, dst):
                for c in range(NC):
                    act.wait_ge(*turned.after((st, b, c)))
                    copy(dst[:, 0, c, :] if st == "B" else dst[:, 0, c, BLK * b:BLK * (b + 1)], ps[:, 6 + c, :]) \
                        .then_inc(turned_hi.sem, 1)

            for b in range(NB):
                turn_hi("B", b, xtb)
                act.wait_ge(*gap_ready.after(b))
                act.activation(exp0[:, :], gap0[:, :], ACT.Exp).then_inc(gap_exp.sem, 1)
                for k in range(2):
                    act.wait_ge(*mask_ps.after((b, k)))
                    copy(maskbc[:, k, :], ps[:, 6 + k, :]).then_inc(mask_sb.sem, 1)
                order = list(tile_order())

                def hi(n):
                    j, k = order[n]
                    act.wait_ge(*x2_full.after((b, j, k)))
                    copy(x2[:, 0, k, j, :], x2f[:, n % 2, :]).then_inc(x2_hi.sem, 1)

                for n, (j, k) in enumerate(order):
                    act.wait_ge(*mlp_ps.after((b, j, k)))
                    if n >= 3:
                        act.wait_ge(*x2_full.after((b,) + order[n - 3]))
                    s = (j + 2) % 3
                    act.activation(silu0[:, n % 3, :], ps[:, 2 * s, :], ACT.Silu).then_inc(silu_ready.sem, 1)
                    if n:
                        hi(n - 1)
                hi(len(order) - 1)
                for t in range(TPB):
                    act.wait_ge(*g_turned.after((b, t)))
                    copy(gt[:, :, :].rearrange("p c t -> p (c t)"), ps[:, 6, 0:H]).then_inc(gt_ready.sem, 1)

            act.wait_ge(wqkv_in, 16)
            copy(wqkv[:, 0, :, :], wqkv_raw[:, :, :]).then_inc(wqkv_hi, 1)
            for b in range(NB):
                turn_hi("C", b, xtc)
                for m in range(4):
                    n = 4 * b + m
                    act.wait_ge(*qk_ps.after((b, m)))
                    if n >= 2:
                        act.wait_ge(qk_out_sem[n % 2], 16 * (n // 2))
                    copy(qk_out[:, n % 2, 0, :], ps[:, m, :]).then_inc(qk_hi.sem, 1)
                for t in range(TPB * b, TPB * (b + 1)):
                    act.wait_ge(*v_ps.after(t))
                    act.wait_ge(v_ones, 1)
                    copy(vaug[:, 0:NT * HEADS * VW].rearrange("p (t h d) -> p t h d", t=NT, d=VW)[:, t, :, 0:HD],
                         ps[:, 4 + t % 2, 0:H].rearrange("p (h d) -> p h d", d=HD)).then_inc(v_ready.sem, 1)
            for s, (g, qb, kt) in enumerate(real):
                off = max(0, kt - TPB * qb) * P
                for p in range(2):
                    act.wait_ge(*st_ready.after((s, p)))
                    if s >= 2:
                        act.wait_ge(*pv_done.after(s - 2))
                    act.activation(probs[:, (2 * s + p) % 4, :, off:BLK], ps[:, 2 * p:2 * p + 2, off:BLK], ACT.Exp,
                                   scale=float(HD) ** -0.5).then_inc(exp_done.sem, 1)
            act.wait_ge(wo_in, 16)
            copy(wo[:, 0, :, :], wo_raw[:, :, :]).then_inc(wo_hi, 1)
            for b in range(NB):
                turn_hi("O", b, ot)
            act.wait_ge(wg1_in, 16)
            copy(wg1[:, 0, :, :], wg1_raw[:, :, :]).then_inc(wg1_hi, 1)
            for b in range(NB):
                turn_hi("D", b, xtd)
            act.wait_ge(lg1_shift, 1)
            act.activation(prob1[:, :, :], lg1[:, :, :], ACT.Exp).then_inc(prob_exp, 1)

            def weights_hi(hf, j):
                n = hj_no(hf, j)
                act.wait_ge(raw_in[n % 3], 32 * (n // 3 + 1))
                if n >= 3:
                    act.wait_ge(*down1.after(hj[n - 3]))
                copy(gu[:, n % 3, 0, :, :, :].rearrange("p a b c -> p (a b c)"), gu_raw[:, n % 3, :]) \
                    .then_inc(gu_hi_only, 1)
                copy(dn[:, n % 3, 0, :], dn_raw[:, n % 3, :]).then_inc(wd_hi.sem, 1)

            for n in range(2):
                weights_hi(*hj[n])
            for b in range(NB):
                act.wait_ge(*ce_ps.after(b))
                copy(ce_bc[:, BLK * b:BLK * (b + 1)], ps[:, b, :]).then_inc(ce_sb.sem, 1)
            for i, (hf, j, tb) in enumerate(hjt):
                act.wait_ge(*gu_ps.after((hf, j, tb)))
                if i >= 2:
                    act.wait_ge(*hmul_ready.after(hjt[i - 2]))
                act.activation(silu1[:, tb, :], ps[:, 4 + 2 * tb, :], ACT.Silu).then_inc(silu1_ready.sem, 1)
                act.wait_ge(*h_full.after((hf, j, tb)))
                n = hj_no(hf, j)
                if n >= 2:
                    act.wait_ge(*down1.after(hj[n - 2]))
                copy(hpart[:, n % 2, tb, 0, :], hfull[:, tb, :]).then_inc(h_hi.sem, 1)
                if tb == 1 and n + 2 < len(hj):
                    weights_hi(*hj[n + 2])

        @block.vector
        def _(dve):
            done = [0]

            def step(ins):
                done[0] += 1
                ins.then_inc(dve_step, 1)

            def settle():
                dve.wait_ge(dve_step, done[0])

            def low(out, full, hi):
                return dve.tensor_tensor(out, full, hi.bitcast(F32), ALU.subtract)

            def layer_norm(st, b, n_prior=None):
                settle()
                q = b % 2
                for t in range(TPB):
                    step(dve.bn_stats(ln_stats[:, q, t, :], x[:, TPB * b + t, :]))
                settle()
                for t in range(TPB):
                    step(dve.bn_aggr(ln_mv[:, q, t, :], ln_stats[:, q, t, :]))
                settle()
                dve.tensor_scalar(ln_var[:, q, :], ln_mv[:, q, :, 1], EPS, None, ALU.add).then_inc(var_ready.sem, 1)
                dve.wait_ge(*rstd_ready.after((st, b)))
                for t in range(TPB):
                    ins = dve.tensor_scalar(x[:, TPB * b + t, :], x[:, TPB * b + t, :], ln_mv[:, q, t, 0:1],
                                            ln_rstd[:, q, t:t + 1], ALU.subtract, ALU.mult)
                    if t < TPB - 1:
                        step(ins)
                    else:
                        ins.then_inc(ln_ready.sem, 1)

            for n, raw, part in (("a13", a13_raw, a13), ("w13", w13_raw, w13), ("w2a2", w2a2_raw, w2a2),
                                 ("wg0", wg0_raw, wg0)):
                dve.wait_ge(*act_split.after("a13" if n == "a13" else n))
                full = (slice(None),) * (len(raw.shape) - 1)
                low(part[(full[0], 1) + full[1:]], raw[full + (slice(None),)],
                    part[(full[0], 0) + full[1:]]).then_inc(w0_ready.sem, 1)

            for c in range(NC):
                dve.wait_ge(*energy_ready.after(c))
                dve.tensor_reduce(nmax_a[:, c:c + 1], ps[:, c, 0:H], AX_X, ALU.max, negate=True) \
                    .then_inc(nmax_ready.sem, 1)
            for c in range(NC):
                dve.wait_ge(*att_exp.after(c))
                step(dve.reciprocal(rec_a[:, c:c + 1], sum_a[:, c:c + 1]))
                settle()
                dve.tensor_scalar(attn[:, c, :], att[:, c, :], rec_a[:, c:c + 1], None, ALU.mult) \
                    .then_inc(att_norm.sem, 1)
            for j in range(NC):
                dve.wait_ge(*att_tps.after(j))
                dve.tensor_copy(att_t[:, j, :], ps[:, 2 + j, 0:H]).then_inc(att_tsb.sem, 1)
            for b in range(NB):
                for t in range(TPB * b, TPB * (b + 1)):
                    dve.wait_ge(*mix_ready.after(t))
                    dve.tensor_tensor(x[:, t, :], ps[:, 4 + t % 4, 0:H], x[:, t, :], ALU.add).then_inc(mix_read.sem, 1)
                dve.wait_ge(*mix_read.after(TPB * (b + 1) - 1))
                layer_norm("A", b)

            def turn_lo(st, b, dst):
                for c in range(NC):
                    dve.wait_ge(*turned_hi.after((st, b, c)))
                    if st == "B":
                        out, hi = dst[:, 1, c, :], dst[:, 0, c, :]
                    else:
                        out, hi = (dst[:, i, c, BLK * b:BLK * (b + 1)] for i in (1, 0))
                    low(out, ps[:, 6 + c, :], hi).then_inc(turned_lo.sem, 1)

            for b in range(NB):
                turn_lo("B", b, xtb)
                dve.wait_ge(*logits0.after(b))
                step(dve.tensor_copy(lg0[:, :, :].rearrange("p t e -> p (t e)"), ps[:, 6, 0:TPB * E0]))
                settle()
                for t in range(TPB):
                    step(dve.max(top0[:, t, :], lg0[:, t, :]))
                settle()
                for t in range(TPB):
                    step(dve.max_index(idx0[:, t, :], top0[:, t, :], lg0[:, t, :]))
                dve.tensor_tensor(gap0[:, :], top0[:, :, 1], top0[:, :, 0], ALU.subtract).then_inc(gap_ready.sem, 1)
                settle()
                step(dve.tensor_copy(idx0f[:, :, :], idx0[:, :, :]))
                settle()
                for k in range(2):
                    step(dve.tensor_tensor(mask0[:, k, :, :], iota[:, None, 0:E0].broadcast_to([P, TPB, E0]),
                                           idx0f[:, :, k:k + 1].broadcast_to([P, TPB, E0]), ALU.is_equal))
                settle()
                step(dve.tensor_tensor(mdiff[:, :, :], mask0[:, 1, :, :], mask0[:, 0, :, :], ALU.subtract))
                settle()
                for k, src in ((0, mask0[:, 0, :, :]), (1, mdiff[:, :, :])):
                    dve.tensor_copy(mx[:, k, :, :].rearrange("p t (r e) -> p t r e", e=E0),
                                    src[:, :, None, :].broadcast_to([P, TPB, P // E0, E0])) \
                        .then_inc(mask_wide.sem, 1)
                dve.wait_ge(*gap_exp.after(b))
                step(dve.tensor_scalar(den0[:, :], exp0[:, :], 1.0, None, ALU.add))
                settle()
                step(dve.reciprocal(rw0[:, 0, :], den0[:, :]))
                settle()
                step(dve.tensor_tensor(rw0[:, 1, :], exp0[:, :], rw0[:, 0, :], ALU.mult))
                settle()
                for k in range(2):
                    step(dve.tensor_tensor(mw0[:, k, :, :], mask0[:, k, :, :],
                                           rw0[:, k, :, None].broadcast_to([P, TPB, E0]), ALU.mult))
                for k in range(2):
                    dve.wait_ge(*mask_sb.after((b, k)))
                    for w in range(2):
                        for c in range(NC):
                            dve.wait_ge(*a_ps.after((b, w, c)))
                            dve.tensor_tensor(ma[:, w, k, c, :], ps[:, 2 * w + c, :], maskbc[:, k, :], ALU.mult) \
                                .then_inc(ma_ready.sem, 1)
                order = list(tile_order())

                def lo(n):
                    j, k = order[n]
                    dve.wait_ge(*x2_hi.after((b, j, k)))
                    low(x2[:, 1, k, j, :], x2f[:, n % 2, :], x2[:, 0, k, j, :]).then_inc(x2_lo.sem, 1)

                for n, (j, k) in enumerate(order):
                    dve.wait_ge(*silu_ready.after((b, j, k)))
                    if n >= 2:
                        lo(n - 2)
                        dve.wait_ge(*x2_lo.after((b,) + order[n - 2]))
                    s = (j + 2) % 3
                    dve.tensor_tensor(x2f[:, n % 2, :], ps[:, 2 * s + 1, :], silu0[:, n % 3, :], ALU.mult) \
                        .then_inc(x2_full.sem, 1)
                lo(len(order) - 2)
                lo(len(order) - 1)

                def residual(t):
                    dve.wait_ge(*lora2_ps.after((b, t)))
                    dve.tensor_tensor(x[:, TPB * b + t, :], ps[:, 7, 0:H], x[:, TPB * b + t, :], ALU.add) \
                        .then_inc(lora2_read.sem, 1)

                for t in range(TPB):
                    xt = x[:, TPB * b + t, :]
                    if t:
                        dve.wait_ge(*gt_ready.after((b, t - 1)))
                    for k in range(2):
                        dve.wait_ge(*down0.after((b, t, k)))
                        bank = (2 * t + k) % 4
                        settle()
                        step(dve.tensor_tensor(gk[:, k, :].rearrange("p (r e) -> p r e", e=E0),
                                               ps[:, bank, H:2 * H].rearrange("p (r e) -> p r e", e=E0),
                                               mw0[:, k, t, None, :].broadcast_to([P, R0, E0]), ALU.mult))
                        settle()
                        dve.scalar_tensor_tensor(out=xt, in0=ps[:, bank, 0:H], scalar=rw0[:, k, t:t + 1], in1=xt,
                                                 op0=ALU.mult, op1=ALU.add).then_inc(down0_read.sem, 1)
                        dve.wait_ge(*down0_read.after((b, t, k)))
                    dve.tensor_tensor(gsum[:, :], gk[:, 0, :], gk[:, 1, :], ALU.add).then_inc(g_ready.sem, 1)
                    dve.wait_ge(*g_ready.after((b, t)))
                    if t:
                        residual(t - 1)
                residual(TPB - 1)
                dve.wait_ge(*lora2_read.after((b, TPB - 1)))
                layer_norm("B", b)

            dve.wait_ge(*ln_ready.after(("B", NB - 1)))
            dve.memset(vaug[:, :], 1.0).then_inc(v_ones, 1)
            dve.wait_ge(wqkv_hi, 1)
            low(wqkv[:, 1, :, :], wqkv_raw[:, :, :], wqkv[:, 0, :, :]).then_inc(wqkv_ready, 1)
            for b in range(NB):
                turn_lo("C", b, xtc)
                for m in range(4):
                    n = 4 * b + m
                    dve.wait_ge(*qk_hi.after((b, m)))
                    low(qk_out[:, n % 2, 1, :], ps[:, m, :], qk_out[:, n % 2, 0, :]).then_inc(qk_lo.sem, 1)
            step(dve.memset(mpart[:, :, :, :], NEG))

            def turned_max(g, h):
                n = GH * g + h
                dve.wait_ge(*max_turned.after((g, h)))
                if n >= 2:
                    dve.wait_ge(max_in[(n - 2) % GH], 32 * ((n - 2) // GH + 1))
                dve.tensor_copy(mrow[:, n % 2, 0, :], ps[0:NT, 7, 0:P]).then_inc(max_hi.sem, 1)
                dve.wait_ge(*max_hi.after((g, h)))
                low(mrow[:, n % 2, 1, :], ps[0:NT, 7, 0:P], mrow[:, n % 2, 0, :]).then_inc(max_lo.sem, 1)

            def head_out(g, qb):
                dve.wait_ge(*u_turned.after((g, qb)))
                view = ps[:, 7, :].rearrange("p (t h d) -> p t h d", t=TPB, h=GH)
                step(dve.reciprocal(rec_c[:, :, :], view[:, :, :, HD]))
                settle()
                dve.tensor_tensor(o_tm[:, TPB * qb:TPB * (qb + 1), GH * HD * g:GH * HD * (g + 1)]
                                  .rearrange("p t (h d) -> p t h d", d=HD), view[:, :, :, 0:HD],
                                  rec_c[:, :, :, None].broadcast_to([P, TPB, GH, HD]), ALU.mult) \
                    .then_inc(o_ready.sem, 1)

            settle()
            for s in range(len(steps) + 3):
                for u in units_of.get(s, []):
                    g, h, qt, kb = u
                    n = GH * g + h
                    width = BLK if kb < qt // TPB else P * (qt % TPB + 1)
                    dve.wait_ge(*scored.after(u))
                    dve.tensor_reduce(mpart[:, n % 2, qt, kb:kb + 1], ps[:, 4 + unit_no[u] % 2, 0:width], AX_X,
                                      ALU.max).then_inc(reduced.sem, 1)
                    if (qt, kb) == max_units[-1]:
                        dve.wait_ge(*reduced.after(u))
                        dve.tensor_reduce(nmx[:, n % 2, :], mpart[:, n % 2, :, :], AX_X, ALU.max, negate=True) \
                            .then_inc(head_max.sem, 1)
                if s in head_end:
                    turned_max(*head_end[s])
                if s in out_at:
                    head_out(*out_at[s])
                r = s - n_pre - 1
                if 0 <= r < len(real):
                    g, qb, kt = real[r]
                    if kt == TPB * (qb + 1) - 1:
                        dve.wait_ge(*pv_done.after(r))
                        if gq.index((g, qb)):
                            dve.wait_ge(*u_turned.after(gq[gq.index((g, qb)) - 1]))
                        dve.tensor_copy(usum[:, :], ps[:, 6, :]).then_inc(u_copied.sem, 1)

            dve.wait_ge(wo_hi, 1)
            low(wo[:, 1, :, :], wo_raw[:, :, :], wo[:, 0, :, :]).then_inc(wo_ready, 1)
            for b in range(NB):
                turn_lo("O", b, ot)
            for b in range(NB):
                for t in range(TPB * b, TPB * (b + 1)):
                    dve.wait_ge(*proj_ps.after(t))
                    dve.tensor_tensor(x[:, t, :], ps[:, t % 4, 0:H], x[:, t, :], ALU.add).then_inc(proj_read.sem, 1)
                dve.wait_ge(*proj_read.after(TPB * (b + 1) - 1))
                layer_norm("C", b)

            dve.wait_ge(wg1_hi, 1)
            low(wg1[:, 1, :, :], wg1_raw[:, :, :], wg1[:, 0, :, :]).then_inc(wg1_ready, 1)
            for b in range(NB):
                turn_lo("D", b, xtd)
            dve.wait_ge(logits1, 1)
            lgv = ps[:, 5, :].rearrange("p (t e) -> p t e", e=E1)
            wide = [P, NT, E1]
            step(dve.tensor_reduce(r_max[:, :], lgv, AX_X, ALU.max))
            settle()
            dve.tensor_tensor(lg1[:, :, :], lgv, r_max[:, :, None].broadcast_to(wide), ALU.subtract) \
                .then_inc(lg1_shift, 1)
            dve.wait_ge(prob_exp, 1)
            step(dve.tensor_reduce(r_sum[:, :], prob1[:, :, :], AX_X, ALU.add))
            settle()
            step(dve.reciprocal(r_rec[:, :], r_sum[:, :]))
            settle()
            step(dve.tensor_tensor(lg1[:, :, :], prob1[:, :, :], r_rec[:, :, None].broadcast_to(wide), ALU.mult))
            settle()
            for t in range(NT):
                step(dve.max(r_top[:, t, :], lg1[:, t, :]))
            settle()
            for t in range(NT):
                step(dve.max_index(r_idx[:, t, :], r_top[:, t, :], lg1[:, t, :]))
            eight = [P, NT, TOP]
            step(dve.tensor_reduce(r_sum[:, :], r_top[:, :, :], AX_X, ALU.add))
            settle()
            step(dve.tensor_copy(r_idxf[:, :, :], r_idx[:, :, :]))
            step(dve.tensor_scalar(r_max[:, :], r_sum[:, :], 1e-12, None, ALU.max))
            settle()
            step(dve.reciprocal(r_rec[:, :], r_max[:, :]))
            settle()
            step(dve.tensor_tensor(r_cum[:, :, :], r_top[:, :, :], r_rec[:, :, None].broadcast_to(eight), ALU.mult))
            settle()
            for r in range(1, TOP):
                step(dve.tensor_tensor(r_cum[:, :, r], r_cum[:, :, r - 1], r_cum[:, :, r], ALU.add))
                settle()
            step(dve.tensor_scalar(r_on[:, :, 1:TOP], r_cum[:, :, 0:TOP - 1], KEEP, None, ALU.is_lt))
            step(dve.memset(r_on[:, :, 0:1], 1.0))
            settle()
            step(dve.tensor_tensor(r_rw[:, :, :], r_top[:, :, :], r_on[:, :, :], ALU.mult))
            settle()
            step(dve.tensor_reduce(r_sum[:, :], r_rw[:, :, :], AX_X, ALU.add))
            settle()
            step(dve.tensor_scalar(r_max[:, :], r_sum[:, :], 1e-12, None, ALU.max))
            settle()
            step(dve.reciprocal(r_rec[:, :], r_max[:, :]))
            settle()
            step(dve.tensor_tensor(r_cum[:, :, :], r_rw[:, :, :], r_rec[:, :, None].broadcast_to(eight), ALU.mult))
            settle()
            for r in range(TOP):
                step(dve.tensor_tensor(hit1[:, :, :], iota[:, None, :].broadcast_to(wide),
                                       r_idxf[:, :, r:r + 1].broadcast_to(wide), ALU.is_equal))
                settle()
                if r == 0:
                    step(dve.tensor_tensor(comb1[:, :, :], hit1[:, :, :],
                                           r_cum[:, :, r:r + 1].broadcast_to(wide), ALU.mult))
                else:
                    step(dve.tensor_tensor(prob1[:, :, :], hit1[:, :, :],
                                           r_cum[:, :, r:r + 1].broadcast_to(wide), ALU.mult))
                    settle()
                    step(dve.tensor_tensor(comb1[:, :, :], comb1[:, :, :], prob1[:, :, :], ALU.add))
                settle()
            for b in range(NB):
                dve.tensor_copy(cex[:, TPB * b:TPB * (b + 1), :].rearrange("p t (r e) -> p t r e", e=E1),
                                comb1[:, TPB * b:TPB * (b + 1), None, :].broadcast_to([P, TPB, RPT, E1])) \
                    .then_inc(ce_wide.sem, 1)

            for hf in range(2):
                for j in range(JT):
                    n = hj_no(hf, j)
                    for tb in range(2):
                        key = (hf, j, tb)
                        dve.wait_ge(*silu1_ready.after(key))
                        dve.tensor_tensor(hmul[:, tb, :], ps[:, 5 + 2 * tb, :], silu1[:, tb, :], ALU.mult) \
                            .then_inc(hmul_ready.sem, 1)
                        dve.wait_ge(*hmul_ready.after(key))
                        col = BLK * (2 * hf + tb)
                        if n == 0 and tb == 0:
                            dve.wait_ge(*ce_sb.after(NB - 1))
                        dve.tensor_tensor(hfull[:, tb, :], hmul[:, tb, :], ce_bc[:, col:col + BLK], ALU.mult) \
                            .then_inc(h_full.sem, 1)
                        dve.wait_ge(*h_hi.after(key))
                        low(hpart[:, n % 2, tb, 1, :], hfull[:, tb, :], hpart[:, n % 2, tb, 0, :]) \
                            .then_inc(h_lo.sem, 1)
                dve.wait_ge(*down1.after((hf, JT - 1)))
                for b in range(2 * hf, 2 * hf + 2):
                    for t in range(TPB * b, TPB * (b + 1)):
                        a = t - 8 * hf
                        dve.tensor_tensor(x[:, t, :], ps[:, a // 2, H * (a % 2):H * (a % 2 + 1)], x[:, t, :], ALU.add) \
                            .then_inc(acc_read.sem, 1)
                    dve.wait_ge(*acc_read.after((hf, TPB * (b + 1) - 1 - 8 * hf)))
                    layer_norm("D", b)

        @block.tensor
        def _(pe):
            def product(out, pairs, first=True, last=True, **more):
                n, todo = 0, len(pairs) * len(PARTS)
                for lhs, rhs in pairs:
                    for i, k in PARTS:
                        n += 1
                        mm = pe.matmul(out, lhs(i), rhs(k), start=first and n == 1, stop=last and n == todo, **more)
                return mm

            def turn(st, b, src):
                for c in range(NC):
                    for t in range(TPB):
                        mm = pe.transpose(ps[:, 6 + c, P * t:P * (t + 1)], src[:, TPB * b + t, P * c:P * (c + 1)],
                                          ident[:, :])
                    mm.then_inc(turned.sem, 1)

            for t in range(NT):
                if t % TPB == 0:
                    pe.wait_ge(x_in[t // TPB], 16)
                for c in range(NC):
                    mm = pe.matmul(ps[:, c, 0:H], x[:, t, P * c:P * (c + 1)], x[:, t, :], start=t == 0, stop=t == NT - 1)
                    if t == NT - 1:
                        mm.then_inc(energy_ready.sem, 1)
            pe.wait_ge(consts_in, 80)
            for j in range(NC):
                for c in range(NC):
                    if j == 0:
                        pe.wait_ge(*att_norm.after(c))
                    mm = pe.transpose(ps[:, 2 + j, P * c:P * (c + 1)], attn[:, c, P * j:P * (j + 1)], ident[:, :])
                mm.then_inc(att_tps.sem, 1)
            pe.wait_ge(xfm_in, 16)
            pe.wait_ge(*att_tsb.after(NC - 1))
            for t in range(NT):
                if t >= 4:
                    pe.wait_ge(*mix_read.after(t - 4))
                for j in range(NC):
                    mm = pe.matmul(ps[:, 4 + t % 4, 0:H], xt_in[:, j, P * t:P * (t + 1)], att_t[:, j, :],
                                   start=j == 0, stop=j == NC - 1)
                mm.then_inc(mix_ready.sem, 1)

            pe.wait_ge(*w0_ready.after("wg0"))
            pe.wait_ge(lora_in, 32)
            for b in range(NB):
                pe.wait_ge(*ln_ready.after(("A", b)))
                if b == 0:
                    pe.wait_ge(*mix_read.after(NT - 1))
                else:
                    pe.wait_ge(*lora2_read.after((b - 1, TPB - 1)))
                turn("B", b, x)
                for c in range(NC):
                    pe.wait_ge(*turned_lo.after(("B", b, c)))
                for t in range(TPB):
                    mm = product(ps[:, 6, E0 * t:E0 * (t + 1)],
                                 [(lambda i, c=c: xtb[:, i, c, P * t:P * (t + 1)], lambda k, c=c: wg0[:, k, c, :])
                                  for c in range(NC)])
                mm.then_inc(logits0.sem, 1)
                for w in range(2):
                    for m in range(NC):
                        product(ps[:, 2 * w + m, :],
                                [(lambda i, c=c: a13[:, i, c, w, P * m:P * (m + 1)], lambda k, c=c: xtb[:, k, c, :])
                                 for c in range(NC)]).then_inc(a_ps.sem, 1)

                def hidden(j, w, first, last):
                    s = (j + 2) % 3
                    return product(ps[:, 2 * s + w, :],
                                   [(lambda i, c=c: w13[:, i, c, w, P * j:P * (j + 1)], lambda k, c=c: xtb[:, k, c, :])
                                    for c in range(NC)], first, last, skip_group_check=True)

                def lora(j, k, w):
                    s = (j + 2) % 3
                    for c in range(NC):
                        if j == 0:
                            pe.wait_ge(*ma_ready.after((b, k, w, c)))
                        mm = pe.matmul(ps[:, 2 * s + w, :], b13[:, c, w, P * j:P * (j + 1)], ma[:, w, k, c, :],
                                       start=False, stop=c == NC - 1, skip_group_check=True)
                    return mm

                order = list(tile_order())
                for w in range(2):
                    hidden(0, w, True, False)
                for k in range(2):
                    pe.wait_ge(*mask_wide.after((b, k)))
                    for t in range(TPB):
                        mm = pe.transpose(ps[:, 6 + k, P * t:P * (t + 1)], mx[:, k, t, :], ident[:, :])
                    mm.then_inc(mask_ps.sem, 1)
                for n, (j, k) in enumerate(order):
                    if k == 0 and j:
                        if j >= 3:
                            pe.wait_ge(*x2_full.after((b, j - 3, 1)))
                        elif j >= 1:
                            pe.wait_ge(*ma_ready.after((b, 1, 1, NC - 1)))
                        for w in range(2):
                            hidden(j, w, True, False)
                    if k == 1:
                        pe.wait_ge(*x2_full.after((b, j, 0)))
                    for w in range(2):
                        mm = lora(j, k, w)
                    mm.then_inc(mlp_ps.sem, 1)

                def lora_out(t):
                    pe.wait_ge(*gt_ready.after((b, t)))
                    if t:
                        pe.wait_ge(*lora2_read.after((b, t - 1)))
                    for c in range(NC):
                        mm = pe.matmul(ps[:, 7, 0:H], gt[:, c, :], b2[:, c, :], start=c == 0, stop=c == NC - 1)
                    mm.then_inc(lora2_ps.sem, 1)

                def turn_g(t):
                    pe.wait_ge(*g_ready.after((b, t)))
                    if t:
                        pe.wait_ge(*gt_ready.after((b, t - 1)))
                    for c in range(NC):
                        mm = pe.transpose(ps[:, 6, P * c:P * (c + 1)], gsum[:, P * c:P * (c + 1)], ident[:, :])
                    mm.then_inc(g_turned.sem, 1)

                pe.wait_ge(*x2_full.after((b,) + order[-1]))
                pe.wait_ge(*x2_lo.after((b,) + order[-1]))
                for t in range(TPB):
                    for k in range(2):
                        if 2 * t + k >= 4:
                            pe.wait_ge(*down0_read.after((b, t - 2, k)))
                        product(ps[:, (2 * t + k) % 4, :],
                                [(lambda i, j=j: x2[:, i, k, j, P * t:P * (t + 1)], lambda q, j=j: w2a2[:, q, j, :])
                                 for j in range(FT)]).then_inc(down0.sem, 1)
                        if t and k == 0:
                            turn_g(t - 1)
                    if t:
                        lora_out(t - 1)
                turn_g(TPB - 1)
                lora_out(TPB - 1)

            pe.wait_ge(wqkv_ready, 1)
            for b in range(NB):
                pe.wait_ge(*ln_ready.after(("B", b)))
                if b:
                    for c in range(NC):
                        pe.wait_ge(*turned_lo.after(("C", b - 1, c)))
                turn("C", b, x)
                pe.wait_ge(*turned_lo.after(("C", b, NC - 1)))
                for m in range(4):
                    if b:
                        pe.wait_ge(*qk_lo.after((b - 1, m)))
                    product(ps[:, m, :],
                            [(lambda i, c=c: wqkv[:, i, c, P * m:P * (m + 1)],
                              lambda k, c=c: xtc[:, k, c, BLK * b:BLK * (b + 1)]) for c in range(NC)]) \
                        .then_inc(qk_ps.sem, 1)
                for t in range(TPB * b, TPB * (b + 1)):
                    if t >= 2:
                        pe.wait_ge(*v_ready.after(t - 2))
                    product(ps[:, 4 + t % 2, 0:H],
                            [(lambda i, c=c: xtc[:, i, c, P * t:P * (t + 1)], lambda k, c=c: wqkv[:, k, c, 2 * H:3 * H])
                             for c in range(NC)]).then_inc(v_ps.sem, 1)

            pe.wait_ge(*v_ready.after(NT - 1))
            pe.wait_ge(*qk_lo.after((NB - 1, 3)))
            pe.wait_ge(ones_in, 16 * 8 * 4)
            per_stack = 12 * 16

            def score_units(s):
                for u in units_of.get(s, []):
                    g, h, qt, kb = u
                    if (qt, kb) == (0, 0):
                        pe.wait_ge(stack_in[g % 2][h], per_stack * (g // 2 + 1))
                    last = kb == qt // TPB
                    width = P * (qt % TPB + 1) if last else BLK
                    n = unit_no[u]
                    if n >= 2:
                        pe.wait_ge(*reduced.after(all_units[n - 2]))
                    mm = pe.matmul(ps[:, 4 + n % 2, 0:width], stack[:, g % 2, 0, h, P * qt:P * (qt + 1)],
                                   stack[:, g % 2, 1, h, BLK * kb:BLK * kb + width], start=True, stop=not last)
                    if last:
                        mm = pe.matmul(ps[:, 4 + n % 2, width - P:width], identb[:, :], trimax[:, :],
                                       start=False, stop=True)
                    mm.then_inc(scored.sem, 1)

            def values(r):
                g, qb, kt = real[r]
                off = max(0, kt - TPB * qb) * P
                pe.wait_ge(*exp_done.after((r, 1)))
                if kt == 0 and gq.index((g, qb)):
                    pe.wait_ge(*u_copied.after(gq[gq.index((g, qb)) - 1]))
                for h in range(GH):
                    v0 = (kt * HEADS + GH * g + h) * VW
                    mm = pe.matmul(ps[32 * h:32 * (h + 1), 6, off:BLK], vaug[:, v0:v0 + 32],
                                   probs[:, (2 * r + h // 2) % 4, h % 2, off:BLK],
                                   start=kt == 0, stop=kt == TPB * (qb + 1) - 1, skip_group_check=True)
                mm.then_inc(pv_done.sem, 1)

            for s in range(len(steps) + 3):
                r = s - n_pre
                if 0 <= r < len(real):
                    g, qb, kt = real[r]
                    diag = kt >= TPB * qb
                    off = max(0, kt - TPB * qb) * P
                    for p in range(2):
                        if r:
                            pe.wait_ge(*exp_done.after((r - 1, p)))
                        for i in range(2):
                            h = 2 * p + i
                            if qb == 0 and kt == 0:
                                pe.wait_ge(max_in[h], 32 * (g + 1))
                            mm = pe.matmul(ps[:, h, off:BLK], stack[:, g % 2, 1, h, P * kt:P * (kt + 1)],
                                           stack[:, g % 2, 0, h, BLK * qb + off:BLK * (qb + 1)],
                                           start=True, stop=not diag)
                            if diag:
                                mm = pe.matmul(ps[:, h, off:off + P], identb[:, :], triexp[:, :],
                                               start=False, stop=True)
                        mm.then_inc(st_ready.sem, 1)
                score_units(s)
                if s in head_end:
                    g, h = head_end[s]
                    pe.wait_ge(*head_max.after((g, h)))
                    misc_free(pe, ("max", (g, h)))
                    pe.transpose(ps[0:NT, 7, 0:P], nmx[:, (GH * g + h) % 2, :], ident[:, :]).then_inc(max_turned.sem, 1)
                if s in out_at:
                    g, qb = out_at[s]
                    pe.wait_ge(*u_copied.after((g, qb)))
                    misc_free(pe, ("out", (g, qb)))
                    for t in range(TPB):
                        mm = pe.transpose(ps[:, 7, P * t:P * (t + 1)], usum[:, P * t:P * (t + 1)], ident[:, :])
                    mm.then_inc(u_turned.sem, 1)
                if 0 <= r - 1 < len(real):
                    values(r - 1)

            pe.wait_ge(*o_ready.after(gq[-1]))
            pe.wait_ge(wo_ready, 1)
            for b in range(NB):
                if b:
                    for c in range(NC):
                        pe.wait_ge(*turned_lo.after(("O", b - 1, c)))
                turn("O", b, o_tm)
            pe.wait_ge(*turned_lo.after(("O", NB - 1, NC - 1)))
            for t in range(NT):
                if t >= 4:
                    pe.wait_ge(*proj_read.after(t - 4))
                product(ps[:, t % 4, 0:H],
                        [(lambda i, c=c: ot[:, i, c, P * t:P * (t + 1)], lambda k, c=c: wo[:, k, c, :])
                         for c in range(NC)]).then_inc(proj_ps.sem, 1)

            pe.wait_ge(wg1_ready, 1)
            for b in range(NB):
                pe.wait_ge(*ln_ready.after(("C", b)))
                if b:
                    for c in range(NC):
                        pe.wait_ge(*turned_lo.after(("D", b - 1, c)))
                turn("D", b, x)
                pe.wait_ge(*turned_lo.after(("D", b, NC - 1)))
                for t in range(TPB * b, TPB * (b + 1)):
                    mm = product(ps[:, 5, E1 * t:E1 * (t + 1)],
                                 [(lambda i, c=c: xtd[:, i, c, P * t:P * (t + 1)], lambda k, c=c: wg1[:, k, c, :])
                                  for c in range(NC)])
            mm.then_inc(logits1, 1)
            for b in range(NB):
                pe.wait_ge(*ce_wide.after(b))
                for t in range(TPB):
                    mm = pe.transpose(ps[:, b, P * t:P * (t + 1)], cex[:, TPB * b + t, :], ident[:, :])
                mm.then_inc(ce_ps.sem, 1)

            def down(hf, j):
                n = hj_no(hf, j)
                for tb in range(2):
                    pe.wait_ge(*h_lo.after((hf, j, tb)))
                for a in range(8):
                    if j == 0 and hf:
                        pe.wait_ge(*acc_read.after((hf - 1, 7)))
                    tb, t = a // 4, a % 4
                    mm = product(ps[:, a // 2, H * (a % 2):H * (a % 2 + 1)],
                                 [(lambda i: hpart[:, n % 2, tb, i, P * t:P * (t + 1)], lambda k: dn[:, n % 3, k, :])],
                                 j == 0 and a % 2 == 0, j == JT - 1, skip_group_check=True)
                mm.then_inc(down1.sem, 1)

            pe.wait_ge(*ce_sb.after(NB - 1))
            for hf in range(2):
                for j in range(JT):
                    n = hj_no(hf, j)
                    pe.wait_ge(*wd_lo.after((hf, j)))
                    for tb in range(2):
                        if n:
                            pe.wait_ge(*hmul_ready.after(hjt[2 * n + tb - 2]))
                        col = BLK * (2 * hf + tb)
                        for w in range(2):
                            mm = product(ps[:, 4 + 2 * tb + w, :],
                                         [(lambda i, c=c: gu[:, n % 3, i, c, w, :],
                                           lambda k, c=c: xtd[:, k, c, col:col + BLK]) for c in range(NC)])
                        mm.then_inc(gu_ps.sem, 1)
                    if j:
                        down(hf, j - 1)
                down(hf, JT - 1)


def kernel(**inputs):
    from concourse.bass_utils import run_bass_kernel_spmd
    import ml_dtypes

    a = {k: np.asarray(v) for k, v in inputs.items()}

    def lay(v):
        return np.ascontiguousarray(v)

    def rows(v, chunks):
        return v.reshape((chunks, P) + v.shape[1:]).swapaxes(0, 1)

    xs = a["L0_attn_x"][0]
    A = [a["L0_ffn_A1"], a["L0_ffn_A3"]]
    B = [a["L0_ffn_B1"], a["L0_ffn_B3"]]
    gup = a["L1_ffn_gate_up_proj"].reshape(E1, 2, JT, RPT, H)
    k = np.arange(P)
    arrays = {
        "x_tm": rows(xs, NT),
        "x_fm": rows(xs.T, NC),
        "w13": rows(np.stack([a["L0_ffn_W1"].T, a["L0_ffn_W3"].T], 1), NC),
        "a13": rows(np.stack([m.transpose(2, 1, 0).reshape(H, E0 * R0) for m in A], 1), NC),
        "b13": rows(np.stack([m.transpose(2, 0, 1).reshape(E0 * R0, F) for m in B], 1), NC),
        "w2a2": rows(np.concatenate([a["L0_ffn_W2"].T, a["L0_ffn_A2"].transpose(2, 1, 0).reshape(F, E0 * R0)], 1), FT),
        "b2": rows(a["L0_ffn_B2"].transpose(2, 0, 1).reshape(E0 * R0, H), NC),
        "wg0": rows(a["L0_ffn_Wg"].T, NC),
        "wqkv": rows(a["L1_attn_w_qkv"].T, NC),
        "wo": rows(a["L1_attn_w_o"].T, NC),
        "wg1": rows(a["L1_ffn_gate_weight"].T, NC),
        "wgu": gup.transpose(4, 2, 1, 3, 0).reshape(NC, P, JT, 2, P).transpose(1, 2, 0, 3, 4).reshape(P, JT, NC * 2 * P),
        "wdn": a["L1_ffn_down_proj"].reshape(E1, H, JT, RPT).transpose(3, 0, 2, 1).reshape(P, JT, H),
        "ident": np.eye(P, dtype=np.float32),
        "identb": np.eye(P).astype(ml_dtypes.bfloat16),
        "trimax": np.where(k[None, :] > k[:, None], NEG, 0.0).astype(ml_dtypes.bfloat16),
        "triexp": np.where(k[:, None] > k[None, :], NEG, 0.0).astype(ml_dtypes.bfloat16),
        "iota": np.tile(np.arange(E1, dtype=np.float32), (P, 1)),
    }
    arrays = {f"in_{n}": lay(v) for n, v in arrays.items()}
    nc = bacc.Bacc("TRN2", target_bir_lowering=False, num_devices=1)
    args = [nc.dram_tensor(n, v.shape, mybir.dt.from_np(v.dtype), kind="ExternalInput").ap() for n, v in arrays.items()]
    out = nc.dram_tensor("out", (P, NT, H), F32, kind="ExternalOutput").ap()
    build(nc, *args, out)
    r = run_bass_kernel_spmd(nc, [arrays], core_ids=[0])
    return r.results[0]["out"].swapaxes(0, 1).reshape(1, T, H)
```

```python
from contextlib import ExitStack

import concourse.bass as bass
import concourse.bacc as bacc
from concourse import mybir
import numpy as np

F32, F32R, BF16, U32 = mybir.dt.float32, mybir.dt.float32r, mybir.dt.bfloat16, mybir.dt.uint32
ALU = mybir.AluOpType
ACT = mybir.ActivationFunctionType
AX_X = mybir.AxisListType.X

P = 128
T, H = 2048, 256
NT = T // P
NB, BLK = 4, 512
TPB = BLK // P
NC = H // P
F, FT = 896, 896 // P
E0, R0 = 8, 32
HEADS, HD = 16, 16
GH, NG = 4, 4
E1, I1, TOP = 32, 96, 8
RPT = P // E1
JT = I1 // RPT
PAIR = 2 * TPB
KEEP = 0.8
EPS = 1e-5
NEG = -3.0e38
MROW = 4 * HD
STK = 96
VW = HD + 1
PARTS = ((1, 0), (0, 1), (0, 0))


class Signal:

    def __init__(self, sem, events, by=1):
        self.sem, self.by = sem, by
        self.at = {e: n + 1 for n, e in enumerate(events)}

    def after(self, event):
        return self.sem, self.by * self.at[event]


def attention_plan():
    lead, rate = 88, 4
    steps = [None] * (lead // rate)
    steps += [(g, qb, kt) for g in range(NG) for qb in range(NB) for kt in range(TPB * (qb + 1))]
    units = [(g, h, qt, kb) for g in range(NG) for qb in range(NB) for h in range(GH)
             for qt in range(TPB * qb, TPB * (qb + 1)) for kb in range(qb + 1)]
    return steps, [units[rate * s:rate * (s + 1)] for s in range(len(steps) + 4)], units


def build(nc, x_tm, x_fm, w13_d, a13_d, b13_d, w2a2_d, b2_d, wg0_d, wqkv_d, wo_d, wg1_d, wgu_d, wdn_d,
          ident_d, identb_d, trimax_d, triexp_d, iota_d, out_d):
    with ExitStack() as ctx:
        def sem(name):
            return ctx.enter_context(nc.semaphore(name))

        def sig(name, events, by=1):
            return Signal(sem(name), list(events), by)

        base = (nc.sbuf_base + 31) // 32 * 32
        cursor = [base]

        def at(name, shape, dt, offset=None):
            size = int(np.prod(shape[1:])) * (2 if dt == BF16 else 4)
            if offset is None:
                offset = cursor[0]
            cursor[0] = (offset + size + 31) // 32 * 32
            return nc.alloc_sbuf_tensor_at(name, list(shape), dt, offset=offset)

        x = at("x", [P, NT, H], F32)
        ident = at("ident", [P, P], F32)
        identb = at("identb", [P, P], BF16)
        trimax = at("trimax", [P, P], BF16)
        triexp = at("triexp", [P, P], BF16)
        iota = at("iota", [P, E1], F32)
        half_neg = at("half_neg", [P, TPB], F32)
        ln_stats = at("ln_stats", [P, 2, TPB, 6], F32)
        ln_mv = at("ln_mv", [P, 2, TPB, 2], F32)
        ln_var = at("ln_var", [P, 2, TPB], F32)
        ln_rstd = at("ln_rstd", [P, 2, TPB], F32)
        R = cursor[0]

        xtb = at("xtb", [P, 2, NC, BLK], F32R, R)
        w13 = at("w13", [P, 2, NC, 2, F], F32R)
        a13 = at("a13", [P, 2, NC, 2, E0 * R0], F32R)
        b13 = at("b13", [P, 2, NC, 2, F], F32R)
        w2a2 = at("w2a2", [P, 2, FT, 2 * H], F32R)
        b2 = at("b2", [P, 2, NC, H], F32R)
        wg0 = at("wg0", [P, NC, E0], F32)
        MA = cursor[0]
        ma = at("ma", [P, 2, 2, 2, NC, BLK], F32R)
        silu0 = at("silu0", [P, 2, BLK], F32)
        x2f = at("x2f", [P, 2, BLK], F32)
        x2u = at("x2u", [P, 2, BLK], F32)
        bc = at("bc", [P, 4, BLK], F32)
        mx = at("mx", [P, 4, TPB, P], F32)
        lg0 = at("lg0", [P, TPB, E0], F32)
        top0 = at("top0", [P, TPB, 8], F32)
        idx0 = at("idx0", [P, TPB, 8], U32)
        idx0f = at("idx0f", [P, TPB, 2], F32)
        mask0 = at("mask0", [P, 2, TPB, E0], F32)
        mdiff = at("mdiff", [P, TPB, E0], F32)
        mw0 = at("mw0", [P, 2, TPB, E0], F32)
        gap0 = at("gap0", [P, TPB], F32)
        exp0 = at("exp0", [P, TPB], F32)
        den0 = at("den0", [P, TPB], F32)
        rw0 = at("rw0", [P, 2, TPB], F32)
        x2 = at("x2", [P, 2, 2, 3, BLK], F32R)
        B_END = cursor[0]
        g_part = at("g_part", [P, 2, NC, BLK], F32R, MA)
        xt_in = at("xt_in", [P, NC, T], F32, MA)
        att = at("att", [P, NC, H], F32)
        attn = at("attn", [P, NC, H], F32)
        att_t = at("att_t", [P, NC, H], F32)
        nmax_a = at("nmax_a", [P, NC], F32)
        sum_a = at("sum_a", [P, NC], F32)
        rec_a = at("rec_a", [P, NC], F32)
        w13_raw = at("w13_raw", [P, NC, 2, F], F32)
        a13_raw = at("a13_raw", [P, NC, 2, E0 * R0], F32)
        b13_raw = at("b13_raw", [P, NC, 2, F], F32)
        w2a2_raw = at("w2a2_raw", [P, FT, 2 * H], F32)
        b2_raw = at("b2_raw", [P, NC, H], F32)
        assert cursor[0] <= B_END, (cursor[0], B_END)

        o_tm = at("o_tm", [P, NT, H], F32, R)
        vaug = at("vaug", [P, NT * HEADS * VW + 15], F32)
        stack = at("stack", [STK, 2, 2, GH, T], F32R)
        SET = 2 * GH * T * 4
        S0 = cursor[0] - 2 * SET
        S1 = S0 + SET
        probs = at("probs", [P, 4, 2, BLK], F32)
        PR = cursor[0] - 4 * 2 * BLK * 4
        usum = at("usum", [P, BLK], F32)
        mpart = at("mpart", [P, 2, GH * TPB, NB], F32)
        nmx = at("nmx", [P, 2, GH * TPB], F32)
        mrow = at("mrow", [GH * TPB, 2, 2, P], F32R)
        row_fill = at("row_fill", [2, 2, 256], F32R)
        rec_c = at("rec_c", [P, TPB, GH], F32)
        xtc = at("xtc", [P, 2, NC, T], F32R, S1)
        wqkv = at("wqkv", [P, 2, NC, 3 * H], F32R)
        qk_out = at("qk_out", [P, 2, 2, BLK], F32R)
        assert cursor[0] <= S1 + SET
        wqkv_raw = at("wqkv_raw", [P, NC, 3 * H], F32, PR)
        ot = at("ot", [P, 2, NC, T], F32R, S0)
        wo = at("wo", [P, 2, NC, H], F32R)
        wo_raw = at("wo_raw", [P, NC, H], F32)
        gu_raw = at("gu_raw", [P, 3, NC * 2 * P], F32)
        dn_raw = at("dn_raw", [P, 3, H], F32)
        wg1_raw = at("wg1_raw", [P, NC, E1], F32)
        wg1 = at("wg1", [P, 2, NC, E1], F32R)
        assert cursor[0] <= S1
        xtd = at("xtd", [P, 2, NC, T], F32R, S1)
        gu = at("gu", [P, 3, 2, NC, 2, P], F32R)
        dn = at("dn", [P, 3, 2, H], F32R)
        assert cursor[0] <= PR
        lg1 = at("lg1", [P, 2, PAIR, E1], F32, R)
        exp1 = at("exp1", [P, 2, PAIR, E1], F32)
        prob1 = at("prob1", [P, PAIR, E1 + 8], F32)
        rest1 = at("rest1", [P, PAIR, E1 + 8], F32)
        comb1 = at("comb1", [P, PAIR, E1], F32)
        cex = at("cex", [P, 2, TPB, P], F32)
        ce_bc = at("ce_bc", [P, T], F32)
        assert cursor[0] <= S0, (cursor[0], S0)
        silu1 = at("silu1", [P, 2, BLK], F32, PR)
        hmul = at("hmul", [P, 2, BLK], F32)
        hfull = at("hfull", [P, 2, BLK], F32)
        r_max = at("r_max", [P, PAIR], F32)
        r_sum = at("r_sum", [P, PAIR], F32)
        r_rec = at("r_rec", [P, PAIR], F32)
        r_top = at("r_top", [P, PAIR, 8], F32)
        r_cum = at("r_cum", [P, PAIR, 8], F32)
        r_on = at("r_on", [P, PAIR, 8], F32)
        r_rw = at("r_rw", [P, PAIR, 8], F32)
        r_val = at("r_val", [P, PAIR, 8], F32)
        assert cursor[0] <= nc.sbuf_usable_end
        hpart = at("hpart", [P, 2, 2, 2, BLK], F32R, S0)

        ps = nc.alloc_psum_tensor("ps", [P, 8, 512], F32)
        qk_dram = nc.dram_tensor("qk_dram", [4, 2, P, T], F32)

        consts_in = sem("consts_in")
        x_in = [sem(f"x_in{b}") for b in range(NB)]
        xfm_in = sem("xfm_in")
        w0_in = {n: sem(f"w0_in_{n}") for n in ("w13", "a13", "b13", "w2a2", "b2")}
        lora_in = sem("lora_in")
        pool_const = sem("pool_const")
        w0_order = ["w13", "a13", "b13", "w2a2", "b2"]
        w0_hi = sig("w0_hi", w0_order)
        dve_step = sem("dve_step")
        pool_step = sem("pool_step")
        w0_ready = sig("w0_ready", w0_order)

        energy_ready = sig("energy_ready", range(NC))
        nmax_ready = sig("nmax_ready", range(NC))
        att_exp = sig("att_exp", range(NC))
        att_norm = sig("att_norm", range(NC))
        att_tps = sig("att_tps", range(NC))
        att_tsb = sig("att_tsb", range(NC))
        mix_ready = sig("mix_ready", range(NT))
        mix_read = sig("mix_read", range(NT))

        blocks = [(st, b) for st in "ABCD" for b in range(NB)]
        var_ready = sig("var_ready", blocks)
        rstd_ready = sig("rstd_ready", blocks)
        ln_ready = sig("ln_ready", blocks)

        turns = [(st, b, c) for st in "BCOD" for b in range(NB) for c in range(NC)]
        turned = sig("turned", turns)
        turned_hi = sig("turned_hi", turns)
        turned_lo = sig("turned_lo", turns)

        bb = range(NB)
        logits0 = sig("logits0", bb)
        gap_ready = sig("gap_ready", bb)
        gap_exp = sig("gap_exp", bb)
        wides = [(b, i) for b in bb for i in ("mask0", "mask1", "rw0", "rw1", "mw0", "mw1")]
        wide = sig("wide", wides)
        wide_ps = sig("wide_ps", wides)
        wide_sb = sig("wide_sb", wides)
        a_ps = sig("a_ps", [(b, w, c) for b in bb for w in range(2) for c in range(NC)])
        bkwc = [(b, k, w, c) for b in bb for k in range(2) for w in range(2) for c in range(NC)]
        ma_full = sig("ma_full", bkwc)
        ma_hi = sig("ma_hi", bkwc)
        ma_lo = sig("ma_lo", bkwc)
        jk = [(b, j, k) for b in bb for j in range(FT) for k in range(2)]
        mlp_ps = sig("mlp_ps", jk)
        silu_ready = sig("silu_ready", jk)
        jks = [(b, j, k) for b in bb for j in range(FT) for k in range(3)]
        x2_full = sig("x2_full", jks)
        x2_hi = sig("x2_hi", jks)
        x2_lo = sig("x2_lo", jks)
        down0 = sig("down0", [(b, j) for b in bb for j in range(FT)])
        bc2 = [(b, c) for b in bb for c in range(NC)]
        g_full = sig("g_full", bc2)
        g_hi = sig("g_hi", bc2)
        g_lo = sig("g_lo", bc2)
        out0 = sig("out0", bb)
        bt = [(b, t) for b in bb for t in range(TPB)]
        out0_read = sig("out0_read", bt)

        wqkv_in = sem("wqkv_in")
        wqkv_hi = sem("wqkv_hi")
        wqkv_ready = sem("wqkv_ready")
        bm = [(b, m) for b in bb for m in range(4)]
        qk_ps = sig("qk_ps", bm)
        qk_hi = sig("qk_hi", bm)
        qk_lo = sig("qk_lo", bm)
        qk_out_sem = [sem(f"qk_out_slot{i}") for i in range(2)]
        v_ps = sig("v_ps", range(NT))
        v_ready = sig("v_ready", range(NT))
        v_ones = sem("v_ones")

        fill_ready = sem("fill_ready")
        pad_zero = [sem(f"pad_zero{i}") for i in range(2)]
        ones_in = [sem(f"ones_in{i}") for i in range(2)]
        first_in = [sem(f"first_in{b}") for b in bb]
        stack_in = [sem(f"stack_in{i}") for i in range(2)]
        max_in = [sem(f"max_in{b}") for b in bb]

        steps, units_at, units = attention_plan()
        real = [r for r in steps if r]
        n_pre = len(steps) - len(real)
        per_group = len(real) // NG
        unit_no = {u: n for n, u in enumerate(units)}
        scored = sig("scored", units)
        reduced = sig("reduced", units)
        rounds = [(g, qb) for g in range(NG) for qb in range(NB)]
        round_no = {r: n for n, r in enumerate(rounds)}
        round_max = sig("round_max", rounds)
        max_turned = sig("max_turned", rounds)
        max_hi = sig("max_hi", rounds)
        max_lo = sig("max_lo", rounds)
        sp = [(s, p) for s in range(len(real)) for p in range(2)]
        st_ready = sig("st_ready", sp)
        exp_done = sig("exp_done", sp)
        pv_done = sig("pv_done", range(len(real)))
        u_copied = sig("u_copied", rounds)
        u_turned = sig("u_turned", rounds)
        o_ready = sig("o_ready", rounds)

        def closes(u):
            g, h, qt, kb = u
            return (g, kb) if (h, qt) == (GH - 1, TPB * kb + TPB - 1) else None

        max_at = {s + 1: closes(u) for s in range(len(units_at)) for u in units_at[s] if closes(u)}
        out_at = {n_pre + n + 2: (g, qb) for n, (g, qb, kt) in enumerate(real) if kt == TPB * (qb + 1) - 1}
        n_steps = len(steps) + 3
        misc = []
        for s in range(n_steps):
            if s in max_at:
                misc.append(("max", max_at[s]))
            if s in out_at:
                misc.append(("out", out_at[s]))

        def misc_free(eng, item):
            n = misc.index(item)
            if n:
                kind, key = misc[n - 1]
                eng.wait_ge(*(max_lo if kind == "max" else o_ready).after(key))

        wo_in = sem("wo_in")
        wo_hi = sem("wo_hi")
        wo_ready = sem("wo_ready")
        proj_ps = sig("proj_ps", range(NT))
        proj_read = sig("proj_read", range(NT))

        wg1_in = sem("wg1_in")
        wg1_hi = sem("wg1_hi")
        wg1_ready = sem("wg1_ready")
        logits1 = sig("logits1", bb)
        lg1_shift = sig("lg1_shift", range(2))
        prob_exp = sig("prob_exp", range(2))
        ce_wide = sig("ce_wide", bb)
        ce_ps = sig("ce_ps", bb)
        ce_sb = sig("ce_sb", bb)
        hj = [(hf, j) for hf in range(2) for j in range(JT)]
        raw_in = [sem(f"raw_in{i}") for i in range(3)]
        gu_hi_only = sem("gu_hi")
        wd_hi = sig("wd_hi", hj)
        wd_lo = sig("wd_lo", hj)
        hjt = [(hf, j, tb) for hf, j in hj for tb in range(2)]
        gu_ps = sig("gu_ps", hjt)
        silu1_ready = sig("silu1_ready", hjt)
        hmul_ready = sig("hmul_ready", hjt)
        h_full = sig("h_full", hjt)
        h_hi = sig("h_hi", hjt)
        h_lo = sig("h_lo", hjt)
        down1 = sig("down1", hj)
        acc_read = sig("acc_read", [(hf, t) for hf in range(2) for t in range(8)])
        stored = sem("stored")

        def hj_no(hf, j):
            return hf * JT + j

        wide_place = {"mask0": (0, 0), "mask1": (1, 1), "rw0": (2, 2), "rw1": (3, 3), "mw0": (0, 4), "mw1": (1, 5)}

        def turn_bank(st, b, c):
            return {"B": 0, "C": 6, "O": 4, "D": 2 + 2 * (b % 2)}[st] + c

        last_round = real.index((NG - 1, NB - 1, 0))

        def tail_turn(r):
            n = r - last_round
            return n // 5 if n >= 0 and n % 5 == 0 and n // 5 < NB - 1 else None

        def tail_tile(r):
            n = r - last_round
            return TPB * (n // 5) + n % 5 - 1 if n >= 0 and n % 5 and n // 5 < NB - 1 else None

        def proj_bank(t):
            return t % 2 + (4 if t < NT - TPB else 0)

        block = ctx.enter_context(nc.Block())

        @block.sync
        def _(sp_):
            for b in range(NB):
                sp_.dma_start(x[:, TPB * b:TPB * (b + 1), :], x_tm[:, TPB * b:TPB * (b + 1), :]).then_inc(x_in[b], 16)
            sp_.dma_start(ident[:, :], ident_d).then_inc(consts_in, 16)
            sp_.dma_start(identb[:, :], identb_d).then_inc(consts_in, 16)
            sp_.dma_start(trimax[:, :], trimax_d).then_inc(consts_in, 16)
            sp_.dma_start(triexp[:, :], triexp_d).then_inc(consts_in, 16)
            sp_.dma_start(iota[:, :], iota_d).then_inc(consts_in, 16)
            sp_.dma_start(xt_in[:, :, :], x_fm).then_inc(xfm_in, 16)
            for n, raw, src in (("w13", w13_raw, w13_d), ("a13", a13_raw, a13_d), ("b13", b13_raw, b13_d), ("w2a2", w2a2_raw, w2a2_d),
                                ("b2", b2_raw, b2_d)):
                sp_.dma_start(raw.ap(), src).then_inc(w0_in[n], 16)
            sp_.dma_start(wg0[:, :, :], wg0_d).then_inc(lora_in, 16)
            sp_.wait_ge(*out0_read.after((NB - 1, TPB - 1)))
            sp_.dma_start(wqkv_raw[:, :, :], wqkv_d).then_inc(wqkv_in, 16)

            def load_stacks(g, t0, t1, done):
                m, r = g // 2, GH * HD * (g % 2)
                for i in range(2):
                    for n in range(2):
                        for which, part in ((0, i), (1, n)):
                            lo = HD * (2 * i + n)
                            sp_.dma_start(stack[lo:lo + HD, g % 2, which, :, t0:t1].bitcast(F32),
                                          qk_dram[2 * which + m, part, r:r + GH * HD, t0:t1]
                                          .rearrange("(h r) t -> r h t", r=HD)).then_inc(done, 16)

            def fill_rows(i, which, value, done):
                for n in range(T // 256):
                    sp_.dma_start(stack[MROW:MROW + 2, i, which, :, 256 * n:256 * (n + 1)].bitcast(F32),
                                  row_fill[:, value, None, :].broadcast_to([2, GH, 256]).bitcast(F32)) \
                        .then_inc(done, 16)

            sp_.wait_ge(fill_ready, 2)
            sp_.wait_ge(pad_zero[0], 1)
            fill_rows(0, 1, 1, ones_in[0])
            for b in range(NB):
                for m in range(4):
                    n = 4 * b + m
                    sp_.wait_ge(*qk_lo.after((b, m)))
                    sp_.dma_start(qk_dram[m, :, :, BLK * b:BLK * (b + 1)].rearrange("s p t -> p s t"),
                                  qk_out[:, n % 2, :, :].bitcast(F32)).then_inc(qk_out_sem[n % 2], 16)
                for i in range(2):
                    sp_.wait_ge(qk_out_sem[i], 32 * (b + 1))
                load_stacks(0, BLK * b, BLK * (b + 1), first_in[b])
            for g in range(1, NG):
                if g == 1:
                    sp_.wait_ge(pad_zero[1], 1)
                    fill_rows(1, 1, 1, ones_in[1])
                else:
                    sp_.wait_ge(*st_ready.after(((g - 1) * per_group - 1, 1)))
                    fill_rows(g % 2, 0, 0, stack_in[g % 2])
                load_stacks(g, 0, T, stack_in[g % 2])
            sp_.wait_ge(*st_ready.after(((NG - 1) * per_group - 1, 1)))
            sp_.dma_start(wo_raw[:, :, :], wo_d).then_inc(wo_in, 16)
            sp_.dma_start(wg1_raw[:, :, :], wg1_d).then_inc(wg1_in, 16)
            for n, (hf, j) in enumerate(hj):
                if n >= 3:
                    sp_.wait_ge(*wd_lo.after(hj[n - 3]))
                sp_.dma_start(gu_raw[:, n % 3, :], wgu_d[:, j, :]).then_inc(raw_in[n % 3], 16)
                sp_.dma_start(dn_raw[:, n % 3, :], wdn_d[:, j, :]).then_inc(raw_in[n % 3], 16)
            for b in range(NB):
                sp_.wait_ge(*ln_ready.after(("D", b)))
                sp_.dma_start(out_d[:, TPB * b:TPB * (b + 1), :], x[:, TPB * b:TPB * (b + 1), :]).then_inc(stored, 16)
            sp_.wait_ge(stored, 16 * NB)

        @block.gpsimd
        def _(pool):
            steps_done = [0]

            def settle(ins):
                steps_done[0] += 1
                ins.then_inc(pool_step, 1)
                pool.wait_ge(pool_step, steps_done[0])

            pool.memset(half_neg[:, :], -0.5).then_inc(pool_const, 1)
            pool.wait_ge(pool_const, 1)

            def rstd(st, b):
                pool.wait_ge(*var_ready.after((st, b)))
                pool.tensor_tensor(ln_rstd[:, b % 2, :], ln_var[:, b % 2, :], half_neg[:, :], ALU.pow) \
                    .then_inc(rstd_ready.sem, 1)

            def max_rows(g, qb):
                n = round_no[g, qb]
                pool.wait_ge(*max_lo.after((g, qb)))
                for h in range(GH):
                    for part in range(2):
                        row = MROW + part
                        pool.dma_start(stack[row:row + 1, g % 2, 0, h, BLK * qb:BLK * (qb + 1)].bitcast(F32)
                                       .rearrange("a (t q) -> a t q", q=P),
                                       mrow[TPB * h:TPB * (h + 1), n % 2, part, :].bitcast(F32)) \
                            .then_inc(max_in[qb], 16)

            for b in range(NB):
                rstd("A", b)
            for b in range(NB):
                rstd("B", b)
            pool.wait_ge(*out0_read.after((NB - 1, TPB - 1)))
            pool.wait_ge(*rstd_ready.after(("B", NB - 1)))
            for i in range(2):
                pool.memset(row_fill[:, i, :].bitcast(F32), float(i)).then_inc(fill_ready, 1)
            for i in range(2):
                if i:
                    pool.wait_ge(*v_ps.after(NT - 1))
                    for n in range(2):
                        pool.wait_ge(qk_out_sem[n], 32 * NB)
                pool.wait_ge(fill_ready, 2)
                if i:
                    pool.wait_ge(pad_zero[0], 1)
                pool.memset(stack[MROW:STK, i, :, :, :].rearrange("p a h t -> p (a h t)").bitcast(F32), 0.0) \
                    .then_inc(pad_zero[i], 1)
            for g, qb in rounds:
                max_rows(g, qb)
            for b in range(NB):
                rstd("C", b)
            for hf in range(2):
                for j in range(JT):
                    n = hj_no(hf, j)
                    pool.wait_ge(*wd_hi.after((hf, j)))
                    settle(pool.tensor_tensor(gu[:, n % 3, 1, :, :, :].rearrange("p a b c -> p (a b c)"),
                                              gu_raw[:, n % 3, :],
                                              gu[:, n % 3, 0, :, :, :].rearrange("p a b c -> p (a b c)").bitcast(F32),
                                              ALU.subtract))
                    pool.tensor_tensor(dn[:, n % 3, 1, :], dn_raw[:, n % 3, :], dn[:, n % 3, 0, :].bitcast(F32),
                                       ALU.subtract).then_inc(wd_lo.sem, 1)
                    if hf and j == 3:
                        for b in range(2):
                            rstd("D", b)
            for b in range(2, NB):
                rstd("D", b)

        @block.scalar
        def _(act):
            def copy(out, in_):
                return act.activation(out, in_, ACT.Copy)

            for c in range(NC):
                act.wait_ge(*nmax_ready.after(c))
                act.activation(att[:, c, :], ps[:, c, 0:H], ACT.Exp, bias=nmax_a[:, c:c + 1],
                               accum_out=sum_a[:, c:c + 1]).then_inc(att_exp.sem, 1)

            def turn_hi(st, b, dst):
                for c in range(NC):
                    act.wait_ge(*turned.after((st, b, c)))
                    copy(dst[:, 0, c, :] if st == "B" else dst[:, 0, c, BLK * b:BLK * (b + 1)], ps[:, turn_bank(st, b, c), :]) \
                        .then_inc(turned_hi.sem, 1)

            for n, raw, part in (("w13", w13_raw, w13), ("a13", a13_raw, a13), ("b13", b13_raw, b13), ("w2a2", w2a2_raw, w2a2),
                                 ("b2", b2_raw, b2)):
                act.wait_ge(w0_in[n], 16)
                copy(part[:, 0], raw.ap()).then_inc(w0_hi.sem, 1)

            def widen(b, names):
                for i in names:
                    act.wait_ge(*wide_ps.after((b, i)))
                    slot, bank = wide_place[i]
                    if b and i in ("rw0", "rw1"):
                        act.wait_ge(*x2_full.after((b - 1, FT - 1, 2)))
                    elif b and i in ("mask0", "mask1"):
                        act.wait_ge(*g_full.after((b - 1, NC - 1)))
                    elif i in ("mw0", "mw1"):
                        act.wait_ge(*ma_full.after((b, 1, 1, NC - 1)))
                    copy(bc[:, slot, :], ps[:, bank, :]).then_inc(wide_sb.sem, 1)

            turn_hi("B", 0, xtb)
            for b in range(NB):
                act.wait_ge(*gap_ready.after(b))
                act.activation(exp0[:, :], gap0[:, :], ACT.Exp).then_inc(gap_exp.sem, 1)
                widen(b, ("mask0", "mask1"))
                if b:
                    for c in range(NC):
                        act.wait_ge(*g_full.after((b - 1, c)))
                        copy(g_part[:, 0, c, :], x2f[:, c, :]).then_inc(g_hi.sem, 1)
                for i, (k, w, c) in enumerate([(k, w, c) for k in range(2) for w in range(2) for c in range(NC)]):
                    act.wait_ge(*ma_full.after((b, k, w, c)))
                    copy(ma[:, 0, w, k, c, :], x2f[:, i % 2, :]).then_inc(ma_hi.sem, 1)
                widen(b, ("rw0", "rw1", "mw0", "mw1"))

                for j in range(FT):
                    if j >= 2:
                        act.wait_ge(*down0.after((b, j - 2)))
                    elif b:
                        act.wait_ge(*down0.after((b - 1, FT - 1)))
                    for k in range(2):
                        act.wait_ge(*mlp_ps.after((b, j, k)))
                        act.activation(silu0[:, k, :], ps[:, 0, :], ACT.Silu).then_inc(silu_ready.sem, 1)
                        act.wait_ge(*x2_full.after((b, j, k)))
                        copy(x2[:, (b * FT + j) % 2, 0, k, :], x2f[:, k, :]).then_inc(x2_hi.sem, 1)
                    act.wait_ge(*x2_full.after((b, j, 2)))
                    copy(x2[:, (b * FT + j) % 2, 0, 2, :], x2u[:, 0, :]).then_inc(x2_hi.sem, 1)
                if b < NB - 1:
                    turn_hi("B", b + 1, xtb)
            for c in range(NC):
                act.wait_ge(*g_full.after((NB - 1, c)))
                copy(g_part[:, 0, c, :], x2f[:, c, :]).then_inc(g_hi.sem, 1)

            act.wait_ge(wqkv_in, 16)
            copy(wqkv[:, 0, :, :], wqkv_raw[:, :, :]).then_inc(wqkv_hi, 1)
            for b in range(NB):
                turn_hi("C", b, xtc)
                for m in range(4):
                    n = 4 * b + m
                    act.wait_ge(*qk_ps.after((b, m)))
                    if n >= 2:
                        act.wait_ge(qk_out_sem[n % 2], 16 * (n // 2))
                    copy(qk_out[:, n % 2, 0, :], ps[:, m, :]).then_inc(qk_hi.sem, 1)
                for t in range(TPB * b, TPB * (b + 1)):
                    act.wait_ge(*v_ps.after(t))
                    act.wait_ge(v_ones, 1)
                    copy(vaug[:, 0:NT * HEADS * VW].rearrange("p (t h d) -> p t h d", t=NT, d=VW)[:, t, :, 0:HD],
                         ps[:, 4 + t % 2, 0:H].rearrange("p (h d) -> p h d", d=HD)).then_inc(v_ready.sem, 1)
            for s, (g, qb, kt) in enumerate(real):
                off = max(0, kt - TPB * qb) * P
                for p in range(2):
                    act.wait_ge(*st_ready.after((s, p)))
                    if s >= 2:
                        act.wait_ge(*pv_done.after(s - 2))
                    act.activation(probs[:, (2 * s + p) % 4, :, off:BLK], ps[:, 2 * p:2 * p + 2, off:BLK], ACT.Exp,
                                   scale=float(HD) ** -0.5).then_inc(exp_done.sem, 1)
                if (g, qb, kt) == (NG - 1, NB - 2, 0):
                    act.wait_ge(wo_in, 16)
                    copy(wo[:, 0, :, :], wo_raw[:, :, :]).then_inc(wo_hi, 1)
                    act.wait_ge(wg1_in, 16)
                    copy(wg1[:, 0, :, :], wg1_raw[:, :, :]).then_inc(wg1_hi, 1)
                if tail_turn(s) is not None:
                    turn_hi("O", tail_turn(s), ot)
            turn_hi("O", NB - 1, ot)
            def weights_hi(hf, j):
                n = hj_no(hf, j)
                act.wait_ge(raw_in[n % 3], 32 * (n // 3 + 1))
                if n >= 3:
                    act.wait_ge(*down1.after(hj[n - 3]))
                copy(gu[:, n % 3, 0, :, :, :].rearrange("p a b c -> p (a b c)"), gu_raw[:, n % 3, :]) \
                    .then_inc(gu_hi_only, 1)
                copy(dn[:, n % 3, 0, :], dn_raw[:, n % 3, :]).then_inc(wd_hi.sem, 1)

            def wide_weights(hf):
                for b in range(2 * hf, 2 * hf + 2):
                    act.wait_ge(*ce_ps.after(b))
                    copy(ce_bc[:, BLK * b:BLK * (b + 1)], ps[:, b % 2, :]).then_inc(ce_sb.sem, 1)

            turn_hi("D", 0, xtd)
            weights_hi(*hj[0])
            turn_hi("D", 1, xtd)
            weights_hi(*hj[1])
            for b in range(2, NB):
                turn_hi("D", b, xtd)
            for h in range(2):
                act.wait_ge(*lg1_shift.after(h))
                act.activation(exp1[:, h, :, :], lg1[:, h, :, :], ACT.Exp).then_inc(prob_exp.sem, 1)
            for i, (hf, j, tb) in enumerate(hjt):
                act.wait_ge(*gu_ps.after((hf, j, tb)))
                if i >= 2:
                    act.wait_ge(*hmul_ready.after(hjt[i - 2]))
                act.activation(silu1[:, tb, :], ps[:, 4 + 2 * tb, :], ACT.Silu).then_inc(silu1_ready.sem, 1)
                if (j, tb) == (0, 0):
                    wide_weights(hf)
                act.wait_ge(*h_full.after((hf, j, tb)))
                n = hj_no(hf, j)
                if n >= 2:
                    act.wait_ge(*down1.after(hj[n - 2]))
                copy(hpart[:, n % 2, tb, 0, :], hfull[:, tb, :]).then_inc(h_hi.sem, 1)
                if tb == 1 and n + 2 < len(hj):
                    weights_hi(*hj[n + 2])

        @block.vector
        def _(dve):
            done = [0]

            def step(ins):
                done[0] += 1
                ins.then_inc(dve_step, 1)

            def settle():
                dve.wait_ge(dve_step, done[0])

            def low(out, full, hi):
                return dve.tensor_tensor(out, full, hi.bitcast(F32), ALU.subtract)

            def layer_norm(st, b, n_prior=None):
                settle()
                q = b % 2
                for t in range(TPB):
                    step(dve.bn_stats(ln_stats[:, q, t, :], x[:, TPB * b + t, :]))
                settle()
                for t in range(TPB):
                    step(dve.bn_aggr(ln_mv[:, q, t, :], ln_stats[:, q, t, :]))
                settle()
                dve.tensor_scalar(ln_var[:, q, :], ln_mv[:, q, :, 1], EPS, None, ALU.add).then_inc(var_ready.sem, 1)
                dve.wait_ge(*rstd_ready.after((st, b)))
                for t in range(TPB):
                    ins = dve.tensor_scalar(x[:, TPB * b + t, :], x[:, TPB * b + t, :], ln_mv[:, q, t, 0:1],
                                            ln_rstd[:, q, t:t + 1], ALU.subtract, ALU.mult)
                    if t < TPB - 1:
                        step(ins)
                    else:
                        ins.then_inc(ln_ready.sem, 1)

            for c in range(NC):
                dve.wait_ge(*energy_ready.after(c))
                dve.tensor_reduce(nmax_a[:, c:c + 1], ps[:, c, 0:H], AX_X, ALU.max, negate=True) \
                    .then_inc(nmax_ready.sem, 1)
            for c in range(NC):
                dve.wait_ge(*att_exp.after(c))
                step(dve.reciprocal(rec_a[:, c:c + 1], sum_a[:, c:c + 1]))
                settle()
                dve.tensor_scalar(attn[:, c, :], att[:, c, :], rec_a[:, c:c + 1], None, ALU.mult) \
                    .then_inc(att_norm.sem, 1)
            for j in range(NC):
                dve.wait_ge(*att_tps.after(j))
                dve.tensor_copy(att_t[:, j, :], ps[:, 2 + j, 0:H]).then_inc(att_tsb.sem, 1)
            for b in range(NB):
                for t in range(TPB * b, TPB * (b + 1)):
                    dve.wait_ge(*mix_ready.after(t))
                    dve.tensor_tensor(x[:, t, :], ps[:, 4 + t % 4, 0:H], x[:, t, :], ALU.add).then_inc(mix_read.sem, 1)
                dve.wait_ge(*mix_read.after(TPB * (b + 1) - 1))
                layer_norm("A", b)
                if b == 0:
                    for n, raw, part in (("w13", w13_raw, w13), ("a13", a13_raw, a13), ("b13", b13_raw, b13), ("w2a2", w2a2_raw, w2a2),
                                         ("b2", b2_raw, b2)):
                        dve.wait_ge(*w0_hi.after(n))
                        low(part[:, 1], raw.ap(), part[:, 0]).then_inc(w0_ready.sem, 1)

            def turn_lo(st, b, dst):
                for c in range(NC):
                    dve.wait_ge(*turned_hi.after((st, b, c)))
                    if st == "B":
                        out, hi = dst[:, 1, c, :], dst[:, 0, c, :]
                    else:
                        out, hi = (dst[:, i, c, BLK * b:BLK * (b + 1)] for i in (1, 0))
                    low(out, ps[:, turn_bank(st, b, c), :], hi).then_inc(turned_lo.sem, 1)

            def masks(b):
                dve.wait_ge(*logits0.after(b))
                step(dve.tensor_copy(lg0[:, :, :].rearrange("p t e -> p (t e)"), ps[:, 0, 0:TPB * E0]))
                settle()
                for t in range(TPB):
                    step(dve.max(top0[:, t, :], lg0[:, t, :]))
                settle()
                for t in range(TPB):
                    step(dve.max_index(idx0[:, t, :], top0[:, t, :], lg0[:, t, :]))
                dve.tensor_tensor(gap0[:, :], top0[:, :, 1], top0[:, :, 0], ALU.subtract).then_inc(gap_ready.sem, 1)
                settle()
                step(dve.tensor_copy(idx0f[:, :, :], idx0[:, :, 0:2]))
                settle()
                for k in range(2):
                    step(dve.tensor_tensor(mask0[:, k, :, :], iota[:, None, 0:E0].broadcast_to([P, TPB, E0]),
                                           idx0f[:, :, k:k + 1].broadcast_to([P, TPB, E0]), ALU.is_equal))
                settle()
                step(dve.tensor_tensor(mdiff[:, :, :], mask0[:, 1, :, :], mask0[:, 0, :, :], ALU.subtract))
                settle()
                for k, src in ((0, mask0[:, 0, :, :]), (1, mdiff[:, :, :])):
                    if b:
                        dve.wait_ge(*wide_ps.after((b - 1, f"mw{k}")))
                    dve.tensor_copy(mx[:, k, :, :].rearrange("p t (r e) -> p t r e", e=E0),
                                    src[:, :, None, :].broadcast_to([P, TPB, P // E0, E0])).then_inc(wide.sem, 1)

            def weights(b):
                dve.wait_ge(*gap_exp.after(b))
                step(dve.tensor_scalar(den0[:, :], exp0[:, :], 1.0, None, ALU.add))
                settle()
                step(dve.reciprocal(rw0[:, 0, :], den0[:, :]))
                settle()
                step(dve.tensor_tensor(rw0[:, 1, :], exp0[:, :], rw0[:, 0, :], ALU.mult))
                settle()
                for k in range(2):
                    step(dve.tensor_tensor(mw0[:, k, :, :], mask0[:, k, :, :],
                                           rw0[:, k, :, None].broadcast_to([P, TPB, E0]), ALU.mult))
                settle()
                for k in range(2):
                    if b:
                        dve.wait_ge(*wide_ps.after((b - 1, f"rw{k}")))
                    dve.tensor_copy(mx[:, 2 + k, :, :], rw0[:, k, :, None].broadcast_to([P, TPB, P])) \
                        .then_inc(wide.sem, 1)
                for k in range(2):
                    dve.wait_ge(*wide_ps.after((b, f"mask{k}")))
                    dve.tensor_copy(mx[:, k, :, :].rearrange("p t (r e) -> p t r e", e=E0),
                                    mw0[:, k, :, None, :].broadcast_to([P, TPB, P // E0, E0])).then_inc(wide.sem, 1)

            def lora_sum(b):
                dve.wait_ge(*down0.after((b, FT - 1)))
                for c in range(NC):
                    for k in range(2):
                        dve.wait_ge(*wide_sb.after((b, f"mw{k}")))
                        step(dve.tensor_tensor(x2u[:, k, :], ps[:, 2 + 2 * k + c, :], bc[:, k, :], ALU.mult))
                    settle()
                    dve.wait_ge(*x2_hi.after((b, FT - 1, c)))
                    dve.tensor_tensor(x2f[:, c, :], x2u[:, 0, :], x2u[:, 1, :], ALU.add).then_inc(g_full.sem, 1)
                    dve.wait_ge(*g_full.after((b, c)))
                for c in range(NC):
                    dve.wait_ge(*g_hi.after((b, c)))
                    low(g_part[:, 1, c, :], x2f[:, c, :], g_part[:, 0, c, :]).then_inc(g_lo.sem, 1)

            def residual(b):
                dve.wait_ge(*out0.after(b))
                for t in range(TPB):
                    xt = x[:, TPB * b + t, :]
                    dve.tensor_tensor(xt, ps[:, 6 + t // 2, H * (t % 2):H * (t % 2 + 1)], xt, ALU.add) \
                        .then_inc(out0_read.sem, 1)

            turn_lo("B", 0, xtb)
            for b in range(NB):
                masks(b)
                if b:
                    lora_sum(b - 1)
                weights(b)
                if b:
                    residual(b - 1)
                todo = [(k, w, c) for k in range(2) for w in range(2) for c in range(NC)]

                def ma_low(i):
                    k, w, c = todo[i]
                    dve.wait_ge(*ma_hi.after((b, k, w, c)))
                    low(ma[:, 1, w, k, c, :], x2f[:, i % 2, :], ma[:, 0, w, k, c, :]).then_inc(ma_lo.sem, 1)

                for i, (k, w, c) in enumerate(todo):
                    dve.wait_ge(*wide_sb.after((b, f"mask{k}")))
                    dve.wait_ge(*a_ps.after((b, w, c)))
                    if i >= 2:
                        ma_low(i - 2)
                        dve.wait_ge(*ma_lo.after((b,) + todo[i - 2]))
                    elif b:
                        dve.wait_ge(*g_lo.after((b - 1, NC - 1)))
                    dve.tensor_tensor(x2f[:, i % 2, :], ps[:, 2 + 2 * w + c, :], bc[:, k, :], ALU.mult) \
                        .then_inc(ma_full.sem, 1)
                ma_low(6)
                ma_low(7)
                for j in range(FT):
                    slot = (b * FT + j) % 2
                    for k in range(2):
                        dve.wait_ge(*silu_ready.after((b, j, k)))
                        if j:
                            dve.wait_ge(*x2_lo.after((b, j - 1, k)))
                        else:
                            dve.wait_ge(*ma_lo.after((b, 1, 1, NC - 1)))
                        dve.tensor_tensor(x2f[:, k, :], ps[:, 1, :], silu0[:, k, :], ALU.mult) \
                            .then_inc(x2_full.sem, 1)
                        if k == 0:
                            dve.wait_ge(*x2_hi.after((b, j, 0)))
                            low(x2[:, slot, 1, 0, :], x2f[:, 0, :], x2[:, slot, 0, 0, :]).then_inc(x2_lo.sem, 1)
                    dve.wait_ge(*x2_full.after((b, j, 1)))
                    if j:
                        dve.wait_ge(*x2_lo.after((b, j - 1, 2)))
                    elif b:
                        dve.wait_ge(*g_full.after((b - 1, NC - 1)))
                    for k in range(2):
                        dve.wait_ge(*wide_sb.after((b, f"rw{k}")))
                        step(dve.tensor_tensor(x2u[:, k, :], x2f[:, k, :], bc[:, 2 + k, :], ALU.mult))
                    dve.wait_ge(*x2_hi.after((b, j, 1)))
                    low(x2[:, slot, 1, 1, :], x2f[:, 1, :], x2[:, slot, 0, 1, :]).then_inc(x2_lo.sem, 1)
                    settle()
                    dve.tensor_tensor(x2u[:, 0, :], x2u[:, 0, :], x2u[:, 1, :], ALU.add).then_inc(x2_full.sem, 1)
                    dve.wait_ge(*x2_hi.after((b, j, 2)))
                    low(x2[:, slot, 1, 2, :], x2u[:, 0, :], x2[:, slot, 0, 2, :]).then_inc(x2_lo.sem, 1)
                    if j == 1 and b:
                        dve.wait_ge(*out0_read.after((b - 1, TPB - 1)))
                        layer_norm("B", b - 1)
                dve.wait_ge(*x2_lo.after((b, FT - 1, 2)))
                if b < NB - 1:
                    turn_lo("B", b + 1, xtb)
            lora_sum(NB - 1)
            residual(NB - 1)
            dve.wait_ge(*out0_read.after((NB - 1, TPB - 1)))
            layer_norm("B", NB - 1)

            dve.wait_ge(*ln_ready.after(("B", NB - 1)))
            dve.memset(vaug[:, :], 1.0).then_inc(v_ones, 1)
            dve.wait_ge(wqkv_hi, 1)
            low(wqkv[:, 1, :, :], wqkv_raw[:, :, :], wqkv[:, 0, :, :]).then_inc(wqkv_ready, 1)
            for b in range(NB):
                turn_lo("C", b, xtc)
                for m in range(4):
                    n = 4 * b + m
                    dve.wait_ge(*qk_hi.after((b, m)))
                    low(qk_out[:, n % 2, 1, :], ps[:, m, :], qk_out[:, n % 2, 0, :]).then_inc(qk_lo.sem, 1)
            def turned_max(g, qb):
                n = round_no[g, qb]
                dve.wait_ge(*max_turned.after((g, qb)))
                if n >= 2:
                    g2, qb2 = rounds[n - 2]
                    dve.wait_ge(max_in[qb2], 128 * (g2 + 1))
                dve.tensor_copy(mrow[:, n % 2, 0, :], ps[0:GH * TPB, 7, 0:P]).then_inc(max_hi.sem, 1)
                dve.wait_ge(*max_hi.after((g, qb)))
                low(mrow[:, n % 2, 1, :], ps[0:GH * TPB, 7, 0:P], mrow[:, n % 2, 0, :]).then_inc(max_lo.sem, 1)

            def head_out(g, qb):
                dve.wait_ge(*u_turned.after((g, qb)))
                view = ps[:, 7, :].rearrange("p (t h d) -> p t h d", t=TPB, h=GH)
                step(dve.reciprocal(rec_c[:, :, :], view[:, :, :, HD]))
                settle()
                dve.tensor_tensor(o_tm[:, TPB * qb:TPB * (qb + 1), GH * HD * g:GH * HD * (g + 1)]
                                  .rearrange("p t (h d) -> p t h d", d=HD), view[:, :, :, 0:HD],
                                  rec_c[:, :, :, None].broadcast_to([P, TPB, GH, HD]), ALU.mult) \
                    .then_inc(o_ready.sem, 1)

            def attention_residual(t):
                dve.wait_ge(*proj_ps.after(t))
                dve.tensor_tensor(x[:, t, :], ps[:, proj_bank(t), 0:H], x[:, t, :], ALU.add).then_inc(proj_read.sem, 1)
                if t % TPB == TPB - 1:
                    dve.wait_ge(*proj_read.after(t))
                    layer_norm("C", t // TPB)

            for s in range(n_steps):
                for u in units_at[s] if s < len(units_at) else []:
                    g, h, qt, kb = u
                    qb = qt // TPB
                    n = round_no[g, qb]
                    width = BLK if kb < qb else P * (qt % TPB + 1)
                    dve.wait_ge(*scored.after(u))
                    dve.tensor_reduce(mpart[:, n % 2, TPB * h + qt % TPB, kb:kb + 1],
                                      ps[:, 4 + unit_no[u] % 2, 0:width], AX_X, ALU.max).then_inc(reduced.sem, 1)
                    if closes(u):
                        dve.wait_ge(*reduced.after(u))
                        if n >= 2:
                            dve.wait_ge(*max_turned.after(rounds[n - 2]))
                        dve.tensor_reduce(nmx[:, n % 2, :], mpart[:, n % 2, :, 0:qb + 1], AX_X, ALU.max, negate=True) \
                            .then_inc(round_max.sem, 1)
                if s in max_at:
                    turned_max(*max_at[s])
                if s in out_at:
                    head_out(*out_at[s])
                r = s - n_pre - 1
                if 0 <= r < len(real):
                    g, qb, kt = real[r]
                    if kt == TPB * (qb + 1) - 1:
                        dve.wait_ge(*pv_done.after(r))
                        n = round_no[g, qb]
                        if n:
                            dve.wait_ge(*u_turned.after(rounds[n - 1]))
                        dve.tensor_copy(usum[:, :], ps[:, 6, :]).then_inc(u_copied.sem, 1)
                r = s - n_pre
                if 0 <= r < len(real):
                    if real[r] == (NG - 1, NB - 2, 0):
                        dve.wait_ge(wo_hi, 1)
                        low(wo[:, 1, :, :], wo_raw[:, :, :], wo[:, 0, :, :]).then_inc(wo_ready, 1)
                        dve.wait_ge(wg1_hi, 1)
                        low(wg1[:, 1, :, :], wg1_raw[:, :, :], wg1[:, 0, :, :]).then_inc(wg1_ready, 1)
                    if tail_turn(r) is not None:
                        turn_lo("O", tail_turn(r), ot)
                    if tail_tile(r) is not None:
                        attention_residual(tail_tile(r))

            turn_lo("O", NB - 1, ot)
            turn_lo("D", 0, xtd)
            for t in range(NT - TPB, NT):
                attention_residual(t)
            for b in range(1, NB):
                turn_lo("D", b, xtd)

            wide1, eight = [P, PAIR, E1], [P, PAIR, TOP]

            def shifted_logits(h):
                for b in range(2 * h, 2 * h + 2):
                    dve.wait_ge(*logits1.after(b))
                lgv = ps[:, 7 - h, 0:PAIR * E1].rearrange("p (t e) -> p t e", e=E1)
                step(dve.tensor_reduce(r_max[:, :], lgv, AX_X, ALU.max))
                settle()
                dve.tensor_tensor(lg1[:, h, :, :], lgv, r_max[:, :, None].broadcast_to(wide1), ALU.subtract) \
                    .then_inc(lg1_shift.sem, 1)
                dve.wait_ge(*lg1_shift.after(h))

            def best_eight(h):
                settle()
                dve.wait_ge(*prob_exp.after(h))
                step(dve.tensor_reduce(r_sum[:, :], exp1[:, h, :, :], AX_X, ALU.add))
                settle()
                step(dve.reciprocal(r_rec[:, :], r_sum[:, :]))
                settle()
                step(dve.tensor_tensor(prob1[:, :, 0:E1], exp1[:, h, :, :], r_rec[:, :, None].broadcast_to(wide1),
                                       ALU.mult))
                settle()
                for t in range(PAIR):
                    step(dve.max(r_top[:, t, :], prob1[:, t, 0:E1]))
                settle()

            def running_share():
                step(dve.tensor_reduce(r_sum[:, :], r_top[:, :, :], AX_X, ALU.add))
                settle()
                step(dve.tensor_scalar(r_max[:, :], r_sum[:, :], 1e-12, None, ALU.max))
                settle()
                step(dve.reciprocal(r_rec[:, :], r_max[:, :]))
                settle()
                step(dve.tensor_tensor(r_cum[:, :, :], r_top[:, :, :], r_rec[:, :, None].broadcast_to(eight),
                                       ALU.mult))
                settle()
                for r in range(1, TOP):
                    step(dve.tensor_tensor(r_cum[:, :, r], r_cum[:, :, r - 1], r_cum[:, :, r], ALU.add))
                    settle()

            def kept():
                step(dve.tensor_scalar(r_on[:, :, 1:TOP], r_cum[:, :, 0:TOP - 1], KEEP, None, ALU.is_lt))
                step(dve.memset(r_on[:, :, 0:1], 1.0))
                settle()
                step(dve.tensor_tensor(r_rw[:, :, :], r_top[:, :, :], r_on[:, :, :], ALU.mult))
                settle()
                step(dve.tensor_reduce(r_sum[:, :], r_rw[:, :, :], AX_X, ALU.add))
                step(dve.scalar_tensor_tensor(out=r_val[:, :, :], in0=r_on[:, :, :], scalar=-1.0, in1=r_rw[:, :, :],
                                              op0=ALU.add, op1=ALU.add))
                settle()
                step(dve.tensor_scalar(r_max[:, :], r_sum[:, :], 1e-12, None, ALU.max))
                for t in range(PAIR):
                    step(dve.match_replace(rest1[:, t, :], r_val[:, t, :], prob1[:, t, :], 0.0))
                settle()

            def combine(h):
                step(dve.reciprocal(r_rec[:, :], r_max[:, :]))
                step(dve.tensor_tensor(comb1[:, :, :], prob1[:, :, 0:E1], rest1[:, :, 0:E1], ALU.subtract))
                settle()
                step(dve.tensor_tensor(comb1[:, :, :], comb1[:, :, :], r_rec[:, :, None].broadcast_to(wide1),
                                       ALU.mult))
                settle()
                for i in range(2):
                    if h:
                        dve.wait_ge(*ce_ps.after(i))
                    dve.tensor_copy(cex[:, i, :, :].rearrange("p t (r e) -> p t r e", e=E1),
                                    comb1[:, TPB * i:TPB * (i + 1), None, :].broadcast_to([P, TPB, RPT, E1])) \
                        .then_inc(ce_wide.sem, 1)

            step(dve.memset(prob1[:, :, E1:E1 + 8], -1.0))
            shifted_logits(0)
            shifted_logits(1)
            best_eight(0)
            running_share()
            kept()
            combine(0)

            for hf in range(2):
                for j in range(JT):
                    n = hj_no(hf, j)
                    for tb in range(2):
                        key = (hf, j, tb)
                        dve.wait_ge(*silu1_ready.after(key))
                        dve.tensor_tensor(hmul[:, tb, :], ps[:, 5 + 2 * tb, :], silu1[:, tb, :], ALU.mult) \
                            .then_inc(hmul_ready.sem, 1)
                        dve.wait_ge(*hmul_ready.after(key))
                        col = BLK * (2 * hf + tb)
                        if j == 0:
                            dve.wait_ge(*ce_sb.after(2 * hf + tb))
                        dve.tensor_tensor(hfull[:, tb, :], hmul[:, tb, :], ce_bc[:, col:col + BLK], ALU.mult) \
                            .then_inc(h_full.sem, 1)
                        dve.wait_ge(*h_hi.after(key))
                        low(hpart[:, n % 2, tb, 1, :], hfull[:, tb, :], hpart[:, n % 2, tb, 0, :]) \
                            .then_inc(h_lo.sem, 1)
                    if (hf, j) == (0, 1):
                        best_eight(1)
                    if (hf, j) == (0, 2):
                        running_share()
                    if (hf, j) == (0, 3):
                        kept()
                    if (hf, j) == (0, 4):
                        combine(1)
                    if (hf, j) == (1, 1):
                        for b in range(2):
                            layer_norm("D", b)
                dve.wait_ge(*down1.after((hf, JT - 1)))
                for b in range(2 * hf, 2 * hf + 2):
                    for t in range(TPB * b, TPB * (b + 1)):
                        a = t - PAIR * hf
                        dve.tensor_tensor(x[:, t, :], ps[:, a // 2, H * (a % 2):H * (a % 2 + 1)], x[:, t, :], ALU.add) \
                            .then_inc(acc_read.sem, 1)
                    dve.wait_ge(*acc_read.after((hf, TPB * (b + 1) - 1 - PAIR * hf)))
                    if hf:
                        layer_norm("D", b)

        @block.tensor
        def _(pe):
            def product(out, pairs, first=True, last=True, **more):
                n, todo = 0, len(pairs) * len(PARTS)
                for lhs, rhs in pairs:
                    for i, k in PARTS:
                        n += 1
                        mm = pe.matmul(out, lhs(i), rhs(k), start=first and n == 1, stop=last and n == todo, **more)
                return mm

            def turn(st, b, src):
                for c in range(NC):
                    for t in range(TPB):
                        mm = pe.transpose(ps[:, turn_bank(st, b, c), P * t:P * (t + 1)], src[:, TPB * b + t, P * c:P * (c + 1)],
                                          ident[:, :])
                    mm.then_inc(turned.sem, 1)

            for t in range(NT):
                if t % TPB == 0:
                    pe.wait_ge(x_in[t // TPB], 16)
                for c in range(NC):
                    mm = pe.matmul(ps[:, c, 0:H], x[:, t, P * c:P * (c + 1)], x[:, t, :], start=t == 0, stop=t == NT - 1)
                    if t == NT - 1:
                        mm.then_inc(energy_ready.sem, 1)
            pe.wait_ge(consts_in, 80)
            for j in range(NC):
                for c in range(NC):
                    if j == 0:
                        pe.wait_ge(*att_norm.after(c))
                    mm = pe.transpose(ps[:, 2 + j, P * c:P * (c + 1)], attn[:, c, P * j:P * (j + 1)], ident[:, :])
                mm.then_inc(att_tps.sem, 1)
            pe.wait_ge(xfm_in, 16)
            pe.wait_ge(*att_tsb.after(NC - 1))
            for t in range(NT):
                if t >= 4:
                    pe.wait_ge(*mix_read.after(t - 4))
                for j in range(NC):
                    mm = pe.matmul(ps[:, 4 + t % 4, 0:H], xt_in[:, j, P * t:P * (t + 1)], att_t[:, j, :],
                                   start=j == 0, stop=j == NC - 1)
                mm.then_inc(mix_ready.sem, 1)

            pe.wait_ge(lora_in, 16)

            def logits(b):
                for c in range(NC):
                    pe.wait_ge(*turned_lo.after(("B", b, c)))
                for t in range(TPB):
                    n = 0
                    for c in range(NC):
                        for i in (1, 0):
                            mm = pe.matmul(ps[:, 0, E0 * t:E0 * (t + 1)],
                                           xtb[:, i, c, P * t:P * (t + 1)].bitcast(F32), wg0[:, c, :],
                                           start=n == 0, stop=n == 3)
                            n += 1
                mm.then_inc(logits0.sem, 1)

            def widen(b, names):
                for i in names:
                    pe.wait_ge(*wide.after((b, i)))
                    slot, bank = wide_place[i]
                    for t in range(TPB):
                        mm = pe.transpose(ps[:, bank, P * t:P * (t + 1)], mx[:, slot, t, :], ident[:, :])
                    mm.then_inc(wide_ps.sem, 1)

            def hidden(j):
                for w in range(2):
                    product(ps[:, w, :],
                            [(lambda i, c=c: w13[:, i, c, w, P * j:P * (j + 1)], lambda k, c=c: xtb[:, k, c, :])
                             for c in range(NC)], True, False, skip_group_check=True)

            def lora(b, j, k):
                for w in range(2):
                    if j == 0:
                        pe.wait_ge(*ma_lo.after((b, k, w, NC - 1)))
                    mm = product(ps[:, w, :],
                                 [(lambda i, c=c: b13[:, i, c, w, P * j:P * (j + 1)],
                                   lambda q, c=c: ma[:, q, w, k, c, :]) for c in range(NC)],
                                 False, True, skip_group_check=True)
                mm.then_inc(mlp_ps.sem, 1)

            def down_lora(b, j, k, c):
                slot = (b * FT + j) % 2
                pe.wait_ge(*x2_lo.after((b, j, k)))
                product(ps[:, 2 + 2 * k + c, :],
                        [(lambda i: w2a2[:, i, j, H + P * c:H + P * (c + 1)], lambda q: x2[:, slot, q, k, :])],
                        j == 0, j == FT - 1, skip_group_check=True)

            def down_sum(b, j):
                slot = (b * FT + j) % 2
                pe.wait_ge(*x2_lo.after((b, j, 2)))
                for t in range(TPB):
                    mm = product(ps[:, 6 + t // 2, H * (t % 2):H * (t % 2 + 1)],
                                 [(lambda i: x2[:, slot, i, 2, P * t:P * (t + 1)], lambda q: w2a2[:, q, j, 0:H])],
                                 j == 0 and t % 2 == 0, False, skip_group_check=True)
                mm.then_inc(down0.sem, 1)

            def lora_out(b):
                for c in range(NC):
                    pe.wait_ge(*g_lo.after((b, c)))
                for t in range(TPB):
                    mm = product(ps[:, 6 + t // 2, H * (t % 2):H * (t % 2 + 1)],
                                 [(lambda i, c=c: g_part[:, i, c, P * t:P * (t + 1)], lambda q, c=c: b2[:, q, c, :])
                                  for c in range(NC)], False, True, skip_group_check=True)
                mm.then_inc(out0.sem, 1)

            pe.wait_ge(*ln_ready.after(("A", 0)))
            turn("B", 0, x)
            logits(0)
            for b in range(NB):
                widen(b, ("mask0", "mask1"))
                pe.wait_ge(*wide_sb.after((b, "mask1")))
                if b == 0:
                    pe.wait_ge(*w0_ready.after("w13"))
                hidden(0)
                if b:
                    pe.wait_ge(*g_full.after((b - 1, NC - 1)))
                    lora_out(b - 1)
                else:
                    pe.wait_ge(*mix_read.after(NT - 1))
                if b == 0:
                    pe.wait_ge(*w0_ready.after("a13"))
                for w in range(2):
                    for c in range(NC):
                        product(ps[:, 2 + 2 * w + c, :],
                                [(lambda q, i=i: a13[:, q, i, w, P * c:P * (c + 1)], lambda q, i=i: xtb[:, q, i, :])
                                 for i in range(NC)]).then_inc(a_ps.sem, 1)
                if b == 0:
                    pe.wait_ge(*w0_ready.after("b2"))
                for j in range(FT):
                    if j:
                        pe.wait_ge(*x2_full.after((b, j - 1, 1)))
                        hidden(j)
                    lora(b, j, 0)
                    if j == 0:
                        pe.wait_ge(*ma_full.after((b, 1, 1, NC - 1)))
                        widen(b, ("rw0", "rw1", "mw0", "mw1"))
                        if b:
                            pe.wait_ge(*out0_read.after((b - 1, TPB - 1)))
                    else:
                        if j == 1:
                            pe.wait_ge(*wide_sb.after((b, "mw1")))
                        for k, c in ((0, 0), (0, 1), (1, 0)):
                            down_lora(b, j - 1, k, c)
                    pe.wait_ge(*x2_full.after((b, j, 0)))
                    lora(b, j, 1)
                    if j:
                        down_lora(b, j - 1, 1, 1)
                        down_sum(b, j - 1)
                pe.wait_ge(*x2_full.after((b, FT - 1, 1)))
                if b < NB - 1:
                    pe.wait_ge(*ln_ready.after(("A", b + 1)))
                    turn("B", b + 1, x)
                for k in range(2):
                    for c in range(NC):
                        down_lora(b, FT - 1, k, c)
                down_sum(b, FT - 1)
                if b < NB - 1:
                    logits(b + 1)
            lora_out(NB - 1)

            pe.wait_ge(wqkv_ready, 1)
            for b in range(NB):
                pe.wait_ge(*ln_ready.after(("B", b)))
                if b:
                    for c in range(NC):
                        pe.wait_ge(*turned_lo.after(("C", b - 1, c)))
                turn("C", b, x)
                pe.wait_ge(*turned_lo.after(("C", b, NC - 1)))
                for m in range(4):
                    if b:
                        pe.wait_ge(*qk_lo.after((b - 1, m)))
                    product(ps[:, m, :],
                            [(lambda i, c=c: wqkv[:, i, c, P * m:P * (m + 1)],
                              lambda k, c=c: xtc[:, k, c, BLK * b:BLK * (b + 1)]) for c in range(NC)]) \
                        .then_inc(qk_ps.sem, 1)
                for t in range(TPB * b, TPB * (b + 1)):
                    if t >= 2:
                        pe.wait_ge(*v_ready.after(t - 2))
                    product(ps[:, 4 + t % 2, 0:H],
                            [(lambda i, c=c: xtc[:, i, c, P * t:P * (t + 1)], lambda k, c=c: wqkv[:, k, c, 2 * H:3 * H])
                             for c in range(NC)]).then_inc(v_ps.sem, 1)

            pe.wait_ge(*v_ready.after(NT - 1))
            pe.wait_ge(*qk_lo.after((NB - 1, 3)))
            pe.wait_ge(ones_in[0], 16 * (T // 256))

            def score_units(s, first, last):
                for u in units_at[s][first:last] if s < len(units_at) else []:
                    g, h, qt, kb = u
                    if (h, qt, kb) == (0, 0, 0) and g:
                        pe.wait_ge(ones_in[g % 2], 16 * (T // 256))
                        pe.wait_ge(stack_in[g % 2], 16 * (8 + (T // 256) * (g >= 2)) + 128 * (g == 3))
                    if g == 0 and (h, qt % TPB, kb) == (0, 0, 0):
                        pe.wait_ge(first_in[qt // TPB], 128)
                    last = kb == qt // TPB
                    width = P * (qt % TPB + 1) if last else BLK
                    n = unit_no[u]
                    if n >= 2:
                        pe.wait_ge(*reduced.after(units[n - 2]))
                    mm = pe.matmul(ps[:, 4 + n % 2, 0:width], stack[:, g % 2, 0, h, P * qt:P * (qt + 1)],
                                   stack[:, g % 2, 1, h, BLK * kb:BLK * kb + width], start=True, stop=not last)
                    if last:
                        mm = pe.matmul(ps[:, 4 + n % 2, width - P:width], identb[:, :], trimax[:, :],
                                       start=False, stop=True)
                    mm.then_inc(scored.sem, 1)

            def values(r):
                g, qb, kt = real[r]
                off = max(0, kt - TPB * qb) * P
                n = round_no[g, qb]
                pe.wait_ge(*exp_done.after((r, 1)))
                if kt == 0 and n:
                    pe.wait_ge(*u_copied.after(rounds[n - 1]))
                for h in range(GH):
                    v0 = (kt * HEADS + GH * g + h) * VW
                    mm = pe.matmul(ps[32 * h:32 * (h + 1), 6, off:BLK], vaug[:, v0:v0 + 32],
                                   probs[:, (2 * r + h // 2) % 4, h % 2, off:BLK],
                                   start=kt == 0, stop=kt == TPB * (qb + 1) - 1, skip_group_check=True)
                mm.then_inc(pv_done.sem, 1)

            def turn_output(b):
                pe.wait_ge(*o_ready.after((NG - 1, b)))
                if b:
                    pe.wait_ge(*proj_read.after(TPB * b - 1))
                turn("O", b, o_tm)

            def project_output(t):
                if t == 0:
                    pe.wait_ge(wo_ready, 1)
                if t % TPB == 0:
                    pe.wait_ge(*turned_lo.after(("O", t // TPB, NC - 1)))
                if t >= 2:
                    pe.wait_ge(*proj_read.after(t - 2))
                product(ps[:, proj_bank(t), 0:H],
                        [(lambda i, c=c: ot[:, i, c, P * t:P * (t + 1)], lambda k, c=c: wo[:, k, c, :])
                         for c in range(NC)]).then_inc(proj_ps.sem, 1)

            for s in range(n_steps):
                r = s - n_pre
                if 0 <= r < len(real):
                    g, qb, kt = real[r]
                    diag = kt >= TPB * qb
                    off = max(0, kt - TPB * qb) * P
                    if kt == 0:
                        pe.wait_ge(max_in[qb], 128 * (g + 1))
                for p in range(2):
                    score_units(s, p, p + 1)
                    if 0 <= r < len(real):
                        if r:
                            pe.wait_ge(*exp_done.after((r - 1, p)))
                        for h in (2 * p, 2 * p + 1):
                            mm = pe.matmul(ps[:, h, off:BLK], stack[:, g % 2, 1, h, P * kt:P * (kt + 1)],
                                           stack[:, g % 2, 0, h, BLK * qb + off:BLK * (qb + 1)],
                                           start=True, stop=not diag)
                            if diag:
                                mm = pe.matmul(ps[:, h, off:off + P], identb[:, :], triexp[:, :],
                                               start=False, stop=True)
                        mm.then_inc(st_ready.sem, 1)
                score_units(s, 2, 3)
                if 0 <= r - 1 < len(real):
                    values(r - 1)
                score_units(s, 3, None)
                if s in max_at:
                    n = round_no[max_at[s]]
                    pe.wait_ge(*round_max.after(max_at[s]))
                    misc_free(pe, ("max", max_at[s]))
                    pe.transpose(ps[0:GH * TPB, 7, 0:P], nmx[:, n % 2, :], ident[:, :]).then_inc(max_turned.sem, 1)
                if s in out_at:
                    pe.wait_ge(*u_copied.after(out_at[s]))
                    misc_free(pe, ("out", out_at[s]))
                    for t in range(TPB):
                        mm = pe.transpose(ps[:, 7, P * t:P * (t + 1)], usum[:, P * t:P * (t + 1)], ident[:, :])
                    mm.then_inc(u_turned.sem, 1)

                if 0 <= r < len(real):
                    if tail_turn(r) is not None:
                        if r == last_round:
                            pe.wait_ge(*reduced.after(units[-1]))
                        turn_output(tail_turn(r))
                    if tail_tile(r) is not None:
                        project_output(tail_tile(r))

            turn_output(NB - 1)

            def turn_x(b):
                pe.wait_ge(*ln_ready.after(("C", b)))
                if b == 1:
                    pe.wait_ge(*turned_lo.after(("O", NB - 1, NC - 1)))
                if b >= 2:
                    pe.wait_ge(*turned_lo.after(("D", b - 2, NC - 1)))
                turn("D", b, x)

            def logits1_of(b):
                pe.wait_ge(*turned_lo.after(("D", b, NC - 1)))
                for t in range(TPB * b, TPB * (b + 1)):
                    at_ = E1 * (t % PAIR)
                    mm = product(ps[:, 7 - b // 2, at_:at_ + E1],
                                 [(lambda i, c=c: xtd[:, i, c, P * t:P * (t + 1)], lambda k, c=c: wg1[:, k, c, :])
                                  for c in range(NC)])
                mm.then_inc(logits1.sem, 1)

            pe.wait_ge(*exp_done.after((len(real) - 1, 1)))
            turn_x(0)
            for t in range(NT - TPB, NT):
                project_output(t)
            pe.wait_ge(wg1_ready, 1)
            logits1_of(0)
            turn_x(1)
            turn_x(2)
            logits1_of(1)
            turn_x(3)
            logits1_of(2)
            logits1_of(3)

            def widen_weights(hf):
                for b in range(2 * hf, 2 * hf + 2):
                    pe.wait_ge(*ce_wide.after(b))
                    for t in range(TPB):
                        mm = pe.transpose(ps[:, b % 2, P * t:P * (t + 1)], cex[:, b % 2, t, :], ident[:, :])
                    mm.then_inc(ce_ps.sem, 1)

            def down(hf, j):
                n = hj_no(hf, j)
                for tb in range(2):
                    pe.wait_ge(*h_lo.after((hf, j, tb)))
                if j == 0:
                    pe.wait_ge(*ce_sb.after(2 * hf + 1))
                for a in range(PAIR):
                    tb, t = a // 4, a % 4
                    mm = product(ps[:, a // 2, H * (a % 2):H * (a % 2 + 1)],
                                 [(lambda i: hpart[:, n % 2, tb, i, P * t:P * (t + 1)], lambda k: dn[:, n % 3, k, :])],
                                 j == 0 and a % 2 == 0, j == JT - 1, skip_group_check=True)
                mm.then_inc(down1.sem, 1)

            pe.wait_ge(*turned_lo.after(("D", NB - 1, NC - 1)))
            pe.wait_ge(*lg1_shift.after(1))
            for hf in range(2):
                for j in range(JT):
                    n = hj_no(hf, j)
                    pe.wait_ge(*wd_lo.after((hf, j)))
                    for tb in range(2):
                        if n:
                            pe.wait_ge(*hmul_ready.after(hjt[2 * n + tb - 2]))
                        col = BLK * (2 * hf + tb)
                        for w in range(2):
                            mm = product(ps[:, 4 + 2 * tb + w, :],
                                         [(lambda i, c=c: gu[:, n % 3, i, c, w, :],
                                           lambda k, c=c: xtd[:, k, c, col:col + BLK]) for c in range(NC)])
                        mm.then_inc(gu_ps.sem, 1)
                    if j:
                        down(hf, j - 1)
                    else:
                        if hf:
                            pe.wait_ge(*acc_read.after((0, PAIR - 1)))
                        widen_weights(hf)
                down(hf, JT - 1)


def kernel(**inputs):
    from concourse.bass_utils import run_bass_kernel_spmd
    import ml_dtypes

    a = {k: np.asarray(v) for k, v in inputs.items()}

    def lay(v):
        return np.ascontiguousarray(v)

    def rows(v, chunks):
        return v.reshape((chunks, P) + v.shape[1:]).swapaxes(0, 1)

    xs = a["L0_attn_x"][0]
    A = [a["L0_ffn_A1"], a["L0_ffn_A3"]]
    B = [a["L0_ffn_B1"], a["L0_ffn_B3"]]
    gup = a["L1_ffn_gate_up_proj"].reshape(E1, 2, JT, RPT, H)
    k = np.arange(P)
    arrays = {
        "x_tm": rows(xs, NT),
        "x_fm": rows(xs.T, NC),
        "w13": rows(np.stack([a["L0_ffn_W1"].T, a["L0_ffn_W3"].T], 1), NC),
        "a13": rows(np.stack([m.transpose(2, 1, 0).reshape(H, E0 * R0) for m in A], 1), NC),
        "b13": rows(np.stack([m.transpose(2, 0, 1).reshape(E0 * R0, F) for m in B], 1), NC),
        "w2a2": rows(np.concatenate([a["L0_ffn_W2"].T, a["L0_ffn_A2"].transpose(2, 1, 0).reshape(F, E0 * R0)], 1), FT),
        "b2": rows(a["L0_ffn_B2"].transpose(2, 0, 1).reshape(E0 * R0, H), NC),
        "wg0": rows(a["L0_ffn_Wg"].T, NC),
        "wqkv": rows(a["L1_attn_w_qkv"].T, NC),
        "wo": rows(a["L1_attn_w_o"].T, NC),
        "wg1": rows(a["L1_ffn_gate_weight"].T, NC),
        "wgu": gup.transpose(4, 2, 1, 3, 0).reshape(NC, P, JT, 2, P).transpose(1, 2, 0, 3, 4).reshape(P, JT, NC * 2 * P),
        "wdn": a["L1_ffn_down_proj"].reshape(E1, H, JT, RPT).transpose(3, 0, 2, 1).reshape(P, JT, H),
        "ident": np.eye(P, dtype=np.float32),
        "identb": np.eye(P).astype(ml_dtypes.bfloat16),
        "trimax": np.where(k[None, :] > k[:, None], NEG, 0.0).astype(ml_dtypes.bfloat16),
        "triexp": np.where(k[:, None] > k[None, :], NEG, 0.0).astype(ml_dtypes.bfloat16),
        "iota": np.tile(np.arange(E1, dtype=np.float32), (P, 1)),
    }
    arrays = {f"in_{n}": lay(v) for n, v in arrays.items()}
    nc = bacc.Bacc("TRN2", target_bir_lowering=False, num_devices=1)
    args = [nc.dram_tensor(n, v.shape, mybir.dt.from_np(v.dtype), kind="ExternalInput").ap() for n, v in arrays.items()]
    out = nc.dram_tensor("out", (P, NT, H), F32, kind="ExternalOutput").ap()
    build(nc, *args, out)
    r = run_bass_kernel_spmd(nc, [arrays], core_ids=[0])
    return r.results[0]["out"].swapaxes(0, 1).reshape(1, T, H)
```

```python
from contextlib import ExitStack

import concourse.bass as bass
import concourse.bacc as bacc
from concourse import mybir
import numpy as np

F32, F32R, BF16, U32 = mybir.dt.float32, mybir.dt.float32r, mybir.dt.bfloat16, mybir.dt.uint32
ALU = mybir.AluOpType
ACT = mybir.ActivationFunctionType
AX_X = mybir.AxisListType.X

P = 128
T, H = 2048, 256
NT = T // P
NB, BLK = 4, 512
TPB = BLK // P
NC = H // P
F, FT = 896, 896 // P
E0, R0 = 8, 32
HEADS, HD = 16, 16
GH, NG = 4, 4
E1, I1, TOP = 32, 96, 8
RPT = P // E1
JT = I1 // RPT
PAIR = 2 * TPB
KEEP = 0.8
EPS = 1e-5
NEG = -3.0e38
MROW = 4 * HD
STK = 96
VW = HD + 1
PARTS = ((1, 0), (0, 1), (0, 0))


class Signal:

    def __init__(self, sem, events, by=1):
        self.sem, self.by = sem, by
        self.at = {e: n + 1 for n, e in enumerate(events)}

    def after(self, event):
        return self.sem, self.by * self.at[event]


def attention_plan():
    lead, rate = 88, 4
    steps = [None] * (lead // rate)
    steps += [(g, qb, kt) for g in range(NG) for qb in range(NB) for kt in range(TPB * (qb + 1))]
    units = [(g, h, qt, kb) for g in range(NG) for qb in range(NB) for h in range(GH)
             for qt in range(TPB * qb, TPB * (qb + 1)) for kb in range(qb + 1)]
    return steps, [units[rate * s:rate * (s + 1)] for s in range(len(steps) + 4)], units


def build(nc, x_tm, x_fm, w13_d, a13_d, b13_d, w2a2_d, b2_d, wg0_d, wqkv_d, wo_d, wg1_d, wgu_d, wdn_d,
          ident_d, identb_d, trimax_d, triexp_d, iota_d, out_d):
    with ExitStack() as ctx:
        def sem(name):
            return ctx.enter_context(nc.semaphore(name))

        def sig(name, events, by=1):
            return Signal(sem(name), list(events), by)

        base = (nc.sbuf_base + 31) // 32 * 32
        cursor = [base]

        def at(name, shape, dt, offset=None):
            size = int(np.prod(shape[1:])) * (2 if dt == BF16 else 4)
            if offset is None:
                offset = cursor[0]
            cursor[0] = (offset + size + 31) // 32 * 32
            return nc.alloc_sbuf_tensor_at(name, list(shape), dt, offset=offset)

        x = at("x", [P, NT, H], F32)
        ident = at("ident", [P, P], F32)
        identb = at("identb", [P, P], BF16)
        trimax = at("trimax", [P, P], BF16)
        triexp = at("triexp", [P, P], BF16)
        iota = at("iota", [P, E1], F32)
        half_neg = at("half_neg", [P, TPB], F32)
        ln_stats = at("ln_stats", [P, 2, TPB, 6], F32)
        ln_mv = at("ln_mv", [P, 2, TPB, 2], F32)
        ln_var = at("ln_var", [P, 2, TPB], F32)
        ln_rstd = at("ln_rstd", [P, 2, TPB], F32)
        R = cursor[0]

        xtb = at("xtb", [P, 2, NC, BLK], F32R, R)
        w13 = at("w13", [P, 2, NC, 2, F], F32R)
        A13 = cursor[0]
        a13 = at("a13", [P, 2, NC, 2, E0 * R0], F32R)
        b13 = at("b13", [P, 2, NC, 2, F], F32R)
        w2a2 = at("w2a2", [P, 2, FT, 2 * H], F32R)
        b2 = at("b2", [P, 2, NC, H], F32R)
        wg0 = at("wg0", [P, NC, E0], F32)
        MA = cursor[0]
        ma = at("ma", [P, 2, 2, 2, NC, BLK], F32R)
        silu0 = at("silu0", [P, 2, BLK], F32)
        x2f = at("x2f", [P, 2, BLK], F32)
        x2u = at("x2u", [P, 2, BLK], F32)
        bc = at("bc", [P, 4, BLK], F32)
        bc_mask = at("bc_mask", [P, 2, BLK], BF16)
        mx = at("mx", [P, 2, TPB, P], F32)
        mx_mask = at("mx_mask", [P, 2, TPB, P], BF16)
        lg0 = at("lg0", [P, TPB, E0], F32)
        top0 = at("top0", [P, TPB, 8], F32)
        idx0 = at("idx0", [P, TPB, 8], U32)
        idx0f = at("idx0f", [P, TPB, 2], F32)
        mask0 = at("mask0", [P, 2, TPB, E0], F32)
        mdiff = at("mdiff", [P, TPB, E0], F32)
        gap0 = at("gap0", [P, TPB], F32)
        exp0 = at("exp0", [P, TPB], F32)
        den0 = at("den0", [P, TPB], F32)
        rw0 = at("rw0", [P, 2, TPB], F32)
        x2 = at("x2", [P, 2, 2, 3, BLK], F32R)
        B_END = cursor[0]
        xt_in = at("xt_in", [P, NC, T], F32, MA)
        att = at("att", [P, NC, H], F32)
        attn = at("attn", [P, NC, H], F32)
        att_t = at("att_t", [P, NC, H], F32)
        nmax_a = at("nmax_a", [P, NC], F32)
        sum_a = at("sum_a", [P, NC], F32)
        rec_a = at("rec_a", [P, NC], F32)
        w2a2_raw = at("w2a2_raw", [P, FT, 2 * H], F32)
        b13_raw = at("b13_raw", [P, NC, 2, F], F32)
        w13_raw = at("w13_raw", [P, NC, 2, F], F32)
        a13_raw = at("a13_raw", [P, NC, 2, E0 * R0], F32)
        b2_raw = at("b2_raw", [P, NC, H], F32)
        assert cursor[0] <= B_END, (cursor[0], B_END)

        o_tm = at("o_tm", [P, NT, H], F32, R)
        vaug = at("vaug", [P, NT * HEADS * VW + 15], F32)
        stack = at("stack", [STK, 2, 2, GH, T], F32R)
        SET = 2 * GH * T * 4
        S0 = cursor[0] - 2 * SET
        S1 = S0 + SET
        probs = at("probs", [P, 4, 2, BLK], F32)
        PR = cursor[0] - 4 * 2 * BLK * 4
        usum = at("usum", [P, BLK], F32)
        mpart = at("mpart", [P, 2, GH * TPB, NB], F32)
        nmx = at("nmx", [P, 2, GH * TPB], F32)
        mrow = at("mrow", [GH * TPB, 2, 2, P], F32R)
        zero_row = at("zero_row", [2, 256], F32R)
        rec_c = at("rec_c", [P, TPB, GH], F32)
        assert MA >= S1
        xtc = at("xtc", [P, 2, NC, T], F32R, MA)
        qk_out = at("qk_out", [P, 2, 2, BLK], F32R)
        assert cursor[0] <= S1 + SET
        wqkv = at("wqkv", [P, 2, NC, 3 * H], F32R, R)
        assert cursor[0] <= R + NT * H * 4
        wqkv_raw = at("wqkv_raw", [P, NC, 3 * H], F32, A13)
        ot = at("ot", [P, 2, NC, T], F32R, S0)
        wo = at("wo", [P, 2, NC, H], F32R)
        wo_raw = at("wo_raw", [P, NC, H], F32)
        gu_raw = at("gu_raw", [P, 3, NC * 2 * P], F32)
        dn_raw = at("dn_raw", [P, 3, H], F32)
        wg1_raw = at("wg1_raw", [P, NC, E1], F32)
        wg1 = at("wg1", [P, 2, NC, E1], F32R)
        assert cursor[0] <= S1
        xtd = at("xtd", [P, 2, NC, T], F32R, S1)
        gu = at("gu", [P, 3, 2, NC, 2, P], F32R)
        dn = at("dn", [P, 3, 2, H], F32R)
        assert cursor[0] <= PR
        lg1 = at("lg1", [P, 2, PAIR, E1], F32, R)
        exp1 = at("exp1", [P, 2, PAIR, E1], F32)
        prob1 = at("prob1", [P, PAIR, E1 + 8], F32)
        rest1 = at("rest1", [P, PAIR, E1 + 8], F32)
        comb1 = at("comb1", [P, PAIR, E1], F32)
        cex = at("cex", [P, 2, TPB, P], F32)
        ce_bc = at("ce_bc", [P, T], F32)
        assert cursor[0] <= S0, (cursor[0], S0)
        silu1 = at("silu1", [P, 2, BLK], F32, PR)
        hmul = at("hmul", [P, 2, BLK], F32)
        hfull = at("hfull", [P, 2, BLK], F32)
        r_max = at("r_max", [P, PAIR], F32)
        r_sum = at("r_sum", [P, PAIR], F32)
        r_rec = at("r_rec", [P, PAIR], F32)
        r_top = at("r_top", [P, PAIR, 8], F32)
        r_cum = at("r_cum", [P, PAIR, 8], F32)
        r_on = at("r_on", [P, PAIR, 8], F32)
        r_rw = at("r_rw", [P, PAIR, 8], F32)
        r_val = at("r_val", [P, PAIR, 8], F32)
        assert cursor[0] <= nc.sbuf_usable_end
        hpart = at("hpart", [P, 2, 2, 2, BLK], F32R, S0)

        ps = nc.alloc_psum_tensor("ps", [P, 8, 512], F32)
        qk_dram = nc.dram_tensor("qk_dram", [4, 2, P, T], F32)

        consts_in = sem("consts_in")
        x_in = [sem(f"x_in{b}") for b in range(NB)]
        xfm_in = sem("xfm_in")
        w0_in = {n: sem(f"w0_in_{n}") for n in ("w13", "a13", "b13", "w2a2", "b2")}
        wg0_in = sem("wg0_in")
        pool_const = sem("pool_const")
        w0_order = ["w13", "a13", "b13", "w2a2", "b2"]
        w0_hi = sig("w0_hi", w0_order)
        dve_step = sem("dve_step")
        pool_step = sem("pool_step")
        w0_ready = {n: sem(f"w0_ready_{n}") for n in w0_order}

        energy_ready = sig("energy_ready", range(NC))
        nmax_ready = sig("nmax_ready", range(NC))
        att_exp = sig("att_exp", range(NC))
        att_norm = sig("att_norm", range(NC))
        att_tps = sig("att_tps", range(NC))
        att_tsb = sig("att_tsb", range(NC))
        mix_ready = sig("mix_ready", range(NT))
        mix_read = sig("mix_read", range(NT))

        blocks = [(st, b) for st in "ABCD" for b in range(NB)]
        var_ready = sig("var_ready", blocks)
        rstd_ready = sig("rstd_ready", blocks)
        ln_ready = sig("ln_ready", blocks)

        turns = [(st, b, c) for st in "BCOD" for b in range(NB) for c in range(NC)]
        turned = sig("turned", turns)
        turned_hi = sig("turned_hi", turns)
        turned_lo = sig("turned_lo", turns)

        bb = range(NB)
        logits0 = sig("logits0", bb)
        gap_ready = sig("gap_ready", bb)
        gap_exp = sig("gap_exp", bb)
        wides = [(b, i) for b in bb for i in ("mask0", "mask1", "rw0", "rw1")]
        wide = sig("wide", wides)
        wide_ps = sig("wide_ps", wides)
        wide_sb = sig("wide_sb", wides)
        a_ps = sig("a_ps", [(b, w, c) for b in bb for w in range(2) for c in range(NC)])
        bwc = [(b, w, c) for b in bb for w in range(2) for c in range(NC)]
        ma_full = sig("ma_full", [i + (k,) for i in bwc for k in range(2)])
        ma_hi = sig("ma_hi", [i + (k,) for i in bwc for k in range(2)])
        ma_lo = [sig(f"ma_lo{k}", bwc) for k in range(2)]
        mw_ready = sig("mw_ready", bb)
        rows2_done = sig("rows2_done", bb)
        jk = [(b, j, k) for b in bb for j in range(FT) for k in range(2)]
        mlp_ps = sig("mlp_ps", jk)
        silu_ready = sig("silu_ready", jk)
        jks = [(b, j, k) for b in bb for j in range(FT) for k in range(3)]
        x2_full = sig("x2_full", jks)
        x2_hi = sig("x2_hi", jks)
        x2_lo = sig("x2_lo", jks)
        down0 = sig("down0", [(b, j) for b in bb for j in range(FT)])
        bc2 = [(b, c) for b in bb for c in range(NC)]
        g_full = sig("g_full", bc2)
        g_hi = sig("g_hi", bc2)
        g_lo = sig("g_lo", bc2)
        out0 = sig("out0", bb)
        bt = [(b, t) for b in bb for t in range(TPB)]
        out0_read = sig("out0_read", bt)

        wqkv_in = sem("wqkv_in")
        wqkv_hi = sem("wqkv_hi")
        wqkv_ready = sem("wqkv_ready")
        bm = [(b, m) for b in bb for m in range(4)]
        qk_ps = sig("qk_ps", bm)
        qk_hi = sig("qk_hi", bm)
        qk_lo = sig("qk_lo", bm)
        qk_out_sem = [sem(f"qk_out_slot{i}") for i in range(2)]
        v_ps = sig("v_ps", range(NT))
        v_ready = sig("v_ready", range(NT))
        v_ones = sem("v_ones")

        fill_ready = sem("fill_ready")
        pad_ready = [sem(f"pad_ready{i}") for i in range(2)]
        first_in = [sem(f"first_in{b}") for b in bb]
        stack_in = [sem(f"stack_in{i}") for i in range(2)]
        max_in = [sem(f"max_in{b}") for b in bb]

        steps, units_at, units = attention_plan()
        real = [r for r in steps if r]
        n_pre = len(steps) - len(real)
        per_group = len(real) // NG
        unit_no = {u: n for n, u in enumerate(units)}
        scored = sig("scored", units)
        reduced = sig("reduced", units)
        rounds = [(g, qb) for g in range(NG) for qb in range(NB)]
        round_no = {r: n for n, r in enumerate(rounds)}
        round_max = sig("round_max", rounds)
        max_turned = sig("max_turned", rounds)
        max_hi = sig("max_hi", rounds)
        max_lo = sig("max_lo", rounds)
        sp = [(s, p) for s in range(len(real)) for p in range(2)]
        st_ready = sig("st_ready", sp)
        exp_done = sig("exp_done", sp)
        pv_done = sig("pv_done", range(len(real)))
        u_copied = sig("u_copied", rounds)
        u_turned = sig("u_turned", rounds)
        o_ready = sig("o_ready", rounds)

        def closes(u):
            g, h, qt, kb = u
            return (g, kb) if (h, qt) == (GH - 1, TPB * kb + TPB - 1) else None

        max_at = {s + 1: closes(u) for s in range(len(units_at)) for u in units_at[s] if closes(u)}
        out_at = {n_pre + n + 2: (g, qb) for n, (g, qb, kt) in enumerate(real) if kt == TPB * (qb + 1) - 1}
        n_steps = len(steps) + 3
        misc = []
        for s in range(n_steps):
            if s in max_at:
                misc.append(("max", max_at[s]))
            if s in out_at:
                misc.append(("out", out_at[s]))

        def misc_free(eng, item):
            n = misc.index(item)
            if n:
                kind, key = misc[n - 1]
                eng.wait_ge(*(max_lo if kind == "max" else o_ready).after(key))

        wo_in = sem("wo_in")
        wo_hi = sem("wo_hi")
        wo_ready = sem("wo_ready")
        proj_ps = sig("proj_ps", range(NT))
        proj_read = sig("proj_read", range(NT))

        wg1_in = sem("wg1_in")
        wg1_hi = sem("wg1_hi")
        wg1_ready = sem("wg1_ready")
        logits1 = sig("logits1", bb)
        lg1_shift = sig("lg1_shift", range(2))
        prob_exp = sig("prob_exp", range(2))
        ce_wide = sig("ce_wide", bb)
        ce_ps = sig("ce_ps", bb)
        ce_sb = sig("ce_sb", bb)
        hj = [(hf, j) for hf in range(2) for j in range(JT)]
        raw_in = [sem(f"raw_in{i}") for i in range(3)]
        gu_hi = sem("gu_hi")
        wd_hi = sig("wd_hi", hj)
        wd_lo = sig("wd_lo", hj)
        hjt = [(hf, j, tb) for hf, j in hj for tb in range(2)]
        gu_ps = sig("gu_ps", hjt)
        silu1_ready = sig("silu1_ready", hjt)
        hmul_ready = sig("hmul_ready", hjt)
        h_full = sig("h_full", hjt)
        h_hi = sig("h_hi", hjt)
        h_lo = sig("h_lo", hjt)
        down1 = sig("down1", hj)
        acc_read = sig("acc_read", [(hf, t) for hf in range(2) for t in range(8)])
        stored = sem("stored")

        def hj_no(hf, j):
            return hf * JT + j

        wide_place = {"mask0": (mx_mask[:, 0], identb, 0, bc_mask[:, 0, :]), "mask1": (mx_mask[:, 1], identb, 1, bc_mask[:, 1, :]),
                      "rw0": (mx[:, 0], ident, 2, bc[:, 2, :]), "rw1": (mx[:, 1], ident, 3, bc[:, 3, :])}

        def g_part(b, part, c):
            return x2[:, (b + 1) * FT % 2, part, c, :]

        def turn_bank(st, b, c):
            return {"B": 0, "C": 0, "O": 4, "D": 2 + 2 * (b % 2)}[st] + c

        last_round = real.index((NG - 1, NB - 1, 0))

        def tail_turn(r):
            n = r - last_round
            return n // 5 if n >= 0 and n % 5 == 0 and n // 5 < NB - 1 else None

        def tail_tile(r):
            n = r - last_round
            return TPB * (n // 5) + n % 5 - 1 if n >= 0 and n % 5 and n // 5 < NB - 1 else None

        def qk_bank(n):
            return (2, 3, 6)[n % 3]

        early = {(2, m): range(m, m + 1) for m in range(4)}
        early.update({(3, m): range(4 + 2 * m, 6 + 2 * m) for m in range(4)})
        n_early = 12
        assert n_early <= n_pre

        def proj_bank(t):
            return t % 2 + (4 if t < NT - TPB else 0)

        block = ctx.enter_context(nc.Block())

        @block.sync
        def _(sp_):
            for b in range(NB):
                sp_.dma_start(x[:, TPB * b:TPB * (b + 1), :], x_tm[:, TPB * b:TPB * (b + 1), :]).then_inc(x_in[b], 16)
            sp_.dma_start(ident[:, :], ident_d).then_inc(consts_in, 16)
            sp_.dma_start(identb[:, :], identb_d).then_inc(consts_in, 16)
            sp_.dma_start(trimax[:, :], trimax_d).then_inc(consts_in, 16)
            sp_.dma_start(triexp[:, :], triexp_d).then_inc(consts_in, 16)
            sp_.dma_start(iota[:, :], iota_d).then_inc(consts_in, 16)
            sp_.dma_start(xt_in[:, :, :], x_fm).then_inc(xfm_in, 16)
            for n, raw, src in (("w13", w13_raw, w13_d), ("a13", a13_raw, a13_d), ("b13", b13_raw, b13_d), ("w2a2", w2a2_raw, w2a2_d),
                                ("b2", b2_raw, b2_d)):
                sp_.dma_start(raw.ap(), src).then_inc(w0_in[n], 16)
            sp_.dma_start(wg0[:, :, :], wg0_d).then_inc(wg0_in, 16)
            sp_.wait_ge(*a_ps.after((NB - 1, 1, NC - 1)))
            sp_.dma_start(wqkv_raw[:, :, :], wqkv_d).then_inc(wqkv_in, 16)

            def load_stacks(g, t0, t1, done):
                m, r = g // 2, GH * HD * (g % 2)
                for i in range(2):
                    for n in range(2):
                        for which, part in ((0, i), (1, n)):
                            lo = HD * (2 * i + n)
                            sp_.dma_start(stack[lo:lo + HD, g % 2, which, :, t0:t1].bitcast(F32),
                                          qk_dram[2 * which + m, part, r:r + GH * HD, t0:t1]
                                          .rearrange("(h r) t -> r h t", r=HD)).then_inc(done, 16)

            for b in range(NB):
                for m in range(4):
                    n = 4 * b + m
                    sp_.wait_ge(*qk_lo.after((b, m)))
                    sp_.dma_start(qk_dram[m, :, :, BLK * b:BLK * (b + 1)].rearrange("s p t -> p s t"),
                                  qk_out[:, n % 2, :, :].bitcast(F32)).then_inc(qk_out_sem[n % 2], 16)
                for i in range(2):
                    sp_.wait_ge(qk_out_sem[i], 32 * (b + 1))
                load_stacks(0, BLK * b, BLK * (b + 1), first_in[b])
            for g in range(1, NG):
                if g == 1:
                    sp_.wait_ge(pad_ready[1], 2)
                else:
                    sp_.wait_ge(*st_ready.after(((g - 1) * per_group - 1, 1)))
                    for n in range(T // 256):
                        sp_.dma_start(stack[MROW:MROW + 2, g % 2, 0, :, 256 * n:256 * (n + 1)].bitcast(F32),
                                      zero_row[:, None, :].broadcast_to([2, GH, 256]).bitcast(F32)) \
                            .then_inc(stack_in[g % 2], 16)
                load_stacks(g, 0, T, stack_in[g % 2])
            sp_.wait_ge(*st_ready.after(((NG - 1) * per_group - 1, 1)))
            sp_.dma_start(wo_raw[:, :, :], wo_d).then_inc(wo_in, 16)
            sp_.dma_start(wg1_raw[:, :, :], wg1_d).then_inc(wg1_in, 16)
            for n, (hf, j) in enumerate(hj):
                if n >= 3:
                    sp_.wait_ge(*wd_lo.after(hj[n - 3]))
                sp_.dma_start(gu_raw[:, n % 3, :], wgu_d[:, j, :]).then_inc(raw_in[n % 3], 16)
                sp_.dma_start(dn_raw[:, n % 3, :], wdn_d[:, j, :]).then_inc(raw_in[n % 3], 16)
            for b in range(NB):
                sp_.wait_ge(*ln_ready.after(("D", b)))
                sp_.dma_start(out_d[:, TPB * b:TPB * (b + 1), :], x[:, TPB * b:TPB * (b + 1), :]).then_inc(stored, 16)
            sp_.wait_ge(stored, 16 * NB)

        @block.gpsimd
        def _(pool):
            steps_done = [0]

            def settle(ins):
                steps_done[0] += 1
                ins.then_inc(pool_step, 1)
                pool.wait_ge(pool_step, steps_done[0])

            pool.memset(half_neg[:, :], -0.5).then_inc(pool_const, 1)
            pool.wait_ge(pool_const, 1)

            def rstd(st, b):
                pool.wait_ge(*var_ready.after((st, b)))
                pool.tensor_tensor(ln_rstd[:, b % 2, :], ln_var[:, b % 2, :], half_neg[:, :], ALU.pow) \
                    .then_inc(rstd_ready.sem, 1)

            def max_rows(g, qb):
                n = round_no[g, qb]
                pool.wait_ge(*max_lo.after((g, qb)))
                for h in range(GH):
                    for part in range(2):
                        row = MROW + part
                        pool.dma_start(stack[row:row + 1, g % 2, 0, h, BLK * qb:BLK * (qb + 1)].bitcast(F32)
                                       .rearrange("a (t q) -> a t q", q=P),
                                       mrow[TPB * h:TPB * (h + 1), n % 2, part, :].bitcast(F32)) \
                            .then_inc(max_in[qb], 16)

            def weights_lo(n, raw, part):
                pool.wait_ge(*w0_hi.after(n))
                pool.tensor_tensor(part[:, 1], raw.ap(), part[:, 0].bitcast(F32), ALU.subtract).then_inc(w0_ready[n], 1)
                pool.wait_ge(w0_ready[n], 1)

            weights_lo("w13", w13_raw, w13)
            rstd("A", 0)
            pool.wait_ge(*rstd_ready.after(("A", 0)))
            weights_lo("b13", b13_raw, b13)
            weights_lo("w2a2", w2a2_raw, w2a2)
            for b in range(NB):
                for i, (w, c) in enumerate([(w, c) for w in range(2) for c in range(NC)]):
                    pool.wait_ge(*ma_hi.after((b, w, c, 1)))
                    pool.tensor_tensor(ma[:, 1, w, 1, c, :], x2u[:, i % 2, :], ma[:, 0, w, 1, c, :].bitcast(F32),
                                       ALU.subtract).then_inc(ma_lo[1].sem, 1)
                pool.wait_ge(*wide_sb.after((b, "rw1")))
                pool.wait_ge(*ma_lo[1].after((b, 1, NC - 1)))
                if b:
                    pool.wait_ge(*g_full.after((b - 1, NC - 1)))
                settle(pool.tensor_tensor(bc[:, 0, :], bc_mask[:, 0, :], bc[:, 2, :], ALU.mult))
                settle(pool.tensor_tensor(bc[:, 1, :], bc_mask[:, 0, :], bc_mask[:, 1, :], ALU.add))
                pool.tensor_tensor(bc[:, 1, :], bc[:, 1, :], bc[:, 3, :], ALU.mult).then_inc(mw_ready.sem, 1)
                if b:
                    rstd("B", b - 1)
                else:
                    for a in range(1, NB):
                        rstd("A", a)
            pool.wait_ge(*mlp_ps.after((NB - 1, FT - 1, 0)))
            pool.wait_ge(*mw_ready.after(NB - 1))
            pool.memset(vaug[:, :], 1.0).then_inc(v_ones, 1)
            rstd("B", NB - 1)
            pool.wait_ge(*out0_read.after((NB - 1, TPB - 1)))
            pool.wait_ge(wqkv_ready, 1)
            pool.wait_ge(*rstd_ready.after(("B", NB - 1)))
            pool.memset(zero_row[:, :].bitcast(F32), 0.0).then_inc(fill_ready, 1)
            def fill_pad(i):
                for which in (1, 0):
                    pool.memset(stack[MROW:STK, i, which, :, :].rearrange("p h t -> p (h t)").bitcast(F32),
                                float(which)).then_inc(pad_ready[i], 1)

            pool.wait_ge(fill_ready, 1)
            fill_pad(0)
            pool.wait_ge(pad_ready[0], 2)
            for n, (g, qb) in enumerate(rounds):
                if n == 2:
                    pool.wait_ge(*v_ps.after(NT - 1))
                    for i in range(2):
                        pool.wait_ge(qk_out_sem[i], 32 * NB)
                    fill_pad(1)
                max_rows(g, qb)
            for b in range(NB):
                rstd("C", b)
            for hf in range(2):
                for j in range(JT):
                    n = hj_no(hf, j)
                    pool.wait_ge(*wd_hi.after((hf, j)))
                    settle(pool.tensor_tensor(gu[:, n % 3, 1, :, :, :].rearrange("p a b c -> p (a b c)"),
                                              gu_raw[:, n % 3, :],
                                              gu[:, n % 3, 0, :, :, :].rearrange("p a b c -> p (a b c)").bitcast(F32),
                                              ALU.subtract))
                    pool.tensor_tensor(dn[:, n % 3, 1, :], dn_raw[:, n % 3, :], dn[:, n % 3, 0, :].bitcast(F32),
                                       ALU.subtract).then_inc(wd_lo.sem, 1)
                    if hf and j in (3, 5):
                        rstd("D", (j - 3) // 2)
            for b in range(2, NB):
                rstd("D", b)

        @block.scalar
        def _(act):
            def copy(out, in_):
                return act.activation(out, in_, ACT.Copy)

            for c in range(NC):
                act.wait_ge(*nmax_ready.after(c))
                act.activation(att[:, c, :], ps[:, c, 0:H], ACT.Exp, bias=nmax_a[:, c:c + 1],
                               accum_out=sum_a[:, c:c + 1]).then_inc(att_exp.sem, 1)

            def turn_hi(st, b, dst):
                for c in range(NC):
                    act.wait_ge(*turned.after((st, b, c)))
                    copy(dst[:, 0, c, :] if st == "B" else dst[:, 0, c, BLK * b:BLK * (b + 1)], ps[:, turn_bank(st, b, c), :]) \
                        .then_inc(turned_hi.sem, 1)

            for n, raw, part in (("w13", w13_raw, w13), ("a13", a13_raw, a13), ("b13", b13_raw, b13), ("w2a2", w2a2_raw, w2a2),
                                 ("b2", b2_raw, b2)):
                act.wait_ge(w0_in[n], 16)
                copy(part[:, 0], raw.ap()).then_inc(w0_hi.sem, 1)

            def widen(b, names):
                for i in names:
                    act.wait_ge(*wide_ps.after((b, i)))
                    _, _, bank, place = wide_place[i]
                    if b and i in ("rw0", "rw1"):
                        act.wait_ge(*x2_full.after((b - 1, FT - 1, 2)))
                    elif b:
                        act.wait_ge(*mw_ready.after(b - 1))
                    copy(place, ps[:, bank, :]).then_inc(wide_sb.sem, 1)

            turn_hi("B", 0, xtb)
            for b in range(NB):
                act.wait_ge(*gap_ready.after(b))
                act.activation(exp0[:, :], gap0[:, :], ACT.Exp).then_inc(gap_exp.sem, 1)
                widen(b, ("mask0", "mask1"))
                if b:
                    for c in range(NC):
                        act.wait_ge(*g_full.after((b - 1, c)))
                        copy(g_part(b - 1, 0, c), x2f[:, c, :]).then_inc(g_hi.sem, 1)
                for i, (w, c) in enumerate([(w, c) for w in range(2) for c in range(NC)]):
                    for k, full in enumerate((x2f, x2u)):
                        act.wait_ge(*ma_full.after((b, w, c, k)))
                        copy(ma[:, 0, w, k, c, :], full[:, i % 2, :]).then_inc(ma_hi.sem, 1)
                for j in range(FT):
                    for k in range(2):
                        act.wait_ge(*mlp_ps.after((b, j, k)))
                        act.activation(silu0[:, k, :], ps[:, 0, :], ACT.Silu).then_inc(silu_ready.sem, 1)
                        if (j, k) == (0, 1):
                            widen(b, ("rw0", "rw1"))
                        act.wait_ge(*x2_full.after((b, j, k)))
                        if k == 0 and j >= 2:
                            act.wait_ge(*down0.after((b, j - 2)))
                        elif k == 0 and b:
                            act.wait_ge(*out0.after(b - 1))
                        copy(x2[:, (b * FT + j) % 2, 0, k, :], x2f[:, k, :]).then_inc(x2_hi.sem, 1)
                    if j == FT - 1:
                        if b < NB - 1:
                            turn_hi("B", b + 1, xtb)
                        else:
                            turn_hi("C", 0, xtc)
                            act.wait_ge(wqkv_in, 16)
                            copy(wqkv[:, 0, :, :], wqkv_raw[:, :, :]).then_inc(wqkv_hi, 1)
                    act.wait_ge(*x2_full.after((b, j, 2)))
                    copy(x2[:, (b * FT + j) % 2, 0, 2, :], x2u[:, 0, :]).then_inc(x2_hi.sem, 1)
            for c in range(NC):
                act.wait_ge(*g_full.after((NB - 1, c)))
                copy(g_part(NB - 1, 0, c), x2f[:, c, :]).then_inc(g_hi.sem, 1)

            def queries_keys_hi(b):
                for m in range(4):
                    n = 4 * b + m
                    act.wait_ge(*qk_ps.after((b, m)))
                    if n >= 2:
                        act.wait_ge(qk_out_sem[n % 2], 16 * (n // 2))
                    copy(qk_out[:, n % 2, 0, :], ps[:, qk_bank(n), :]).then_inc(qk_hi.sem, 1)

            for b in range(NB):
                for t in range(TPB * b, TPB * (b + 1)):
                    act.wait_ge(*v_ps.after(t))
                    act.wait_ge(v_ones, 1)
                    copy(vaug[:, 0:NT * HEADS * VW].rearrange("p (t h d) -> p t h d", t=NT, d=VW)[:, t, :, 0:HD],
                         ps[:, t % 2, 0:H].rearrange("p (h d) -> p h d", d=HD)).then_inc(v_ready.sem, 1)
                if b < NB - 1:
                    turn_hi("C", b + 1, xtc)
                queries_keys_hi(b)
            for s, (g, qb, kt) in enumerate(real):
                off = max(0, kt - TPB * qb) * P
                for p in range(2):
                    act.wait_ge(*st_ready.after((s, p)))
                    if s >= 2:
                        act.wait_ge(*pv_done.after(s - 2))
                    act.activation(probs[:, (2 * s + p) % 4, :, off:BLK], ps[:, 2 * p:2 * p + 2, off:BLK], ACT.Exp,
                                   scale=float(HD) ** -0.5).then_inc(exp_done.sem, 1)
                if (g, qb, kt) == (NG - 1, NB - 2, 0):
                    act.wait_ge(wo_in, 16)
                    copy(wo[:, 0, :, :], wo_raw[:, :, :]).then_inc(wo_hi, 1)
                    act.wait_ge(wg1_in, 16)
                    copy(wg1[:, 0, :, :], wg1_raw[:, :, :]).then_inc(wg1_hi, 1)
                if tail_turn(s) is not None:
                    turn_hi("O", tail_turn(s), ot)
            turn_hi("O", NB - 1, ot)
            def weights_hi(hf, j):
                n = hj_no(hf, j)
                act.wait_ge(raw_in[n % 3], 32 * (n // 3 + 1))
                if n >= 3:
                    act.wait_ge(*down1.after(hj[n - 3]))
                copy(gu[:, n % 3, 0, :, :, :].rearrange("p a b c -> p (a b c)"), gu_raw[:, n % 3, :]) \
                    .then_inc(gu_hi, 1)
                copy(dn[:, n % 3, 0, :], dn_raw[:, n % 3, :]).then_inc(wd_hi.sem, 1)

            def wide_weights(hf):
                for b in range(2 * hf, 2 * hf + 2):
                    act.wait_ge(*ce_ps.after(b))
                    copy(ce_bc[:, BLK * b:BLK * (b + 1)], ps[:, b % 2, :]).then_inc(ce_sb.sem, 1)

            turn_hi("D", 0, xtd)
            weights_hi(*hj[0])
            turn_hi("D", 1, xtd)
            weights_hi(*hj[1])
            for b in range(2, NB):
                turn_hi("D", b, xtd)
            for h in range(2):
                act.wait_ge(*lg1_shift.after(h))
                act.activation(exp1[:, h, :, :], lg1[:, h, :, :], ACT.Exp).then_inc(prob_exp.sem, 1)
            for i, (hf, j, tb) in enumerate(hjt):
                act.wait_ge(*gu_ps.after((hf, j, tb)))
                if i >= 2:
                    act.wait_ge(*hmul_ready.after(hjt[i - 2]))
                act.activation(silu1[:, tb, :], ps[:, 4 + 2 * tb, :], ACT.Silu).then_inc(silu1_ready.sem, 1)
                if (j, tb) == (0, 0):
                    wide_weights(hf)
                act.wait_ge(*h_full.after((hf, j, tb)))
                n = hj_no(hf, j)
                if n >= 2:
                    act.wait_ge(*down1.after(hj[n - 2]))
                copy(hpart[:, n % 2, tb, 0, :], hfull[:, tb, :]).then_inc(h_hi.sem, 1)
                if tb == 1 and n + 2 < len(hj):
                    weights_hi(*hj[n + 2])

        @block.vector
        def _(dve):
            done = [0]

            def step(ins):
                done[0] += 1
                ins.then_inc(dve_step, 1)

            def settle():
                dve.wait_ge(dve_step, done[0])

            def low(out, full, hi):
                return dve.tensor_tensor(out, full, hi.bitcast(F32), ALU.subtract)

            def statistics(st, b):
                settle()
                q = b % 2
                for t in range(TPB):
                    step(dve.bn_stats(ln_stats[:, q, t, :], x[:, TPB * b + t, :]))
                settle()
                for t in range(TPB):
                    step(dve.bn_aggr(ln_mv[:, q, t, :], ln_stats[:, q, t, :]))
                settle()
                dve.tensor_scalar(ln_var[:, q, :], ln_mv[:, q, :, 1], EPS, None, ALU.add).then_inc(var_ready.sem, 1)

            def normalise(st, b):
                q = b % 2
                dve.wait_ge(*rstd_ready.after((st, b)))
                for t in range(TPB):
                    ins = dve.tensor_scalar(x[:, TPB * b + t, :], x[:, TPB * b + t, :], ln_mv[:, q, t, 0:1],
                                            ln_rstd[:, q, t:t + 1], ALU.subtract, ALU.mult)
                    if t < TPB - 1:
                        step(ins)
                    else:
                        ins.then_inc(ln_ready.sem, 1)

            def layer_norm(st, b):
                statistics(st, b)
                normalise(st, b)

            for c in range(NC):
                dve.wait_ge(*energy_ready.after(c))
                dve.tensor_reduce(nmax_a[:, c:c + 1], ps[:, c, 0:H], AX_X, ALU.max, negate=True) \
                    .then_inc(nmax_ready.sem, 1)
            for c in range(NC):
                dve.wait_ge(*att_exp.after(c))
                step(dve.reciprocal(rec_a[:, c:c + 1], sum_a[:, c:c + 1]))
                settle()
                dve.tensor_scalar(attn[:, c, :], att[:, c, :], rec_a[:, c:c + 1], None, ALU.mult) \
                    .then_inc(att_norm.sem, 1)
            for j in range(NC):
                dve.wait_ge(*att_tps.after(j))
                dve.tensor_copy(att_t[:, j, :], ps[:, 2 + j, 0:H]).then_inc(att_tsb.sem, 1)
            for t in range(NT):
                dve.wait_ge(*mix_ready.after(t))
                dve.tensor_tensor(x[:, t, :], ps[:, 4 + t % 4, 0:H], x[:, t, :], ALU.add).then_inc(mix_read.sem, 1)
                if t == TPB - 1:
                    dve.wait_ge(*mix_read.after(t))
                    layer_norm("A", 0)

            def weights_lo(n, raw, part):
                dve.wait_ge(*w0_hi.after(n))
                low(part[:, 1], raw.ap(), part[:, 0]).then_inc(w0_ready[n], 1)

            def turn_lo(st, b, dst):
                for c in range(NC):
                    dve.wait_ge(*turned_hi.after((st, b, c)))
                    if st == "B":
                        out, hi = dst[:, 1, c, :], dst[:, 0, c, :]
                    else:
                        out, hi = (dst[:, i, c, BLK * b:BLK * (b + 1)] for i in (1, 0))
                    low(out, ps[:, turn_bank(st, b, c), :], hi).then_inc(turned_lo.sem, 1)

            def masks(b):
                dve.wait_ge(*logits0.after(b))
                step(dve.tensor_copy(lg0[:, :, :].rearrange("p t e -> p (t e)"), ps[:, 0, 0:TPB * E0]))
                settle()
                for t in range(TPB):
                    step(dve.max(top0[:, t, :], lg0[:, t, :]))
                settle()
                for t in range(TPB):
                    step(dve.max_index(idx0[:, t, :], top0[:, t, :], lg0[:, t, :]))
                dve.tensor_tensor(gap0[:, :], top0[:, :, 1], top0[:, :, 0], ALU.subtract).then_inc(gap_ready.sem, 1)
                settle()
                step(dve.tensor_copy(idx0f[:, :, :], idx0[:, :, 0:2]))
                settle()
                for k in range(2):
                    step(dve.tensor_tensor(mask0[:, k, :, :], iota[:, None, 0:E0].broadcast_to([P, TPB, E0]),
                                           idx0f[:, :, k:k + 1].broadcast_to([P, TPB, E0]), ALU.is_equal))
                settle()
                step(dve.tensor_tensor(mdiff[:, :, :], mask0[:, 1, :, :], mask0[:, 0, :, :], ALU.subtract))
                settle()
                for k, src in ((0, mask0[:, 0, :, :]), (1, mdiff[:, :, :])):
                    if b:
                        dve.wait_ge(*wide_ps.after((b - 1, f"mask{k}")))
                    dve.tensor_copy(mx_mask[:, k, :, :].rearrange("p t (r e) -> p t r e", e=E0),
                                    src[:, :, None, :].broadcast_to([P, TPB, P // E0, E0])).then_inc(wide.sem, 1)

            def weights(b):
                dve.wait_ge(*gap_exp.after(b))
                step(dve.tensor_scalar(den0[:, :], exp0[:, :], 1.0, None, ALU.add))
                settle()
                step(dve.reciprocal(rw0[:, 0, :], den0[:, :]))
                settle()
                step(dve.tensor_tensor(rw0[:, 1, :], exp0[:, :], rw0[:, 0, :], ALU.mult))
                settle()
                for k in range(2):
                    if b:
                        dve.wait_ge(*wide_ps.after((b - 1, f"rw{k}")))
                    dve.tensor_copy(mx[:, k, :, :], rw0[:, k, :, None].broadcast_to([P, TPB, P])) \
                        .then_inc(wide.sem, 1)

            def lora_sum(b):
                dve.wait_ge(*rows2_done.after(b))
                dve.wait_ge(*mw_ready.after(b))
                dve.wait_ge(*x2_hi.after((b, FT - 1, 2)))
                for c in range(NC):
                    for k in range(2):
                        step(dve.tensor_tensor(x2u[:, k, :], ps[:, 2 + 2 * k + c, :], bc[:, k, :], ALU.mult))
                    settle()
                    dve.wait_ge(*x2_hi.after((b, FT - 1, c)))
                    dve.tensor_tensor(x2f[:, c, :], x2u[:, 0, :], x2u[:, 1, :], ALU.add).then_inc(g_full.sem, 1)
                    dve.wait_ge(*g_full.after((b, c)))
                for c in range(NC):
                    dve.wait_ge(*g_hi.after((b, c)))
                    low(g_part(b, 1, c), x2f[:, c, :], g_part(b, 0, c)).then_inc(g_lo.sem, 1)

            def residual(b):
                dve.wait_ge(*out0.after(b))
                for t in range(TPB):
                    xt = x[:, TPB * b + t, :]
                    dve.tensor_tensor(xt, ps[:, 6 + t // 2, H * (t % 2):H * (t % 2 + 1)], xt, ALU.add) \
                        .then_inc(out0_read.sem, 1)

            turn_lo("B", 0, xtb)
            weights_lo("a13", a13_raw, a13)
            dve.wait_ge(w0_ready["w13"], 1)
            for b in range(NB):
                masks(b)
                if b:
                    lora_sum(b - 1)
                weights(b)
                if b == 0:
                    weights_lo("b2", b2_raw, b2)
                    for n in ("b13", "w2a2", "b2"):
                        dve.wait_ge(w0_ready[n], 1)
                for i, (w, c) in enumerate([(w, c) for w in range(2) for c in range(NC)]):
                    dve.wait_ge(*a_ps.after((b, w, c)))
                    for k, full in enumerate((x2f, x2u)):
                        dve.wait_ge(*wide_sb.after((b, f"mask{k}")))
                        if i >= 2 and k:
                            dve.wait_ge(*ma_lo[1].after((b, (i - 2) // NC, (i - 2) % NC)))
                        elif b and i < 2:
                            dve.wait_ge(*g_lo.after((b - 1, NC - 1)))
                        dve.tensor_tensor(full[:, i % 2, :], ps[:, 2 + 2 * w + c, :], bc_mask[:, k, :], ALU.mult) \
                            .then_inc(ma_full.sem, 1)
                    dve.wait_ge(*ma_hi.after((b, w, c, 0)))
                    low(ma[:, 1, w, 0, c, :], x2f[:, i % 2, :], ma[:, 0, w, 0, c, :]).then_inc(ma_lo[0].sem, 1)
                for j in range(FT):
                    slot = (b * FT + j) % 2
                    for k in range(2):
                        dve.wait_ge(*silu_ready.after((b, j, k)))
                        if j:
                            dve.wait_ge(*x2_lo.after((b, j - 1, k)))
                        else:
                            dve.wait_ge(*ma_lo[0].after((b, 1, NC - 1)))
                        dve.tensor_tensor(x2f[:, k, :], ps[:, 1, :], silu0[:, k, :], ALU.mult) \
                            .then_inc(x2_full.sem, 1)
                        if k == 0:
                            dve.wait_ge(*x2_hi.after((b, j, 0)))
                            low(x2[:, slot, 1, 0, :], x2f[:, 0, :], x2[:, slot, 0, 0, :]).then_inc(x2_lo.sem, 1)
                    dve.wait_ge(*x2_full.after((b, j, 1)))
                    if j:
                        dve.wait_ge(*x2_lo.after((b, j - 1, 2)))
                    else:
                        dve.wait_ge(*ma_lo[1].after((b, 1, NC - 1)))
                    for k in range(2):
                        dve.wait_ge(*wide_sb.after((b, f"rw{k}")))
                        step(dve.tensor_tensor(x2u[:, k, :], x2f[:, k, :], bc[:, 2 + k, :], ALU.mult))
                    dve.wait_ge(*x2_hi.after((b, j, 1)))
                    low(x2[:, slot, 1, 1, :], x2f[:, 1, :], x2[:, slot, 0, 1, :]).then_inc(x2_lo.sem, 1)
                    settle()
                    dve.tensor_tensor(x2u[:, 0, :], x2u[:, 0, :], x2u[:, 1, :], ALU.add).then_inc(x2_full.sem, 1)
                    if j == FT - 1:
                        if b < NB - 1:
                            turn_lo("B", b + 1, xtb)
                        else:
                            turn_lo("C", 0, xtc)
                            dve.wait_ge(wqkv_hi, 1)
                            low(wqkv[:, 1, :, :], wqkv_raw[:, :, :], wqkv[:, 0, :, :]).then_inc(wqkv_ready, 1)
                    dve.wait_ge(*x2_hi.after((b, j, 2)))
                    low(x2[:, slot, 1, 2, :], x2u[:, 0, :], x2[:, slot, 0, 2, :]).then_inc(x2_lo.sem, 1)
                    if j == 0 and b:
                        residual(b - 1)
                    if b == 0 and j in (1, 3, 5):
                        statistics("A", (j + 1) // 2)
                    if b == 0 and j in (2, 4, 6):
                        normalise("A", j // 2)
                    if b and j == 1:
                        dve.wait_ge(*out0_read.after((b - 1, TPB - 1)))
                        statistics("B", b - 1)
                    if b and j == 2:
                        normalise("B", b - 1)
                dve.wait_ge(*x2_lo.after((b, FT - 1, 2)))
            lora_sum(NB - 1)
            residual(NB - 1)

            def turned_max(g, qb):
                n = round_no[g, qb]
                dve.wait_ge(*max_turned.after((g, qb)))
                if n >= 2:
                    g2, qb2 = rounds[n - 2]
                    dve.wait_ge(max_in[qb2], 128 * (g2 + 1))
                dve.tensor_copy(mrow[:, n % 2, 0, :], ps[0:GH * TPB, 7, 0:P]).then_inc(max_hi.sem, 1)
                dve.wait_ge(*max_hi.after((g, qb)))
                low(mrow[:, n % 2, 1, :], ps[0:GH * TPB, 7, 0:P], mrow[:, n % 2, 0, :]).then_inc(max_lo.sem, 1)

            def head_out(g, qb):
                dve.wait_ge(*u_turned.after((g, qb)))
                view = ps[:, 7, :].rearrange("p (t h d) -> p t h d", t=TPB, h=GH)
                step(dve.reciprocal(rec_c[:, :, :], view[:, :, :, HD]))
                settle()
                dve.tensor_tensor(o_tm[:, TPB * qb:TPB * (qb + 1), GH * HD * g:GH * HD * (g + 1)]
                                  .rearrange("p t (h d) -> p t h d", d=HD), view[:, :, :, 0:HD],
                                  rec_c[:, :, :, None].broadcast_to([P, TPB, GH, HD]), ALU.mult) \
                    .then_inc(o_ready.sem, 1)

            def attention_residual(t):
                dve.wait_ge(*proj_ps.after(t))
                dve.tensor_tensor(x[:, t, :], ps[:, proj_bank(t), 0:H], x[:, t, :], ALU.add).then_inc(proj_read.sem, 1)
                if t % TPB == TPB - 1 and t // TPB != NB - 2:
                    dve.wait_ge(*proj_read.after(t))
                    layer_norm("C", t // TPB)

            def maxima(s):
                for u in units_at[s] if s < len(units_at) else []:
                    g, h, qt, kb = u
                    qb = qt // TPB
                    n = round_no[g, qb]
                    width = BLK if kb < qb else P * (qt % TPB + 1)
                    dve.wait_ge(*scored.after(u))
                    dve.tensor_reduce(mpart[:, n % 2, TPB * h + qt % TPB, kb:kb + 1],
                                      ps[:, 4 + unit_no[u] % 2, 0:width], AX_X, ALU.max).then_inc(reduced.sem, 1)
                    if closes(u):
                        dve.wait_ge(*reduced.after(u))
                        if n >= 2:
                            dve.wait_ge(*max_turned.after(rounds[n - 2]))
                        dve.tensor_reduce(nmx[:, n % 2, :], mpart[:, n % 2, :, 0:qb + 1], AX_X, ALU.max, negate=True) \
                            .then_inc(round_max.sem, 1)
                if s in max_at:
                    turned_max(*max_at[s])

            for b in range(NB):
                if b < NB - 1:
                    turn_lo("C", b + 1, xtc)
                for m in range(4):
                    for s in early.get((b, m), ()):
                        maxima(s)
                    n = 4 * b + m
                    dve.wait_ge(*qk_hi.after((b, m)))
                    low(qk_out[:, n % 2, 1, :], ps[:, qk_bank(n), :], qk_out[:, n % 2, 0, :]).then_inc(qk_lo.sem, 1)
                if b == 0:
                    dve.wait_ge(*out0_read.after((NB - 1, TPB - 1)))
                    layer_norm("B", NB - 1)
            for s in range(n_early, n_steps):
                maxima(s)
                if s in out_at:
                    head_out(*out_at[s])
                r = s - n_pre - 1
                if 0 <= r < len(real):
                    g, qb, kt = real[r]
                    if kt == TPB * (qb + 1) - 1:
                        dve.wait_ge(*pv_done.after(r))
                        n = round_no[g, qb]
                        if n:
                            dve.wait_ge(*u_turned.after(rounds[n - 1]))
                        dve.tensor_copy(usum[:, :], ps[:, 6, :]).then_inc(u_copied.sem, 1)
                r = s - n_pre
                if 0 <= r < len(real):
                    if real[r] == (NG - 1, NB - 2, 0):
                        dve.wait_ge(wo_hi, 1)
                        low(wo[:, 1, :, :], wo_raw[:, :, :], wo[:, 0, :, :]).then_inc(wo_ready, 1)
                        dve.wait_ge(wg1_hi, 1)
                        low(wg1[:, 1, :, :], wg1_raw[:, :, :], wg1[:, 0, :, :]).then_inc(wg1_ready, 1)
                    if tail_turn(r) is not None:
                        turn_lo("O", tail_turn(r), ot)
                    if tail_tile(r) is not None:
                        attention_residual(tail_tile(r))

            dve.wait_ge(*proj_read.after(NT - TPB - 1))
            statistics("C", NB - 2)
            turn_lo("O", NB - 1, ot)
            turn_lo("D", 0, xtd)
            normalise("C", NB - 2)
            for t in range(NT - TPB, NT):
                attention_residual(t)
            for b in range(1, NB):
                turn_lo("D", b, xtd)

            wide1, eight = [P, PAIR, E1], [P, PAIR, TOP]

            def shifted_logits(h):
                for b in range(2 * h, 2 * h + 2):
                    dve.wait_ge(*logits1.after(b))
                lgv = ps[:, 7 - h, 0:PAIR * E1].rearrange("p (t e) -> p t e", e=E1)
                step(dve.tensor_reduce(r_max[:, :], lgv, AX_X, ALU.max))
                settle()
                dve.tensor_tensor(lg1[:, h, :, :], lgv, r_max[:, :, None].broadcast_to(wide1), ALU.subtract) \
                    .then_inc(lg1_shift.sem, 1)
                dve.wait_ge(*lg1_shift.after(h))

            def best_eight(h):
                settle()
                dve.wait_ge(*prob_exp.after(h))
                step(dve.tensor_reduce(r_sum[:, :], exp1[:, h, :, :], AX_X, ALU.add))
                settle()
                step(dve.reciprocal(r_rec[:, :], r_sum[:, :]))
                settle()
                step(dve.tensor_tensor(prob1[:, :, 0:E1], exp1[:, h, :, :], r_rec[:, :, None].broadcast_to(wide1),
                                       ALU.mult))
                settle()
                for t in range(PAIR):
                    step(dve.max(r_top[:, t, :], prob1[:, t, 0:E1]))
                settle()

            def running_share():
                step(dve.tensor_reduce(r_sum[:, :], r_top[:, :, :], AX_X, ALU.add))
                settle()
                step(dve.tensor_scalar(r_max[:, :], r_sum[:, :], 1e-12, None, ALU.max))
                settle()
                step(dve.reciprocal(r_rec[:, :], r_max[:, :]))
                settle()
                step(dve.tensor_tensor(r_cum[:, :, :], r_top[:, :, :], r_rec[:, :, None].broadcast_to(eight),
                                       ALU.mult))
                settle()
                for r in range(1, TOP):
                    step(dve.tensor_tensor(r_cum[:, :, r], r_cum[:, :, r - 1], r_cum[:, :, r], ALU.add))
                    settle()

            def kept():
                step(dve.tensor_scalar(r_on[:, :, 1:TOP], r_cum[:, :, 0:TOP - 1], KEEP, None, ALU.is_lt))
                step(dve.memset(r_on[:, :, 0:1], 1.0))
                settle()
                step(dve.tensor_tensor(r_rw[:, :, :], r_top[:, :, :], r_on[:, :, :], ALU.mult))
                settle()
                step(dve.tensor_reduce(r_sum[:, :], r_rw[:, :, :], AX_X, ALU.add))
                step(dve.scalar_tensor_tensor(out=r_val[:, :, :], in0=r_on[:, :, :], scalar=-1.0, in1=r_rw[:, :, :],
                                              op0=ALU.add, op1=ALU.add))
                settle()
                step(dve.tensor_scalar(r_max[:, :], r_sum[:, :], 1e-12, None, ALU.max))
                for t in range(PAIR):
                    step(dve.match_replace(rest1[:, t, :], r_val[:, t, :], prob1[:, t, :], 0.0))
                settle()

            def combine(h):
                step(dve.reciprocal(r_rec[:, :], r_max[:, :]))
                step(dve.tensor_tensor(comb1[:, :, :], prob1[:, :, 0:E1], rest1[:, :, 0:E1], ALU.subtract))
                settle()
                step(dve.tensor_tensor(comb1[:, :, :], comb1[:, :, :], r_rec[:, :, None].broadcast_to(wide1),
                                       ALU.mult))
                settle()
                for i in range(2):
                    if h:
                        dve.wait_ge(*ce_ps.after(i))
                    dve.tensor_copy(cex[:, i, :, :].rearrange("p t (r e) -> p t r e", e=E1),
                                    comb1[:, TPB * i:TPB * (i + 1), None, :].broadcast_to([P, TPB, RPT, E1])) \
                        .then_inc(ce_wide.sem, 1)

            step(dve.memset(prob1[:, :, E1:E1 + 8], -1.0))
            shifted_logits(0)
            shifted_logits(1)
            best_eight(0)
            running_share()
            kept()
            combine(0)

            for hf in range(2):
                for j in range(JT):
                    n = hj_no(hf, j)
                    for tb in range(2):
                        key = (hf, j, tb)
                        dve.wait_ge(*silu1_ready.after(key))
                        dve.tensor_tensor(hmul[:, tb, :], ps[:, 5 + 2 * tb, :], silu1[:, tb, :], ALU.mult) \
                            .then_inc(hmul_ready.sem, 1)
                        dve.wait_ge(*hmul_ready.after(key))
                        col = BLK * (2 * hf + tb)
                        if j == 0:
                            dve.wait_ge(*ce_sb.after(2 * hf + tb))
                        dve.tensor_tensor(hfull[:, tb, :], hmul[:, tb, :], ce_bc[:, col:col + BLK], ALU.mult) \
                            .then_inc(h_full.sem, 1)
                        dve.wait_ge(*h_hi.after(key))
                        low(hpart[:, n % 2, tb, 1, :], hfull[:, tb, :], hpart[:, n % 2, tb, 0, :]) \
                            .then_inc(h_lo.sem, 1)
                    if (hf, j) == (0, 1):
                        best_eight(1)
                    if (hf, j) == (0, 2):
                        running_share()
                    if (hf, j) == (0, 3):
                        kept()
                    if (hf, j) == (0, 4):
                        combine(1)
                    if (hf, j) == (1, 1):
                        statistics("D", 0)
                    if (hf, j) == (1, 3):
                        normalise("D", 0)
                        statistics("D", 1)
                    if (hf, j) == (1, 6):
                        normalise("D", 1)
                dve.wait_ge(*down1.after((hf, JT - 1)))
                for b in range(2 * hf, 2 * hf + 2):
                    for t in range(TPB * b, TPB * (b + 1)):
                        a = t - PAIR * hf
                        dve.tensor_tensor(x[:, t, :], ps[:, a // 2, H * (a % 2):H * (a % 2 + 1)], x[:, t, :], ALU.add) \
                            .then_inc(acc_read.sem, 1)
                    dve.wait_ge(*acc_read.after((hf, TPB * (b + 1) - 1 - PAIR * hf)))
                    if hf:
                        layer_norm("D", b)

        @block.tensor
        def _(pe):
            def product(out, pairs, first=True, last=True, **more):
                n, todo = 0, len(pairs) * len(PARTS)
                for lhs, rhs in pairs:
                    for i, k in PARTS:
                        n += 1
                        mm = pe.matmul(out, lhs(i), rhs(k), start=first and n == 1, stop=last and n == todo, **more)
                return mm

            def turn(st, b, src):
                for c in range(NC):
                    for t in range(TPB):
                        mm = pe.transpose(ps[:, turn_bank(st, b, c), P * t:P * (t + 1)], src[:, TPB * b + t, P * c:P * (c + 1)],
                                          ident[:, :])
                    mm.then_inc(turned.sem, 1)

            for t in range(NT):
                if t % TPB == 0:
                    pe.wait_ge(x_in[t // TPB], 16)
                for c in range(NC):
                    mm = pe.matmul(ps[:, c, 0:H], x[:, t, P * c:P * (c + 1)], x[:, t, :], start=t == 0, stop=t == NT - 1)
                    if t == NT - 1:
                        mm.then_inc(energy_ready.sem, 1)
            pe.wait_ge(consts_in, 80)
            for j in range(NC):
                for c in range(NC):
                    if j == 0:
                        pe.wait_ge(*att_norm.after(c))
                    mm = pe.transpose(ps[:, 2 + j, P * c:P * (c + 1)], attn[:, c, P * j:P * (j + 1)], ident[:, :])
                mm.then_inc(att_tps.sem, 1)
            pe.wait_ge(xfm_in, 16)
            pe.wait_ge(*att_tsb.after(NC - 1))
            for t in range(NT):
                if t >= 4:
                    pe.wait_ge(*mix_read.after(t - 4))
                for j in range(NC):
                    mm = pe.matmul(ps[:, 4 + t % 4, 0:H], xt_in[:, j, P * t:P * (t + 1)], att_t[:, j, :],
                                   start=j == 0, stop=j == NC - 1)
                mm.then_inc(mix_ready.sem, 1)

            pe.wait_ge(wg0_in, 16)

            def logits(b):
                for c in range(NC):
                    pe.wait_ge(*turned_lo.after(("B", b, c)))
                for t in range(TPB):
                    n = 0
                    for c in range(NC):
                        for i in (1, 0):
                            mm = pe.matmul(ps[:, 0, E0 * t:E0 * (t + 1)],
                                           xtb[:, i, c, P * t:P * (t + 1)].bitcast(F32), wg0[:, c, :],
                                           start=n == 0, stop=n == 3)
                            n += 1
                mm.then_inc(logits0.sem, 1)

            def widen(b, names):
                for i in names:
                    pe.wait_ge(*wide.after((b, i)))
                    src, unit, bank, _ = wide_place[i]
                    for t in range(TPB):
                        mm = pe.matmul(ps[:, bank, P * t:P * (t + 1)], src[:, t, :], unit[:, :], start=True, stop=True)
                    mm.then_inc(wide_ps.sem, 1)

            def hidden(j):
                for w in range(2):
                    product(ps[:, w, :],
                            [(lambda i, c=c: w13[:, i, c, w, P * j:P * (j + 1)], lambda k, c=c: xtb[:, k, c, :])
                             for c in range(NC)], True, False, skip_group_check=True)

            def lora(b, j, k):
                for w in range(2):
                    if (j, k, w) == (0, 0, 1) and b:
                        lora_out(b - 1)
                    if j == 0:
                        pe.wait_ge(*ma_lo[k].after((b, w, NC - 1)))
                    mm = product(ps[:, w, :],
                                 [(lambda i, c=c: b13[:, i, c, w, P * j:P * (j + 1)],
                                   lambda q, c=c: ma[:, q, w, k, c, :]) for c in range(NC)],
                                 False, True, skip_group_check=True)
                mm.then_inc(mlp_ps.sem, 1)

            def down_lora(b, j, k, c):
                slot = (b * FT + j) % 2
                pe.wait_ge(*x2_lo.after((b, j, k)))
                mm = product(ps[:, 2 + 2 * k + c, :],
                        [(lambda i: w2a2[:, i, j, H + P * c:H + P * (c + 1)], lambda q: x2[:, slot, q, k, :])],
                        j == 0, j == FT - 1, skip_group_check=True)
                return mm

            def down_sum(b, j):
                slot = (b * FT + j) % 2
                pe.wait_ge(*x2_lo.after((b, j, 2)))
                for t in range(TPB):
                    mm = product(ps[:, 6 + t // 2, H * (t % 2):H * (t % 2 + 1)],
                                 [(lambda i: x2[:, slot, i, 2, P * t:P * (t + 1)], lambda q: w2a2[:, q, j, 0:H])],
                                 j == 0 and t % 2 == 0, False, skip_group_check=True)
                mm.then_inc(down0.sem, 1)

            def lora_out(b):
                for c in range(NC):
                    pe.wait_ge(*g_lo.after((b, c)))
                for t in range(TPB):
                    mm = product(ps[:, 6 + t // 2, H * (t % 2):H * (t % 2 + 1)],
                                 [(lambda i, c=c: g_part(b, i, c)[:, P * t:P * (t + 1)], lambda q, c=c: b2[:, q, c, :])
                                  for c in range(NC)], False, True, skip_group_check=True)
                mm.then_inc(out0.sem, 1)

            pe.wait_ge(*ln_ready.after(("A", 0)))
            turn("B", 0, x)
            logits(0)
            for b in range(NB):
                widen(b, ("mask0", "mask1"))
                pe.wait_ge(*wide_sb.after((b, "mask1")))
                if b == 0:
                    pe.wait_ge(w0_ready["w13"], 1)
                hidden(0)
                if b:
                    pe.wait_ge(*g_full.after((b - 1, NC - 1)))
                else:
                    pe.wait_ge(*mix_read.after(NT - 1))
                if b == 0:
                    pe.wait_ge(w0_ready["a13"], 1)
                for w in range(2):
                    for c in range(NC):
                        product(ps[:, 2 + 2 * w + c, :],
                                [(lambda q, i=i: a13[:, q, i, w, P * c:P * (c + 1)], lambda q, i=i: xtb[:, q, i, :])
                                 for i in range(NC)]).then_inc(a_ps.sem, 1)
                if b == 0:
                    for n in ("b13", "w2a2", "b2"):
                        pe.wait_ge(w0_ready[n], 1)
                for j in range(FT):
                    if j:
                        pe.wait_ge(*x2_full.after((b, j - 1, 1)))
                        hidden(j)
                    lora(b, j, 0)
                    if j:
                        if j == 1:
                            pe.wait_ge(*wide_sb.after((b, "rw1")))
                        for k, c in ((0, 0), (0, 1), (1, 0)):
                            down_lora(b, j - 1, k, c)
                    pe.wait_ge(*x2_full.after((b, j, 0)))
                    lora(b, j, 1)
                    if j == 0:
                        pe.wait_ge(*ma_full.after((b, 1, NC - 1, 1)))
                        widen(b, ("rw0", "rw1"))
                    if j:
                        down_lora(b, j - 1, 1, 1)
                        if j == 1 and b:
                            pe.wait_ge(*out0_read.after((b - 1, TPB - 1)))
                        down_sum(b, j - 1)
                pe.wait_ge(*x2_full.after((b, FT - 1, 1)))
                if b < NB - 1:
                    pe.wait_ge(*ln_ready.after(("A", b + 1)))
                    turn("B", b + 1, x)
                else:
                    pe.wait_ge(*ln_ready.after(("B", 0)))
                    turn("C", 0, x)
                for c in range(NC):
                    down_lora(b, FT - 1, 0, c)
                if b < NB - 1:
                    logits(b + 1)
                for c in range(NC):
                    mm = down_lora(b, FT - 1, 1, c)
                mm.then_inc(rows2_done.sem, 1)
                down_sum(b, FT - 1)

            def values_of(b):
                pe.wait_ge(*turned_lo.after(("C", b, NC - 1)))
                for t in range(TPB * b, TPB * (b + 1)):
                    if t >= 2:
                        pe.wait_ge(*v_ready.after(t - 2))
                    product(ps[:, t % 2, 0:H],
                            [(lambda i, c=c: xtc[:, i, c, P * t:P * (t + 1)], lambda k, c=c: wqkv[:, k, c, 2 * H:3 * H])
                             for c in range(NC)]).then_inc(v_ps.sem, 1)

            def query_key_chunk(b, m):
                n = 4 * b + m
                if n >= 3:
                    pe.wait_ge(*qk_lo.after(bm[n - 3]))
                product(ps[:, qk_bank(n), :],
                        [(lambda i, c=c: wqkv[:, i, c, P * m:P * (m + 1)],
                          lambda k, c=c: xtc[:, k, c, BLK * b:BLK * (b + 1)]) for c in range(NC)]) \
                    .then_inc(qk_ps.sem, 1)

            def score_units(s, first, last):
                for u in units_at[s][first:last] if s < len(units_at) else []:
                    g, h, qt, kb = u
                    if (h, qt, kb) == (0, 0, 0) and g:
                        pe.wait_ge(pad_ready[g % 2], 2)
                        pe.wait_ge(stack_in[g % 2], 16 * (8 + (T // 256) * (g >= 2)) + 128 * (g == 3))
                    if g == 0 and (h, qt % TPB, kb) == (0, 0, 0):
                        pe.wait_ge(first_in[qt // TPB], 128)
                    last = kb == qt // TPB
                    width = P * (qt % TPB + 1) if last else BLK
                    n = unit_no[u]
                    if n >= 2:
                        pe.wait_ge(*reduced.after(units[n - 2]))
                    mm = pe.matmul(ps[:, 4 + n % 2, 0:width], stack[:, g % 2, 0, h, P * qt:P * (qt + 1)],
                                   stack[:, g % 2, 1, h, BLK * kb:BLK * kb + width], start=True, stop=not last)
                    if last:
                        mm = pe.matmul(ps[:, 4 + n % 2, width - P:width], identb[:, :], trimax[:, :],
                                       start=False, stop=True)
                    mm.then_inc(scored.sem, 1)

            def turn_maxima(s):
                if s in max_at:
                    n = round_no[max_at[s]]
                    pe.wait_ge(*round_max.after(max_at[s]))
                    misc_free(pe, ("max", max_at[s]))
                    pe.transpose(ps[0:GH * TPB, 7, 0:P], nmx[:, n % 2, :], ident[:, :]).then_inc(max_turned.sem, 1)

            pe.wait_ge(wqkv_ready, 1)
            for b in range(NB):
                values_of(b)
                if b < NB - 1:
                    pe.wait_ge(*ln_ready.after(("B", b + 1)))
                    pe.wait_ge(*v_ready.after(TPB * (b + 1) - 1))
                    turn("C", b + 1, x)
                if b == 0:
                    pe.wait_ge(*g_full.after((NB - 1, NC - 1)))
                    lora_out(NB - 1)
                for m in range(4):
                    if (b, m) == (0, 2):
                        pe.wait_ge(*out0_read.after((NB - 1, TPB - 1)))
                    for n, s in enumerate(early.get((b, m), ())):
                        if s == 0:
                            pe.wait_ge(pad_ready[0], 2)
                        score_units(s, 0, 2)
                        if n == 0:
                            query_key_chunk(b, m)
                        score_units(s, 2, None)
                        turn_maxima(s)
                    if (b, m) not in early:
                        query_key_chunk(b, m)
            pe.wait_ge(*v_ready.after(NT - 1))
            pe.wait_ge(*qk_lo.after((NB - 1, 3)))

            def values(r, half):
                g, qb, kt = real[r]
                off = max(0, kt - TPB * qb) * P
                lo, hi = max(off, BLK // 2 * half), BLK // 2 * (half + 1)
                if half == 0:
                    n = round_no[g, qb]
                    pe.wait_ge(*exp_done.after((r, 1)))
                    if kt == 0 and n:
                        pe.wait_ge(*u_copied.after(rounds[n - 1]))
                if lo >= hi:
                    return
                for h in range(GH):
                    v0 = (kt * HEADS + GH * g + h) * VW
                    mm = pe.matmul(ps[32 * h:32 * (h + 1), 6, lo:hi], vaug[:, v0:v0 + 32],
                                   probs[:, (2 * r + h // 2) % 4, h % 2, lo:hi],
                                   start=kt == 0 and half == 0, stop=kt == TPB * (qb + 1) - 1, skip_group_check=True)
                if half:
                    mm.then_inc(pv_done.sem, 1)

            def turn_output(b):
                pe.wait_ge(*o_ready.after((NG - 1, b)))
                if b:
                    pe.wait_ge(*proj_read.after(TPB * b - 1))
                turn("O", b, o_tm)

            def project_output(t):
                if t == 0:
                    pe.wait_ge(wo_ready, 1)
                if t % TPB == 0:
                    pe.wait_ge(*turned_lo.after(("O", t // TPB, NC - 1)))
                if t >= 2:
                    pe.wait_ge(*proj_read.after(t - 2))
                product(ps[:, proj_bank(t), 0:H],
                        [(lambda i, c=c: ot[:, i, c, P * t:P * (t + 1)], lambda k, c=c: wo[:, k, c, :])
                         for c in range(NC)]).then_inc(proj_ps.sem, 1)

            for s in range(n_early, n_steps):
                r = s - n_pre
                if 0 <= r < len(real):
                    g, qb, kt = real[r]
                    diag = kt >= TPB * qb
                    off = max(0, kt - TPB * qb) * P
                    if kt == 0:
                        pe.wait_ge(max_in[qb], 128 * (g + 1))
                for p in range(2):
                    score_units(s, p, p + 1)
                    if 0 <= r < len(real):
                        if r:
                            pe.wait_ge(*exp_done.after((r - 1, p)))
                        for h in (2 * p, 2 * p + 1):
                            mm = pe.matmul(ps[:, h, off:BLK], stack[:, g % 2, 1, h, P * kt:P * (kt + 1)],
                                           stack[:, g % 2, 0, h, BLK * qb + off:BLK * (qb + 1)],
                                           start=True, stop=not diag)
                            if diag:
                                mm = pe.matmul(ps[:, h, off:off + P], identb[:, :], triexp[:, :],
                                               start=False, stop=True)
                        mm.then_inc(st_ready.sem, 1)
                score_units(s, 2, 3)
                if 0 <= r - 1 < len(real):
                    values(r - 1, 0)
                score_units(s, 3, None)
                if 0 <= r - 1 < len(real):
                    values(r - 1, 1)
                turn_maxima(s)
                if s in out_at:
                    pe.wait_ge(*u_copied.after(out_at[s]))
                    misc_free(pe, ("out", out_at[s]))
                    for t in range(TPB):
                        mm = pe.transpose(ps[:, 7, P * t:P * (t + 1)], usum[:, P * t:P * (t + 1)], ident[:, :])
                    mm.then_inc(u_turned.sem, 1)

                if 0 <= r < len(real):
                    if tail_turn(r) is not None:
                        if r == last_round:
                            pe.wait_ge(*reduced.after(units[-1]))
                        turn_output(tail_turn(r))
                    if tail_tile(r) is not None:
                        project_output(tail_tile(r))

            turn_output(NB - 1)

            def turn_x(b):
                pe.wait_ge(*ln_ready.after(("C", b)))
                if b == 1:
                    pe.wait_ge(*turned_lo.after(("O", NB - 1, NC - 1)))
                if b >= 2:
                    pe.wait_ge(*turned_lo.after(("D", b - 2, NC - 1)))
                turn("D", b, x)

            def logits1_of(b):
                pe.wait_ge(*turned_lo.after(("D", b, NC - 1)))
                for t in range(TPB * b, TPB * (b + 1)):
                    at_ = E1 * (t % PAIR)
                    mm = product(ps[:, 7 - b // 2, at_:at_ + E1],
                                 [(lambda i, c=c: xtd[:, i, c, P * t:P * (t + 1)], lambda k, c=c: wg1[:, k, c, :])
                                  for c in range(NC)])
                mm.then_inc(logits1.sem, 1)

            pe.wait_ge(*exp_done.after((len(real) - 1, 1)))
            turn_x(0)
            for t in range(NT - TPB, NT):
                project_output(t)
            pe.wait_ge(wg1_ready, 1)
            logits1_of(0)
            turn_x(1)
            turn_x(2)
            logits1_of(1)
            turn_x(3)
            logits1_of(2)
            logits1_of(3)

            def widen_weights(hf):
                for b in range(2 * hf, 2 * hf + 2):
                    pe.wait_ge(*ce_wide.after(b))
                    for t in range(TPB):
                        mm = pe.transpose(ps[:, b % 2, P * t:P * (t + 1)], cex[:, b % 2, t, :], ident[:, :])
                    mm.then_inc(ce_ps.sem, 1)

            def down(hf, j):
                n = hj_no(hf, j)
                for tb in range(2):
                    pe.wait_ge(*h_lo.after((hf, j, tb)))
                if j == 0:
                    pe.wait_ge(*ce_sb.after(2 * hf + 1))
                for a in range(PAIR):
                    tb, t = a // 4, a % 4
                    mm = product(ps[:, a // 2, H * (a % 2):H * (a % 2 + 1)],
                                 [(lambda i: hpart[:, n % 2, tb, i, P * t:P * (t + 1)], lambda k: dn[:, n % 3, k, :])],
                                 j == 0 and a % 2 == 0, j == JT - 1, skip_group_check=True)
                mm.then_inc(down1.sem, 1)

            pe.wait_ge(*turned_lo.after(("D", NB - 1, NC - 1)))
            pe.wait_ge(*lg1_shift.after(1))
            for hf in range(2):
                for j in range(JT):
                    n = hj_no(hf, j)
                    pe.wait_ge(*wd_lo.after((hf, j)))
                    for tb in range(2):
                        if n:
                            pe.wait_ge(*hmul_ready.after(hjt[2 * n + tb - 2]))
                        col = BLK * (2 * hf + tb)
                        for w in range(2):
                            mm = product(ps[:, 4 + 2 * tb + w, :],
                                         [(lambda i, c=c: gu[:, n % 3, i, c, w, :],
                                           lambda k, c=c: xtd[:, k, c, col:col + BLK]) for c in range(NC)])
                        mm.then_inc(gu_ps.sem, 1)
                    if j:
                        down(hf, j - 1)
                    else:
                        if hf:
                            pe.wait_ge(*acc_read.after((0, PAIR - 1)))
                        widen_weights(hf)
                down(hf, JT - 1)


def kernel(**inputs):
    from concourse.bass_utils import run_bass_kernel_spmd
    import ml_dtypes

    a = {k: np.asarray(v) for k, v in inputs.items()}

    def lay(v):
        return np.ascontiguousarray(v)

    def rows(v, chunks):
        return v.reshape((chunks, P) + v.shape[1:]).swapaxes(0, 1)

    xs = a["L0_attn_x"][0]
    A = [a["L0_ffn_A1"], a["L0_ffn_A3"]]
    B = [a["L0_ffn_B1"], a["L0_ffn_B3"]]
    gup = a["L1_ffn_gate_up_proj"].reshape(E1, 2, JT, RPT, H)
    k = np.arange(P)
    arrays = {
        "x_tm": rows(xs, NT),
        "x_fm": rows(xs.T, NC),
        "w13": rows(np.stack([a["L0_ffn_W1"].T, a["L0_ffn_W3"].T], 1), NC),
        "a13": rows(np.stack([m.transpose(2, 1, 0).reshape(H, E0 * R0) for m in A], 1), NC),
        "b13": rows(np.stack([m.transpose(2, 0, 1).reshape(E0 * R0, F) for m in B], 1), NC),
        "w2a2": rows(np.concatenate([a["L0_ffn_W2"].T, a["L0_ffn_A2"].transpose(2, 1, 0).reshape(F, E0 * R0)], 1), FT),
        "b2": rows(a["L0_ffn_B2"].transpose(2, 0, 1).reshape(E0 * R0, H), NC),
        "wg0": rows(a["L0_ffn_Wg"].T, NC),
        "wqkv": rows(a["L1_attn_w_qkv"].T, NC),
        "wo": rows(a["L1_attn_w_o"].T, NC),
        "wg1": rows(a["L1_ffn_gate_weight"].T, NC),
        "wgu": gup.transpose(4, 2, 1, 3, 0).reshape(NC, P, JT, 2, P).transpose(1, 2, 0, 3, 4).reshape(P, JT, NC * 2 * P),
        "wdn": a["L1_ffn_down_proj"].reshape(E1, H, JT, RPT).transpose(3, 0, 2, 1).reshape(P, JT, H),
        "ident": np.eye(P, dtype=np.float32),
        "identb": np.eye(P).astype(ml_dtypes.bfloat16),
        "trimax": np.where(k[None, :] > k[:, None], NEG, 0.0).astype(ml_dtypes.bfloat16),
        "triexp": np.where(k[:, None] > k[None, :], NEG, 0.0).astype(ml_dtypes.bfloat16),
        "iota": np.tile(np.arange(E1, dtype=np.float32), (P, 1)),
    }
    arrays = {f"in_{n}": lay(v) for n, v in arrays.items()}
    nc = bacc.Bacc("TRN2", target_bir_lowering=False, num_devices=1)
    args = [nc.dram_tensor(n, v.shape, mybir.dt.from_np(v.dtype), kind="ExternalInput").ap() for n, v in arrays.items()]
    out = nc.dram_tensor("out", (P, NT, H), F32, kind="ExternalOutput").ap()
    build(nc, *args, out)
    r = run_bass_kernel_spmd(nc, [arrays], core_ids=[0])
    return r.results[0]["out"].swapaxes(0, 1).reshape(1, T, H)
```
